# Optimizing a Trainium2 kernel written in Bass

```python
import numpy as np
import jax
import jax.numpy as jnp

def _softmax(x, axis=-1):
    return jax.nn.softmax(x, axis=axis)

def _gelu(x):
    return jax.nn.gelu(x, approximate=True)

def _silu(x):
    return jax.nn.silu(x)

def _sigmoid(x):
    return jax.nn.sigmoid(x)

def _layernorm(x, axis=-1, eps=1e-05):
    m = jnp.mean(x, axis=axis, keepdims=True)
    v = jnp.var(x, axis=axis, keepdims=True)
    return (x - m) / jnp.sqrt(v + eps)

def _scatter_add(tgt, idx, src, axis=0):
    return tgt.at[idx].add(src)

def _segment_sum(src, seg, n):
    return jax.ops.segment_sum(src, seg, n)
kernel_name = 'mk_gnn_resnorm_d4_gnn_r32_9d5462'

def setup_inputs(seed: int=0):
    np.random.seed(seed)
    _w = jnp.asarray

    def _rec_inputs():
        import jax
        import jax.numpy as jnp
        _gk = jax.random.key(seed)
        x = -0.0002117 + 1 * jax.random.normal(jax.random.fold_in(_gk, 1), (3125, 256), jnp.float32)
        src = jax.random.randint(jax.random.fold_in(_gk, 2), (50000,), 0, 3125, jnp.int32)
        dst = jax.random.randint(jax.random.fold_in(_gk, 3), (50000,), 0, 3125, jnp.int32)
        _o = jnp.argsort(dst, stable=True)
        src = src[_o]
        dst = dst[_o]
        edge_weight = jax.random.uniform(jax.random.fold_in(_gk, 12), (50000,), jnp.float32, 0.0, 0.999998)
        return (x, src, dst, edge_weight)
    x, src, dst, edge_weight = _rec_inputs()

    def _L0_gnn_setup():
        import jax, jax.numpy as jnp
        import numpy as np
        N_NODES = 3125
        N_EDGES = 9375
        HIDDEN = 256
        N_LAYERS = 3
        LN_EPS = 1e-05

        def _layer_norm(x, g, b):
            mu = jnp.mean(x, axis=-1, keepdims=True)
            var = jnp.mean(jnp.square(x - mu), axis=-1, keepdims=True)
            return (x - mu) * jax.lax.rsqrt(var + LN_EPS) * g + b

        def _gin_layer(h, src, dst, W1, b1, W2, b2, eps, gamma, beta):
            agg = jax.ops.segment_sum(h[src], dst, num_segments=N_NODES)
            z = (1.0 + eps) * h + agg
            m = jax.nn.relu(z @ W1 + b1) @ W2 + b2
            return jax.nn.relu(_layer_norm(m + h, gamma, beta))
        key = jax.random.key(seed)
        ks = jax.random.split(key, 6)
        h = jax.random.normal(ks[0], (N_NODES, HIDDEN), dtype=jnp.float32)
        edge_index = jax.random.randint(ks[1], (2, N_EDGES), 0, N_NODES, dtype=jnp.int64)
        scale = 1.0 / np.sqrt(HIDDEN)
        W1 = jax.random.normal(ks[2], (N_LAYERS, HIDDEN, HIDDEN), dtype=jnp.float32) * scale
        W2 = jax.random.normal(ks[3], (N_LAYERS, HIDDEN, HIDDEN), dtype=jnp.float32) * scale
        b1 = jnp.zeros((N_LAYERS, HIDDEN), dtype=jnp.float32)
        b2 = jnp.zeros((N_LAYERS, HIDDEN), dtype=jnp.float32)
        eps = jnp.zeros((N_LAYERS,), dtype=jnp.float32)
        gamma = jnp.ones((N_LAYERS, HIDDEN), dtype=jnp.float32)
        beta = jnp.zeros((N_LAYERS, HIDDEN), dtype=jnp.float32)
        return {'h': h, 'edge_index': edge_index, 'W1': W1, 'b1': b1, 'W2': W2, 'b2': b2, 'eps': eps, 'gamma': gamma, 'beta': beta}
    _L0_gnn_all = _L0_gnn_setup()
    _L0_gnn_in = {k: v for k, v in _L0_gnn_all.items() if k in ('W1', 'b1', 'W2', 'b2', 'eps', 'gamma', 'beta')}
    del _L0_gnn_all

    def _L1_gnn_setup():
        import jax, jax.numpy as jnp
        import numpy as np
        N_NODES = 50000
        N_EDGES = 12500
        IN_DIM = 256
        HID = 64
        HEADS = 8
        OUT_DIM = 256
        NEG_SLOPE = 0.2

        def _gat_forward(x, edge_index, W, a, Wo, bo):
            n = x.shape[0]
            src, tgt = (edge_index[0], edge_index[1])
            h = jnp.einsum('ni,hio->nho', x, W)
            a_src, a_tgt = (a[:, :HID], a[:, HID:])
            s_src = jnp.einsum('nho,ho->nh', h, a_src)
            s_tgt = jnp.einsum('nho,ho->nh', h, a_tgt)
            e = s_src[src] + s_tgt[tgt]
            e = jnp.where(e >= 0, e, NEG_SLOPE * e)
            m = jax.ops.segment_max(e, tgt, num_segments=n)
            ex = jnp.exp(e - m[tgt])
            denom = jax.ops.segment_sum(ex, tgt, num_segments=n)
            alpha = ex / (denom[tgt] + 1e-16)
            msgs = h[src] * alpha[:, :, None]
            out = jax.ops.segment_sum(msgs, tgt, num_segments=n)
            out = out.reshape(n, HEADS * HID)
            out = out @ Wo + bo
            return jax.nn.elu(out)
        key = jax.random.key(seed)
        ks = jax.random.split(key, 6)
        x = jax.random.normal(ks[0], (N_NODES, IN_DIM), dtype=jnp.float32)
        edge_index = jax.random.randint(ks[1], (2, N_EDGES), 0, N_NODES, dtype=jnp.int64)
        W = jax.random.normal(ks[2], (HEADS, IN_DIM, HID), dtype=jnp.float32) * (1.0 / np.sqrt(IN_DIM))
        a = jax.random.normal(ks[3], (HEADS, 2 * HID), dtype=jnp.float32) * (1.0 / np.sqrt(2 * HID))
        Wo = jax.random.normal(ks[4], (HEADS * HID, OUT_DIM), dtype=jnp.float32) * (1.0 / np.sqrt(HEADS * HID))
        bo = jnp.zeros((OUT_DIM,), dtype=jnp.float32)
        return {'x': x, 'edge_index': edge_index, 'W': W, 'a': a, 'Wo': Wo, 'bo': bo}
    _L1_gnn_all = _L1_gnn_setup()
    _L1_gnn_in = {k: v for k, v in _L1_gnn_all.items() if k in ('W', 'a', 'Wo', 'bo')}
    del _L1_gnn_all

    def _L2_gnn_setup():
        import jax, jax.numpy as jnp
        import numpy as np
        N_NODES = 50000
        N_EDGES = 25000
        IN_DIM = 256
        HID = 512
        N_LAYERS = 3
        OUT_DIM = 256
        TOTAL_HID = HID * (N_LAYERS + 1)
        key = jax.random.key(seed)
        ks = jax.random.split(key, 10)
        s = 0.02
        return {'x': jax.random.normal(ks[0], (N_NODES, IN_DIM), dtype=jnp.float32), 'edge_index': jax.random.randint(ks[1], (2, N_EDGES), 0, N_NODES, dtype=jnp.int64), 'in_W': jax.random.normal(ks[2], (IN_DIM, HID), dtype=jnp.float32) * s, 'in_b': jnp.zeros((HID,), dtype=jnp.float32), 'conv_W1': jax.random.normal(ks[3], (N_LAYERS, HID, HID), dtype=jnp.float32) * s, 'conv_b1': jnp.zeros((N_LAYERS, HID), dtype=jnp.float32), 'conv_W2': jax.random.normal(ks[4], (N_LAYERS, HID, HID), dtype=jnp.float32) * s, 'conv_b2': jnp.zeros((N_LAYERS, HID), dtype=jnp.float32), 'out_W': jax.random.normal(ks[5], (TOTAL_HID, OUT_DIM), dtype=jnp.float32) * s, 'out_b': jnp.zeros((OUT_DIM,), dtype=jnp.float32)}
    _L2_gnn_all = _L2_gnn_setup()
    _L2_gnn_in = {k: v for k, v in _L2_gnn_all.items() if k in ('in_W', 'in_b', 'conv_W1', 'conv_b1', 'conv_W2', 'conv_b2', 'out_W', 'out_b')}
    del _L2_gnn_all

    def _L3_gnn_setup():
        import jax, jax.numpy as jnp
        import numpy as np
        N_NODES = 50000
        N_EDGES = 25000
        IN_DIM, HID_DIM, OUT_DIM, N_HEADS = (256, 256, 64, 4)
        ATT_DIM = OUT_DIM * 2 + 1
        key = jax.random.key(seed)
        ks = jax.random.split(key, 8)
        s = 0.05
        return {'x': jax.random.normal(ks[0], (N_NODES, IN_DIM), dtype=jnp.float32), 'idx': jax.random.randint(ks[1], (2, N_EDGES), 0, N_NODES, dtype=jnp.int32), 'elem': jax.random.uniform(ks[2], (N_EDGES,), dtype=jnp.float32), 'W1': jax.random.normal(ks[3], (N_HEADS, IN_DIM, HID_DIM), dtype=jnp.float32) * s, 'b1': jnp.zeros((N_HEADS, HID_DIM), jnp.float32), 'W2': jax.random.normal(ks[4], (N_HEADS, HID_DIM, OUT_DIM), dtype=jnp.float32) * s, 'b2': jnp.zeros((N_HEADS, OUT_DIM), jnp.float32), 'A1': jax.random.normal(ks[5], (N_HEADS, ATT_DIM, ATT_DIM), dtype=jnp.float32) * s, 'ab1': jnp.zeros((N_HEADS, ATT_DIM), jnp.float32), 'A2': jax.random.normal(ks[6], (N_HEADS, ATT_DIM, 1), dtype=jnp.float32) * s, 'ab2': jnp.zeros((N_HEADS, 1), jnp.float32)}
    _L3_gnn_all = _L3_gnn_setup()
    _L3_gnn_in = {k: v for k, v in _L3_gnn_all.items() if k in ('W1', 'b1', 'W2', 'b2', 'A1', 'ab1', 'A2', 'ab2')}
    del _L3_gnn_all
    return {'x': x, 'src': src, 'dst': dst, 'edge_weight': edge_weight, 'L0_gnn_W1': _L0_gnn_in['W1'], 'L0_gnn_b1': _L0_gnn_in['b1'], 'L0_gnn_W2': _L0_gnn_in['W2'], 'L0_gnn_b2': _L0_gnn_in['b2'], 'L0_gnn_eps': _L0_gnn_in['eps'], 'L0_gnn_gamma': _L0_gnn_in['gamma'], 'L0_gnn_beta': _L0_gnn_in['beta'], 'L1_gnn_W': _L1_gnn_in['W'], 'L1_gnn_a': _L1_gnn_in['a'], 'L1_gnn_Wo': _L1_gnn_in['Wo'], 'L1_gnn_bo': _L1_gnn_in['bo'], 'L2_gnn_in_W': _L2_gnn_in['in_W'], 'L2_gnn_in_b': _L2_gnn_in['in_b'], 'L2_gnn_conv_W1': _L2_gnn_in['conv_W1'], 'L2_gnn_conv_b1': _L2_gnn_in['conv_b1'], 'L2_gnn_conv_W2': _L2_gnn_in['conv_W2'], 'L2_gnn_conv_b2': _L2_gnn_in['conv_b2'], 'L2_gnn_out_W': _L2_gnn_in['out_W'], 'L2_gnn_out_b': _L2_gnn_in['out_b'], 'L3_gnn_W1': _L3_gnn_in['W1'], 'L3_gnn_b1': _L3_gnn_in['b1'], 'L3_gnn_W2': _L3_gnn_in['W2'], 'L3_gnn_b2': _L3_gnn_in['b2'], 'L3_gnn_A1': _L3_gnn_in['A1'], 'L3_gnn_ab1': _L3_gnn_in['ab1'], 'L3_gnn_A2': _L3_gnn_in['A2'], 'L3_gnn_ab2': _L3_gnn_in['ab2']}

def reference(x, src, dst, edge_weight, L0_gnn_W1, L0_gnn_b1, L0_gnn_W2, L0_gnn_b2, L0_gnn_eps, L0_gnn_gamma, L0_gnn_beta, L1_gnn_W, L1_gnn_a, L1_gnn_Wo, L1_gnn_bo, L2_gnn_in_W, L2_gnn_in_b, L2_gnn_conv_W1, L2_gnn_conv_b1, L2_gnn_conv_W2, L2_gnn_conv_b2, L2_gnn_out_W, L2_gnn_out_b, L3_gnn_W1, L3_gnn_b1, L3_gnn_W2, L3_gnn_b2, L3_gnn_A1, L3_gnn_ab1, L3_gnn_A2, L3_gnn_ab2):
    import jax
    import jax.numpy as jnp

    def _L0_gnn_ref(h, edge_index, W1, b1, W2, b2, eps, gamma, beta):
        import jax, jax.numpy as jnp
        import numpy as np
        N_NODES = 3125
        N_EDGES = 9375
        HIDDEN = 256
        N_LAYERS = 3
        LN_EPS = 1e-05

        def _layer_norm(x, g, b):
            mu = jnp.mean(x, axis=-1, keepdims=True)
            var = jnp.mean(jnp.square(x - mu), axis=-1, keepdims=True)
            return (x - mu) * jax.lax.rsqrt(var + LN_EPS) * g + b

        def _gin_layer(h, src, dst, W1, b1, W2, b2, eps, gamma, beta):
            agg = jax.ops.segment_sum(h[src], dst, num_segments=N_NODES)
            z = (1.0 + eps) * h + agg
            m = jax.nn.relu(z @ W1 + b1) @ W2 + b2
            return jax.nn.relu(_layer_norm(m + h, gamma, beta))
        src, dst = (edge_index[0], edge_index[1])
        for l in range(N_LAYERS):
            h = _gin_layer(h, src, dst, W1[l], b1[l], W2[l], b2[l], eps[l], gamma[l], beta[l])
        return h

    def _L1_gnn_ref(x, edge_index, W, a, Wo, bo):
        import jax, jax.numpy as jnp
        import numpy as np
        N_NODES = 50000
        N_EDGES = 12500
        IN_DIM = 256
        HID = 64
        HEADS = 8
        OUT_DIM = 256
        NEG_SLOPE = 0.2

        def _gat_forward(x, edge_index, W, a, Wo, bo):
            n = x.shape[0]
            src, tgt = (edge_index[0], edge_index[1])
            h = jnp.einsum('ni,hio->nho', x, W)
            a_src, a_tgt = (a[:, :HID], a[:, HID:])
            s_src = jnp.einsum('nho,ho->nh', h, a_src)
            s_tgt = jnp.einsum('nho,ho->nh', h, a_tgt)
            e = s_src[src] + s_tgt[tgt]
            e = jnp.where(e >= 0, e, NEG_SLOPE * e)
            m = jax.ops.segment_max(e, tgt, num_segments=n)
            ex = jnp.exp(e - m[tgt])
            denom = jax.ops.segment_sum(ex, tgt, num_segments=n)
            alpha = ex / (denom[tgt] + 1e-16)
            msgs = h[src] * alpha[:, :, None]
            out = jax.ops.segment_sum(msgs, tgt, num_segments=n)
            out = out.reshape(n, HEADS * HID)
            out = out @ Wo + bo
            return jax.nn.elu(out)
        return _gat_forward(x, edge_index, W, a, Wo, bo)

    def _L2_gnn_ref(x, edge_index, in_W, in_b, conv_W1, conv_b1, conv_W2, conv_b2, out_W, out_b):
        import jax, jax.numpy as jnp
        import numpy as np
        N_NODES = 50000
        N_EDGES = 25000
        IN_DIM = 256
        HID = 512
        N_LAYERS = 3
        OUT_DIM = 256
        TOTAL_HID = HID * (N_LAYERS + 1)
        src, dst = (edge_index[0], edge_index[1])
        n = x.shape[0]
        h = x @ in_W + in_b
        hidden_states = [h]
        for i in range(N_LAYERS):
            agg = jax.ops.segment_sum(h[src], dst, num_segments=n)
            z = h + agg
            z = jax.nn.relu(z @ conv_W1[i] + conv_b1[i])
            h = z @ conv_W2[i] + conv_b2[i]
            hidden_states.append(h)
        cat = jnp.concatenate(hidden_states, axis=1)
        return cat @ out_W + out_b

    def _L3_gnn_ref(x, idx, elem, W1, b1, W2, b2, A1, ab1, A2, ab2):
        import jax, jax.numpy as jnp
        import numpy as np
        N_NODES = 50000
        N_EDGES = 25000
        IN_DIM, HID_DIM, OUT_DIM, N_HEADS = (256, 256, 64, 4)
        ATT_DIM = OUT_DIM * 2 + 1
        row, col = (idx[0], idx[1])
        n = x.shape[0]

        def head(w1, bb1, w2, bb2, a1, aab1, a2, aab2):
            feats = jnp.maximum(x @ w1 + bb1, 0.0) @ w2 + bb2
            x_cat = jnp.concatenate([feats[row], feats[col], elem[:, None]], axis=1)
            hid = jnp.maximum(x_cat @ a1 + aab1, 0.0)
            e1 = (hid @ a2 + aab2)[:, 0]
            e1 = jax.nn.leaky_relu(e1, negative_slope=0.2)
            w = jnp.exp(e1 - jnp.max(e1))
            pooled = jax.ops.segment_sum(w[:, None] * feats[col], row, num_segments=n)
            row_sum = jax.ops.segment_sum(w, row, num_segments=n) + 1e-10
            return pooled / row_sum[:, None]
        h = jax.vmap(head)(W1, b1, W2, b2, A1, ab1, A2, ab2)
        return jnp.transpose(h, (1, 0, 2)).reshape(n, -1)
    edge_index = jnp.stack([src, dst])
    x = _layernorm(x + _L0_gnn_ref(x, edge_index, L0_gnn_W1, L0_gnn_b1, L0_gnn_W2, L0_gnn_b2, L0_gnn_eps, L0_gnn_gamma, L0_gnn_beta), axis=-1)
    x = _layernorm(x + _L1_gnn_ref(x, edge_index, L1_gnn_W, L1_gnn_a, L1_gnn_Wo, L1_gnn_bo), axis=-1)
    x = _layernorm(x + _L2_gnn_ref(x, edge_index, L2_gnn_in_W, L2_gnn_in_b, L2_gnn_conv_W1, L2_gnn_conv_b1, L2_gnn_conv_W2, L2_gnn_conv_b2, L2_gnn_out_W, L2_gnn_out_b), axis=-1)
    x = _layernorm(x + _L3_gnn_ref(x, edge_index, edge_weight, L3_gnn_W1, L3_gnn_b1, L3_gnn_W2, L3_gnn_b2, L3_gnn_A1, L3_gnn_ab1, L3_gnn_A2, L3_gnn_ab2), axis=-1)
    return x

_drawn_inputs = setup_inputs


def setup_inputs(seed=0):
    import zlib

    import numpy as np

    out = dict(_drawn_inputs(seed))
    spreads = {'L0_gnn_b1': (0.0, 0.492),
     'L0_gnn_b2': (0.0, 0.276),
     'L0_gnn_eps': (0.0, 0.8),
     'L0_gnn_gamma': (1.0, 0.2),
     'L0_gnn_beta': (0.0, 0.1),
     'L1_gnn_bo': (0.0, 0.1),
     'L2_gnn_in_b': (0.0, 0.1),
     'L2_gnn_conv_b1': (0.0, 0.1),
     'L2_gnn_conv_b2': (0.0, 0.1),
     'L2_gnn_out_b': (0.0, 0.1),
     'L3_gnn_b1': (0.0, 0.1),
     'L3_gnn_b2': (0.0, 0.1),
     'L3_gnn_ab1': (0.0, 0.8),
     'L3_gnn_ab2': (0.0, 0.8)}
    factors = {'edge_weight': 8.0, 'L3_gnn_A1': 8.0, 'L3_gnn_A2': 8.0}
    for name, (base, spread) in spreads.items():
        noise = np.random.default_rng([zlib.crc32(name.encode()), seed]).standard_normal(out[name].shape)
        drawn = base * np.exp(spread * noise) if base else spread * noise
        out[name] = jnp.asarray(drawn.astype(out[name].dtype))
    for name, factor in factors.items():
        out[name] = (out[name] * factor).astype(out[name].dtype)
    return out
```

```python
import concourse.bass as bass
from concourse import mybir

F32 = mybir.dt.float32
F16 = mybir.dt.float16
BF16 = mybir.dt.bfloat16
I32 = mybir.dt.int32
ALU = mybir.AluOpType
ACT = mybir.ActivationFunctionType
AX = mybir.AxisListType
MAX_OF_ALL = bass.bass_isa.ReduceOp.max

P = 128
NODES = 3125
TILES = 25
NP = TILES * P
ST = 5
NST = TILES // ST
SW = ST * P
HALF = 3 * P
REST = SW - HALF
D = 256
EDGES = 50000
RING = 4
CHUNKS = 392
ROUNDS = CHUNKS // RING
EP = CHUNKS * P
LAYERS = 3
HEADS, HID = 8, 64
GH = HEADS * HID
GW = GH + HEADS
F2 = 512
PH, PO = 4, 64
ATT = 2 * PO + 1
AW = PH * ATT
PF = PH * PO
PW = PF + PH
LN_EPS = 1e-5
ACC_ROWS = NP + P


class Chain:

    def __init__(self, eng, sem):
        self.eng, self.sem, self.n = eng, sem, 0

    def __call__(self, ins):
        self.n += 1
        ins.then_inc(self.sem, 1)
        self.eng.wait_ge(self.sem, self.n)

    def reset(self):
        self.eng.sem_clear(self.sem)
        self.n = 0


class Semaphores:

    def __init__(self, nc):
        self.nc, self.all = nc, []

    def __call__(self, name):
        self.all.append(self.nc.alloc_semaphore(name))
        return self.all[-1]

    def clear(self):
        self.nc.clear_and_free_semaphores(self.all)
        self.nc.all_engine_barrier(sem_only=True)


def row_bc(ap, parts=P):
    return ap.partition_broadcast(parts)


def gnn_kernel(nc, A, out):
    dram = lambda name, shape, dt: nc.dram_tensor(name, shape, dt, kind="Internal").ap()
    T = {
        "counts": dram("counts", [NP * NP + RING * P, 1], F16),
        "tab0": dram("tab0", [NP, 2 * D], F16),
        "tab2": dram("tab2", [NP, 2 * F2], F16),
        "gat_src": dram("gat_src", [NP, GW], F32),
        "gat_dst": dram("gat_dst", [NP, 2 * HEADS], F32),
        "gat_at": dram("gat_at", [HEADS, NP], F32),
        "acc1": [dram(f"acc1_{k}", [ACC_ROWS, GW], F32) for k in range(RING)],
        "att_row": dram("att_row", [NP, AW], F32),
        "att_col": dram("att_col", [NP, AW + PF], F32),
        "spill": dram("spill", [EP, PF], F32),
        "acc3": [dram(f"acc3_{k}", [ACC_ROWS, PW], F32) for k in range(RING)],
    }
    sb = lambda name, shape, dt=F32: nc.alloc_sbuf_tensor(name, shape, dt)
    K = {
        "X": sb("X", [P, TILES, D]),
        "I32": sb("ident", [P, P]), "I16": sb("ident16", [P, P], F16),
        "ones": sb("ones", [P, P]),
        "early": sb("early", [P, (2 * RING - 1) * P]),
        "trash": sb("trash", [P, RING]),
        "trash_row": sb("trash_row", [P, 1]),
        "eps": sb("eps", [P, 1]),
        "srci": sb("srci", [P, CHUNKS + RING], I32), "dsti": sb("dsti", [P, CHUNKS + RING], I32),
        "srcf": sb("srcf", [P, CHUNKS]), "dstf": sb("dstf", [P, CHUNKS]),
        "keyf": sb("keyf", [P, CHUNKS]),
    }
    PS = [nc.alloc_psum_tensor(f"ps{k}", [P, 1024], F32) for k in range(4)]
    setup(nc, A, T, K)
    if PHASES > 1:
        build_counts(nc, A, T, K)
    if PHASES > 2:
        gin(nc, A, T, K, PS)
    if PHASES > 3:
        gat_nodes(nc, A, T, K, PS)
    if PHASES > 4:
        gat_edges(nc, A, T, K, PS)
    if PHASES > 5:
        gat_out(nc, A, T, K, PS)
    if PHASES > 6:
        deep_gin(nc, A, T, K, PS)
    if PHASES > 7:
        att_nodes(nc, A, T, K, PS)
    if PHASES > 8:
        att_edges(nc, A, T, K, PS)
    if PHASES > 9:
        att_out(nc, A, T, K, PS)
    s = nc.alloc_semaphore("out_done")
    with nc.Block() as block:
        @block.sync
        def _(sp):
            sp.dma_start(out[0:P * (TILES - 1), :].rearrange("(t p) d -> p t d", p=P),
                         K["X"][:, 0:TILES - 1, :]).then_inc(s, 16)
            sp.dma_start(out[P * (TILES - 1):NODES, :], K["X"][0:NODES - P * (TILES - 1), TILES - 1, :]).then_inc(s, 16)
            sp.wait_ge(s, 32)


def setup(nc, A, T, K):
    sem = Semaphores(nc)
    s_in, s_pad, s_zero, s_io = sem("su_in"), sem("su_pad"), sem("su_zero"), sem("su_iota")
    s_z, s_self = sem("su_zeroed"), sem("su_self")
    s_scat = [nc.alloc_semaphore(f"gat_scattered{k}") for k in range(RING)]
    s_scat3 = [nc.alloc_semaphore(f"att_scattered{k}") for k in range(RING)]
    T["scat"], T["scat3"] = s_scat, s_scat3
    with nc.sbuf_tensor("zeros", [P, 26 * 128], F32) as Z, nc.Block() as block:
        @block.vector
        def _(dve):
            ch = Chain(dve, s_self)
            dve.memset(Z[:, :], 0.0).then_inc(s_zero, 1)
            dve.memset(K["ones"][:, :], 1.0)
            dve.memset(K["eps"][:, :], LN_EPS)
            dve.memset(K["srci"][:, CHUNKS:], 0)
            dve.memset(K["dsti"][:, CHUNKS:], 0)
            dve.wait_ge(s_in, 16 * 3)
            ch(dve.tensor_copy(K["srcf"][:, :], K["srci"][:, 0:CHUNKS]))
            ch(dve.tensor_copy(K["dstf"][:, :], K["dsti"][:, 0:CHUNKS]))
            dve.scalar_tensor_tensor(out=K["keyf"][:, :], in0=K["srcf"][:, :], scalar=float(NP), in1=K["dstf"][:, :],
                                     op0=ALU.mult, op1=ALU.add)
            dve.wait_ge(s_io, 8)
            dve.tensor_copy(K["I16"][:, :], K["I32"][:, :])

        @block.gpsimd
        def _(pool):
            pool.memset(K["I32"][:, :], 0.0).then_inc(s_io, 1)
            pool.memset(K["early"][:, :], 1.0).then_inc(s_io, 1)
            pool.iota(K["trash"][:, :], [[P, RING]], base=NP * NP, channel_multiplier=1,
                      allow_small_or_imprecise_dtypes=True).then_inc(s_io, 1)
            pool.iota(K["trash_row"][:, :], [[0, 1]], base=NP, channel_multiplier=1,
                      allow_small_or_imprecise_dtypes=True).then_inc(s_io, 1)
            pool.wait_ge(s_io, 4)
            pool.affine_select(out=K["I32"][:, :], in_=K["I32"][:, :], compare_op=ALU.not_equal, fill=1.0,
                               base=0, pattern=[[-1, P]], channel_multiplier=1).then_inc(s_io, 2)
            pool.affine_select(out=K["early"][:, :], in_=K["early"][:, :], compare_op=ALU.is_gt, fill=0.0,
                               base=(RING - 1) * P, pattern=[[-1, (2 * RING - 1) * P]],
                               channel_multiplier=1).then_inc(s_io, 2)
            pool.wait_ge(s_zero, 1)
            for k in range(RING):
                pool.dma_start(T["acc1"][k][NP:ACC_ROWS, :], Z[:, 0:GW]).then_inc(s_scat[k], 16)
                pool.dma_start(T["acc3"][k][NP:ACC_ROWS, :], Z[:, 0:PW]).then_inc(s_scat3[k], 16)
            for k in range(RING):
                pool.wait_ge(s_scat[k], 16)
                pool.wait_ge(s_scat3[k], 16)

        @block.sync
        def _(sp):
            sp.dma_start(K["srci"][:, 0:CHUNKS], A["src_col"]).then_inc(s_in, 16)
            sp.dma_start(K["dsti"][:, 0:CHUNKS], A["dst_col"]).then_inc(s_in, 16)
            sp.dma_start(K["X"][:, :, :], A["x"].rearrange("(t p) d -> p t d", p=P)).then_inc(s_in, 16)
            sp.wait_ge(s_in, 48)
            sp.wait_ge(s_zero, 1)
            n = 0
            cz = T["counts"][0:NP * NP, :].rearrange("(t p n) a -> t p (n a)", p=P, n=NP)
            zh = Z[:, :].bitcast(F16)
            with sp.Fori(0, TILES) as t:
                sp.dma_start(cz[bass.ds(t, 1), :, :].rearrange("a p n -> (a p) n"), zh[:, 0:NP]).then_inc(s_z, 16)
            n += TILES
            sp.dma_start(T["counts"][NP * NP:, :].rearrange("(p n) a -> p (n a)", p=P), zh[:, 0:RING]).then_inc(s_z, 16)
            n += 1
            for k in range(RING):
                for acc, w, per in ((T["acc1"][k], GW, 5), (T["acc3"][k], PW, 5)):
                    for t in range(0, TILES, per):
                        sp.dma_start(acc[t * P:(t + per) * P, :].rearrange("(t p) w -> p t w", p=P),
                                     Z[:, 0:per * w].rearrange("p (t w) -> p t w", t=per)).then_inc(s_z, 16)
                        n += 1
            sp.wait_ge(s_z, 16 * n)
    sem.clear()


def build_counts(nc, A, T, K):
    sem = Semaphores(nc)
    s_row, s_idx, s_self = [sem("bc_row0"), sem("bc_row1")], [sem("bc_idx0"), sem("bc_idx1")], sem("bc_self")
    s_one = sem("bc_one")
    s_rfree, s_sc = [sem("bc_rfree0"), sem("bc_rfree1")], [sem("bc_scat0"), sem("bc_scat1")]
    GC = RING * P
    srow = A["src_row"].rearrange("(g n) -> g n", n=GC)
    drow = A["dst_row"].rearrange("(g n) -> g n", n=GC)
    with nc.sbuf_tensor("rows", [P, 2, 2, GC], I32) as R, nc.sbuf_tensor("keyrow", [P, GC], F32) as KR, \
            nc.sbuf_tensor("junk", [P, GC], F32) as J, nc.sbuf_tensor("allone", [P, GC], F32) as ONE, \
            nc.sbuf_tensor("kcol", [P, RING], F32) as KC, \
            nc.sbuf_tensor("cnt", [P, 2 * RING], F32) as CN, nc.sbuf_tensor("tmp", [P, 3 * RING], F32) as TM, \
            nc.sbuf_tensor("idx", [P, 2, RING], I32) as IX, nc.sbuf_tensor("val", [P, 2, RING], F16) as VA, \
            nc.Block() as block:
        @block.sync
        def _(sp):
            with sp.Fori(0, ROUNDS // 2) as it:
                for h in range(2):
                    sp.wait_ge(s_rfree[h], it + 1)
                    sp.dma_start(R[:, h, 0, :], row_bc(srow[bass.ds(2 * it + h, 1), :].rearrange("a n -> (a n)"))).then_inc(s_row[h], 16)
                    sp.dma_start(R[:, h, 1, :], row_bc(drow[bass.ds(2 * it + h, 1), :].rearrange("a n -> (a n)"))).then_inc(s_row[h], 16)

        @block.vector
        def _(dve):
            ch = Chain(dve, s_self)
            for h in range(2):
                dve.sem_inc(s_rfree[h], 1)
            ch(dve.memset(ONE[:, :], 1.0))
            ch.reset()
            with dve.Fori(0, ROUNDS // 2) as it:
                for h in range(2):
                    dve.wait_ge(s_row[h], 32 * (it + 1))
                    ch(dve.scalar_tensor_tensor(out=KR[:, :], in0=R[:, h, 0, :], scalar=float(NP), in1=R[:, h, 1, :],
                                                op0=ALU.mult, op1=ALU.add))
                    dve.sem_inc(s_rfree[h], 1)
                    ch(dve.tensor_copy(KC[:, :], K["keyf"][:, bass.ds((2 * it + h) * RING, RING)]))
                    for k in range(RING):
                        e0 = (RING - 1 - k) * P
                        ch(dve.scalar_tensor_tensor(out=J[:, :], in0=KR[:, :], scalar=KC[:, k:k + 1], in1=ONE[:, :],
                                                    op0=ALU.is_equal, op1=ALU.mult, accum_out=CN[:, k:k + 1]))
                        ch(dve.scalar_tensor_tensor(out=J[:, :], in0=KR[:, :], scalar=KC[:, k:k + 1],
                                                    in1=K["early"][:, e0:e0 + GC],
                                                    op0=ALU.is_equal, op1=ALU.mult, accum_out=CN[:, RING + k:RING + k + 1]))
                    ch(dve.tensor_scalar(TM[:, 0:RING], CN[:, RING:], 0.5, None, ALU.is_lt))
                    dve.tensor_tensor(TM[:, RING:2 * RING], KC[:, :], TM[:, 0:RING], ALU.mult)
                    ch(dve.tensor_scalar(TM[:, 2 * RING:], TM[:, 0:RING], -1.0, 1.0, ALU.mult, ALU.add))
                    ch(dve.tensor_tensor(TM[:, 2 * RING:], TM[:, 2 * RING:], K["trash"][:, :], ALU.mult))
                    dve.wait_ge(s_sc[h], 16 * (RING * it + 1))
                    ch(dve.tensor_tensor(IX[:, h, :], TM[:, RING:2 * RING], TM[:, 2 * RING:], ALU.add))
                    ch(dve.tensor_copy(VA[:, h, :], CN[:, 0:RING]))
                    dve.sem_inc(s_idx[h], 1)
                ch.reset()

        @block.gpsimd
        def _(pool):
            for h in range(2):
                pool.dma_start(IX[:, h, :], A["src_col"][:, 0:RING]).then_inc(s_sc[h], 16)
            for h in range(2):
                pool.wait_ge(s_sc[h], 16)
            with pool.Fori(0, ROUNDS // 2) as it:
                for h in range(2):
                    pool.wait_ge(s_idx[h], it + 1)
                    pool.wait_ge(s_sc[1 - h], 16 * (RING * (it + h) + 1))
                    pool.sem_inc(s_one, 1)
                    for k in range(RING):
                        pool.indirect_dma_start(
                            out=T["counts"], out_offset=bass.IndirectOffsetOnAxis(ap=IX[:, h, k:k + 1], axis=0),
                            in_=VA[:, h, k:k + 1], in_offset=None, compute_op=ALU.add).then_inc(s_sc[h], 16)
            for h in range(2):
                pool.wait_ge(s_sc[h], 16 * (RING * (ROUNDS // 2) + 1))
    sem.clear()


def split16(ch, dve, x, hi, lo):
    ch(dve.tensor_copy(hi, x))
    ch(dve.tensor_tensor(lo, x, hi, ALU.subtract))


def norm_stats(ch, dve, x, stats, mv, n):
    for i in range(n):
        dve_i = dve.bn_stats(stats[:, i, :], x[:, i, :])
        ch(dve_i)
        ch(dve.bn_aggr(mv[:, i, :], stats[:, i, :]))


def final_norm(nc, K, name, add, width=ST):
    sem = Semaphores(nc)
    s_self, s_mv, s_sd = (sem(f"{name}_{x}") for x in ("self", "var", "sd"))
    X = K["X"]
    with nc.sbuf_tensor(name + "_st", [P, TILES, 6], F32) as S, nc.sbuf_tensor(name + "_mv", [P, TILES, 2], F32) as MV, \
            nc.sbuf_tensor(name + "_sd", [P, TILES], F32) as SD, nc.sbuf_tensor(name + "_rs", [P, TILES], F32) as RS, \
            nc.Block() as block:
        @block.vector
        def _(dve):
            ch = Chain(dve, s_self)
            if add is not None:
                ch(dve.tensor_tensor(X[:, :, :], X[:, :, :], add[:, :, :], ALU.add))
            for i in range(TILES):
                dve.bn_stats(S[:, i, :], X[:, i, :]).then_inc(s_self, 1)
            ch.n += TILES
            dve.wait_ge(s_self, ch.n)
            for i in range(TILES):
                dve.bn_aggr(MV[:, i, :], S[:, i, :]).then_inc(s_mv, 1)
            dve.wait_ge(s_sd, 1)
            ch(dve.reciprocal(RS[:, :], SD[:, :]))
            for i in range(TILES):
                dve.tensor_scalar(X[:, i, :], X[:, i, :], MV[:, i, 0:1], RS[:, i:i + 1], ALU.subtract, ALU.mult)

        @block.scalar
        def _(act):
            act.wait_ge(s_mv, TILES)
            act.activation(SD[:, :], MV[:, :, 1], ACT.Sqrt, bias=K["eps"][:, 0:1]).then_inc(s_sd, 1)
    sem.clear()


def load_counts(sp, T, C, s_in, s_out, j, round_):
    view = T["counts"][0:NP * NP, :].rearrange("(k s p t c) a -> k t p s (c a)", k=ST, s=ST, p=P, c=SW)
    for q in range(ST):
        sp.wait_ge(s_out[q], round_ + 1)
        sp.dma_start(C[:, q, :, :], view[q, bass.ds(j, 1), :, :, :].rearrange("a p s c -> (a p) s c")).then_inc(s_in[q], 16)


def neighbour_sum(pe, TAB, C, ps, fb, width, s_in, s_out, round_, last, own):
    for s in range(TILES):
        q = s // ST
        if fb == 0 and s % ST == 0:
            pe.wait_ge(s_in[q], 16 * (round_ + 1))
        for part in range(2):
            w = TAB[:, s, part * width + fb * P:part * width + (fb + 1) * P]
            first, end = s == 0 and part == 0, s == TILES - 1 and part == 1
            pe.matmul(ps[:, 0:HALF], w, C[:, q, s % ST, 0:HALF], start=first, stop=end, skip_group_check=True)
            m = pe.matmul(ps[:, 512:512 + REST], w, C[:, q, s % ST, HALF:SW], start=first, stop=end, skip_group_check=True)
        if last and s % ST == ST - 1 and q < ST - 1:
            m.then_inc(s_out[q], 1)
        if s == ST:
            own()
    return m


def cols(i):
    return slice(i * P, (i + 1) * P) if i < 3 else slice(512 + (i - 3) * P, 512 + (i - 2) * P)


HALVES = ((slice(0, HALF), slice(0, HALF)), (slice(512, 512 + REST), slice(HALF, SW)))


def gin(nc, A, T, K, PS):
    sem = Semaphores(nc)
    n_ = lambda x: sem("gin_" + x)
    s_tab, s_w, s_self, s_hl, s_taken = n_("tab_in"), n_("weights_in"), n_("self"), n_("split"), n_("taken")
    s_tabout, s_own, s_zt, s_ut = n_("tab_out"), n_("own"), n_("zt"), n_("ut")
    s_mv, s_sd = n_("var"), n_("sd")
    s_cin, s_cout = [n_(f"c_in{q}") for q in range(ST)], [n_(f"c_out{q}") for q in range(ST)]
    s_full, s_free = [n_(f"full{k}") for k in range(4)], [n_(f"free{k}") for k in range(4)]
    X = K["X"]
    NW = 7
    with nc.sbuf_tensor("gin_h", [P, TILES, D], F32) as H:
        with nc.sbuf_tensor("gin_tab", [P, TILES, 2 * D], F16) as TAB, \
                nc.sbuf_tensor("gin_c", [P, ST, ST, SW], F16) as C, \
                nc.sbuf_tensor("gin_w1", [P, 2, D], F32) as W1, nc.sbuf_tensor("gin_w2", [P, 2, D], F32) as W2, \
                nc.sbuf_tensor("gin_b1", [P, 2], F32) as B1, nc.sbuf_tensor("gin_rows", [P, 3, D], F32) as RW, \
                nc.sbuf_tensor("gin_eps", [P, 1], F32) as EPS, nc.sbuf_tensor("gin_eps1", [P, 1], F32) as EPS1, \
                nc.sbuf_tensor("gin_own", [P, ST, D], F32) as OWN, nc.sbuf_tensor("gin_hb", [P, ST, D], F32) as HB, \
                nc.sbuf_tensor("gin_r", [P, ST, D], F32) as R, nc.sbuf_tensor("gin_hl", [P, ST, 2 * D], F16) as HL, \
                nc.sbuf_tensor("gin_zt", [P, 2, SW], F32) as ZT, nc.sbuf_tensor("gin_ut", [P, 2, SW], F32) as UT, \
                nc.sbuf_tensor("gin_st", [P, ST, 6], F32) as S, nc.sbuf_tensor("gin_mv", [P, ST, 2], F32) as MV, \
                nc.sbuf_tensor("gin_sd", [P, ST], F32) as SD, nc.sbuf_tensor("gin_rs", [P, ST], F32) as RS, \
                nc.Block() as block:
            tab_d = T["tab0"].rearrange("(j t p) w -> j p t w", t=ST, p=P)

            @block.sync
            def _(sp):
                with sp.Fori(0, LAYERS) as l:
                    sp.wait_ge(s_tabout, 16 * NST * (l + 1))
                    one = bass.ds(l, 1)
                    sp.dma_start(TAB[:, :, :], T["tab0"].rearrange("(t p) w -> p t w", p=P)).then_inc(s_tab, 16)
                    for dst, name in ((W1, "L0_gnn_W1"), (W2, "L0_gnn_W2")):
                        sp.dma_start(dst[:, :, :], A[name][one, :, :].rearrange("a (k p) n -> p (a k) n", p=P)).then_inc(s_w, 16)
                    sp.dma_start(B1[:, :], A["L0_gnn_b1"][one, :, :].rearrange("a p k -> (a p) k")).then_inc(s_w, 16)
                    for n, name in enumerate(("L0_gnn_b2", "L0_gnn_gamma", "L0_gnn_beta")):
                        sp.dma_start(RW[:, n, :], row_bc(A[name][one, :].rearrange("a n -> (a n)"))).then_inc(s_w, 16)
                    sp.dma_start(EPS[:, :], row_bc(A["L0_gnn_eps"][one])).then_inc(s_w, 16)
                    with sp.Fori(0, NST) as j:
                        load_counts(sp, T, C, s_cin, s_cout, j, l * NST + j)

            @block.gpsimd
            def _(pool):
                def store(j, n):
                    pool.wait_ge(s_hl, n)
                    pool.sem_inc(s_taken, 1)
                    pool.dma_start(tab_d[bass.ds(j, 1), :, :, :].rearrange("a p t w -> (a p) t w"), HL[:, :, :]).then_inc(s_tabout, 16)
                with pool.Fori(0, NST) as j:
                    store(j, j + 1)
                with pool.Fori(0, LAYERS) as l:
                    with pool.Fori(0, NST) as j:
                        store(j, l * NST + j + NST + 1)
                pool.wait_ge(s_tabout, 16 * NST * (LAYERS + 1))

            @block.vector
            def _(dve):
                ch = Chain(dve, s_self)
                ch(dve.tensor_copy(H[:, :, :], X[:, :, :]))
                for j in range(NST):
                    if j:
                        dve.wait_ge(s_tabout, 16 * j)
                    split16(ch, dve, H[:, j * ST:(j + 1) * ST, :], HL[:, :, 0:D], HL[:, :, D:])
                    dve.sem_inc(s_hl, 1)
                ch.reset()
                with dve.Fori(0, LAYERS) as l:
                    dve.wait_ge(s_w, 16 * NW * (l + 1))
                    ch(dve.tensor_scalar(EPS1[:, :], EPS[:, :], 1.0, None, ALU.add))
                    ch.reset()
                    with dve.Fori(0, NST) as j:
                        g = l * NST + j
                        mine = H[:, bass.ds(j * ST, ST), :]
                        ch(dve.tensor_scalar(OWN[:, :, :], mine, EPS1[:, 0:1], None, ALU.mult))
                        dve.sem_inc(s_own, 1)
                        ch(dve.tensor_tensor(HB[:, :, :], mine, RW[:, 0:1, :].broadcast_to([P, ST, D]), ALU.add))
                        for i in range(ST):
                            k = 2 + i % 2
                            per, nth = (4, 1 + i // 2) if k == 2 else (3, 1 + i // 2)
                            dve.wait_ge(s_full[k], per * g + nth + 1)
                            ch(dve.tensor_tensor(R[:, i, :], HB[:, i, :], PS[k][:, 0:D], ALU.add))
                            dve.sem_inc(s_free[k], 1)
                        norm_stats(ch, dve, R, S, MV, ST)
                        dve.sem_inc(s_mv, 1)
                        dve.wait_ge(s_sd, g + 1)
                        ch(dve.reciprocal(RS[:, :], SD[:, :]))
                        for i in range(ST):
                            ch(dve.tensor_scalar(R[:, i, :], R[:, i, :], MV[:, i, 0:1], RS[:, i:i + 1], ALU.subtract, ALU.mult))
                        ch(dve.tensor_tensor(R[:, :, :], R[:, :, :], RW[:, 1:2, :].broadcast_to([P, ST, D]), ALU.mult))
                        ch(dve.tensor_tensor(R[:, :, :], R[:, :, :], RW[:, 2:3, :].broadcast_to([P, ST, D]), ALU.add))
                        ch(dve.tensor_scalar(R[:, :, :], R[:, :, :], 0.0, None, ALU.max))
                        ch(dve.tensor_copy(mine, R[:, :, :]))
                        dve.wait_ge(s_tabout, 16 * (g + NST))
                        split16(ch, dve, R[:, :, :], HL[:, :, 0:D], HL[:, :, D:])
                        dve.sem_inc(s_hl, 1)
                        ch.reset()

            @block.scalar
            def _(act):
                for q in range(ST):
                    act.sem_inc(s_cout[q], 1)
                for k in range(4):
                    act.sem_inc(s_free[k], 1)
                with act.Fori(0, LAYERS) as l:
                    act.wait_ge(s_w, 16 * NW * (l + 1))
                    act.sem_inc(s_taken, 1)
                    with act.Fori(0, NST) as j:
                        g = l * NST + j
                        for fb in range(2):
                            act.wait_ge(s_full[fb], g + 1)
                            for a, b in HALVES:
                                act.activation(ZT[:, fb, b], PS[fb][:, a], ACT.Copy).then_inc(s_zt, 1)
                            act.wait_ge(s_zt, 4 * g + 2 * fb + 2)
                            act.sem_inc(s_free[fb], 1)
                        for hb in range(2):
                            k = 2 + hb
                            act.wait_ge(s_full[k], (4 - hb) * g + 1)
                            for a, b in HALVES:
                                act.activation(UT[:, hb, b], PS[k][:, a], ACT.Relu, bias=B1[:, hb:hb + 1]).then_inc(s_ut, 1)
                            act.wait_ge(s_ut, 4 * g + 2 * hb + 2)
                            act.sem_inc(s_free[k], 1)
                        act.wait_ge(s_mv, g + 1)
                        act.activation(SD[:, :], MV[:, :, 1], ACT.Sqrt, bias=K["eps"][:, 0:1]).then_inc(s_sd, 1)

            @block.tensor
            def _(pe):
                with pe.Fori(0, LAYERS) as l:
                    pe.wait_ge(s_w, 16 * NW * (l + 1))
                    pe.wait_ge(s_tab, 16 * (l + 1))
                    pe.sem_inc(s_taken, 1)
                    with pe.Fori(0, NST) as j:
                        g = l * NST + j
                        for fb in range(2):
                            def own():
                                if fb == 0:
                                    pe.wait_ge(s_own, g + 1)
                                for i in range(ST):
                                    pe.matmul(PS[fb][:, cols(i)], OWN[:, i, fb * P:(fb + 1) * P], K["I32"][:, :],
                                              start=False, stop=False, skip_group_check=True)
                            pe.wait_ge(s_free[fb], g + 1)
                            neighbour_sum(pe, TAB, C, PS[fb], fb, D, s_cin, s_cout, g, fb == 1, own).then_inc(s_full[fb], 1)
                        pe.wait_ge(s_zt, 4 * g + 4)
                        pe.sem_inc(s_cout[ST - 1], 1)
                        for hb in range(2):
                            pe.wait_ge(s_free[2 + hb], (4 - hb) * g + 1)
                            for a, b in HALVES:
                                for kb in range(2):
                                    m = pe.matmul(PS[2 + hb][:, a], W1[:, kb, hb * P:(hb + 1) * P], ZT[:, kb, b],
                                                  start=kb == 0, stop=kb == 1)
                            m.then_inc(s_full[2 + hb], 1)
                        pe.wait_ge(s_ut, 4 * g + 4)
                        for i in range(ST):
                            k = 2 + i % 2
                            per, nth = (4, 1 + i // 2) if k == 2 else (3, 1 + i // 2)
                            pe.wait_ge(s_free[k], per * g + nth + 1)
                            for kb in range(2):
                                m = pe.matmul(PS[k][:, 0:D], UT[:, kb, i * P:(i + 1) * P], W2[:, kb, :], start=kb == 0, stop=kb == 1)
                            m.then_inc(s_full[k], 1)
        final_norm(nc, K, "gin_ln", H)
    sem.clear()


def transposed(pe, ident, ps, src, n, col):
    for i in range(n):
        m = pe.transpose(ps[:, cols(i)], src[:, i, col:col + P], ident)
    return m


def gat_nodes(nc, A, T, K, PS):
    sem = Semaphores(nc)
    n_ = lambda x: sem("gn_" + x)
    s_w, s_self, s_taken, s_xs, s_xt, s_row, s_sc = (n_(x) for x in ("w", "self", "taken", "xs", "xt", "row", "score"))
    s_as, s_as2, s_out, s_aout = n_("as"), n_("as_half"), n_("row_out"), n_("at_out")
    s_full, s_free = [n_(f"full{k}") for k in range(4)], [n_(f"free{k}") for k in range(4)]
    with nc.sbuf_tensor("gn_bm", [P, TILES, 2 * HEADS], F32) as BM:
        with nc.sbuf_tensor("gn_w", [P, 2, GH], F32) as W, nc.sbuf_tensor("gn_a", [P, HEADS, 2, HID], F32) as AV, \
                nc.sbuf_tensor("gn_xs", [P, ST, D], F32) as XS, nc.sbuf_tensor("gn_xt", [P, 2, SW], F32) as XT, \
                nc.sbuf_tensor("gn_row", [P, ST, GW], F32) as ROW, nc.sbuf_tensor("gn_p", [P, HEADS, HID], F32) as PR, \
                nc.sbuf_tensor("gn_as", [HEADS, SW], F32) as AS, nc.Block() as block:
            @block.sync
            def _(sp):
                sp.dma_start(W[:, :, :], A["L1_gnn_W"].rearrange("(k p) n -> p k n", p=P)).then_inc(s_w, 16)
                sp.dma_start(AV[:, :, :, :].rearrange("p h s o -> p (h s o)"),
                             row_bc(A["L1_gnn_a"].rearrange("h o -> (h o)"))).then_inc(s_w, 16)
                rows = T["gat_src"].rearrange("(j t p) w -> j p t w", t=ST, p=P)
                with sp.Fori(0, NST) as j:
                    sp.wait_ge(s_as, j + 1)
                    sp.dma_start(rows[bass.ds(j, 1), :, :, :].rearrange("a p t w -> (a p) t w"), ROW[:, :, :]).then_inc(s_out, 16)
                    sp.dma_start(T["gat_at"][:, bass.ds(j * SW, SW)], AS[:, :]).then_inc(s_out, 16)
                    sp.wait_ge(s_out, 32 * (j + 1))
                    sp.sem_inc(s_aout, 1)

            @block.vector
            def _(dve):
                ch = Chain(dve, s_self)
                dve.sem_inc(s_aout, 1)
                dve.wait_ge(s_w, 32)
                dve.sem_inc(s_taken, 1)
                with dve.Fori(0, NST) as j:
                    ch(dve.tensor_copy(XS[:, :, :], K["X"][:, bass.ds(j * ST, ST), :]))
                    dve.sem_inc(s_xs, 1)
                    for i in range(ST):
                        dve.wait_ge(s_row, ST * j + i + 1)
                        f = ROW[:, i, 0:GH].rearrange("p (h o) -> p h o", h=HEADS)
                        ch(dve.tensor_tensor(PR[:, :, :], f, AV[:, :, 0, :], ALU.mult))
                        ch(dve.tensor_reduce(ROW[:, i, GH:], PR[:, :, :], AX.X, ALU.add))
                        ch(dve.tensor_tensor(PR[:, :, :], f, AV[:, :, 1, :], ALU.mult))
                        ch(dve.tensor_reduce(BM[:, bass.ds(j * ST + i, 1), 0:HEADS], PR[:, :, :].unsqueeze(1), AX.X, ALU.add))
                    dve.sem_inc(s_sc, 1)
                    ch.reset()

            @block.scalar
            def _(act):
                for k in range(4):
                    act.sem_inc(s_free[k], 1)
                with act.Fori(0, NST) as j:
                    for kb in range(2):
                        act.wait_ge(s_full[kb], (2 - kb) * j + 1)
                        for a, b in HALVES:
                            act.activation(XT[:, kb, b], PS[kb][:, a], ACT.Copy).then_inc(s_xt, 1)
                        act.wait_ge(s_xt, 4 * j + 2 * kb + 2)
                        act.sem_inc(s_free[kb], 1)
                    act.wait_ge(s_aout, j + 1)
                    act.sem_inc(s_taken, 1)
                    for i in range(ST):
                        k, per, nth = 2 + i % 2, 3 - i % 2, i // 2
                        act.wait_ge(s_full[k], per * j + nth + 1)
                        act.activation(ROW[:, i, 0:GH], PS[k][:, 0:GH], ACT.Copy).then_inc(s_row, 1)
                        act.wait_ge(s_row, ST * j + i + 1)
                        act.sem_inc(s_free[k], 1)
                    act.wait_ge(s_full[0], 2 * j + 2)
                    for a, b in HALVES:
                        act.activation(AS[:, b], PS[0][0:HEADS, a], ACT.Copy).then_inc(s_as2, 1)
                    act.wait_ge(s_as2, 2 * j + 2)
                    act.sem_inc(s_free[0], 1)
                    act.sem_inc(s_as, 1)

            @block.tensor
            def _(pe):
                pe.wait_ge(s_w, 32)
                pe.sem_inc(s_taken, 1)
                with pe.Fori(0, NST) as j:
                    pe.wait_ge(s_xs, j + 1)
                    for kb in range(2):
                        pe.wait_ge(s_free[kb], (2 - kb) * j + 1)
                        transposed(pe, K["I32"][:, :], PS[kb], XS, ST, kb * P).then_inc(s_full[kb], 1)
                    pe.wait_ge(s_xt, 4 * j + 4)
                    for i in range(ST):
                        k, per, nth = 2 + i % 2, 3 - i % 2, i // 2
                        pe.wait_ge(s_free[k], per * j + nth + 1)
                        for kb in range(2):
                            m = pe.matmul(PS[k][:, 0:GH], XT[:, kb, i * P:(i + 1) * P], W[:, kb, :], start=kb == 0, stop=kb == 1)
                        m.then_inc(s_full[k], 1)
                    pe.wait_ge(s_sc, j + 1)
                    pe.wait_ge(s_free[0], 2 * j + 2)
                    for i in range(ST):
                        m = pe.transpose(PS[0][0:HEADS, cols(i)], ROW[:, i, GH:GW], K["I32"][:, :])
                    m.then_inc(s_full[0], 1)

        n_ = lambda x: sem("gm_" + x)
        s_ab, s_c, s_cf, s_ps, s_psf, s_self, s_bm, s_bo, s_taken = (n_(x) for x in (
            "scores_in", "c_in", "c_free", "ps", "ps_free", "self", "bm", "bm_out", "taken"))
        NEG = -1e30
        with nc.sbuf_tensor("gm_ab", [P, HEADS, NP], F32) as AB, nc.sbuf_tensor("gm_c", [P, 2, TILES, P], F16) as C, \
                nc.sbuf_tensor("gm_mask", [P, NP], BF16) as MK, nc.sbuf_tensor("gm_junk", [P, NP], BF16) as J, \
                nc.sbuf_tensor("gm_am", [P, HEADS], F32) as AM, nc.sbuf_tensor("gm_t", [P, TILES, HEADS], F32) as TM, \
                nc.Block() as block:
            @block.sync
            def _(sp):
                for h in range(HEADS):
                    sp.dma_start(AB[:, h, :], row_bc(T["gat_at"][h, :])).then_inc(s_ab, 16)
                cv = T["counts"][0:NP * NP, :].rearrange("(s p t c) a -> t p s (c a)", s=TILES, p=P, c=P)
                with sp.Fori(0, TILES) as t:
                    sp.wait_ge(s_cf, t + 1)
                    sp.dma_start(C[:, 0, :, :], cv[bass.ds(t, 1), :, :, :].rearrange("a p s c -> (a p) s c")).then_inc(s_c, 16)
                sp.wait_ge(s_bm, 1)
                sp.dma_start(T["gat_dst"].rearrange("(t p) w -> p t w", p=P), BM[:, :, :]).then_inc(s_bo, 16)
                sp.wait_ge(s_bo, 16)

            @block.tensor
            def _(pe):
                pe.sem_inc(s_cf, 1)
                pe.sem_inc(s_psf, 1)
                with pe.Fori(0, TILES) as t:
                    pe.wait_ge(s_c, 16 * (t + 1))
                    pe.wait_ge(s_psf, t + 1)
                    pe.sem_inc(s_taken, 1)
                    for s in range(TILES):
                        o = PS[s // 16][:, :].bitcast(F16)[:, (s % 16) * P:(s % 16 + 1) * P]
                        m = pe.transpose(o, C[:, 0, s, :], K["I16"][:, :])
                    m.then_inc(s_ps, 1)
                    pe.wait_ge(s_ps, t + 1)
                    pe.sem_inc(s_cf, 1)

            @block.vector
            def _(dve):
                ch = Chain(dve, s_self)
                dve.wait_ge(s_ab, 16 * HEADS)
                with dve.Fori(0, TILES) as t:
                    dve.wait_ge(s_ps, t + 1)
                    ch(dve.tensor_scalar(MK[:, 0:16 * P], PS[0][:, :].bitcast(F16), 0.0, NEG, ALU.is_equal, ALU.mult))
                    ch(dve.tensor_scalar(MK[:, 16 * P:], PS[1][:, :].bitcast(F16)[:, 0:NP - 16 * P], 0.0, NEG, ALU.is_equal, ALU.mult))
                    dve.sem_inc(s_psf, 1)
                    for h in range(HEADS):
                        ch(dve.tensor_tensor_reduce(out=J[:, :], in0=MK[:, :], in1=AB[:, h, :], scale=1.0, scalar=NEG,
                                                    op0=ALU.add, op1=ALU.max, accum_out=AM[:, h:h + 1]))
                    ch(dve.tensor_copy(BM[:, bass.ds(t, 1), HEADS:], AM[:, :].unsqueeze(1)))
                    ch.reset()
                ch(dve.tensor_tensor(TM[:, :, :], BM[:, :, 0:HEADS], BM[:, :, HEADS:], ALU.add))
                ch(dve.scalar_tensor_tensor(out=BM[:, :, HEADS:], in0=TM[:, :, :], scalar=0.2, in1=TM[:, :, :], op0=ALU.mult, op1=ALU.max))
                dve.sem_inc(s_bm, 1)
    sem.clear()


def merge_rows(pe, S, M, ps, width):
    m = pe.matmul(ps[:, 0:min(width, 512)], S, M[:, 0:min(width, 512)], start=True, stop=True)
    if width > 512:
        m = pe.matmul(ps[:, 512:width], S, M[:, 512:width], start=True, stop=True)
    return m


def gat_edges(nc, A, T, K, PS):
    sem = Semaphores(nc)
    ks = range(RING)
    n_ = lambda x: [sem(f"ge_{x}{k}") for k in ks]
    s_g, s_h, s_id, s_e, s_x, s_m, s_pe, s_o, s_rin, s_rf, s_ix = (n_(x) for x in (
        "src_in", "dst_in", "ids", "score", "exp", "msg", "merged", "row", "targets_in", "targets_free", "index"))
    s_sc = T["scat"]
    s_self, s_taken, s_taken2, s_oh = sem("ge_self"), sem("ge_taken"), sem("ge_taken2"), sem("ge_oh")
    drow = A["dst_row"].rearrange("(c n) -> c n", n=P)
    with nc.sbuf_tensor("ge_g", [P, RING, GW], F32) as G, nc.sbuf_tensor("ge_h", [P, RING, 2 * HEADS], F32) as H, \
            nc.sbuf_tensor("ge_m", [P, RING, GW], F32) as M, nc.sbuf_tensor("ge_o", [P, RING, GW], F32) as O, \
            nc.sbuf_tensor("ge_s", [P, RING, P], F32) as S, nc.sbuf_tensor("ge_j", [P, RING, P], F32) as J, \
            nc.sbuf_tensor("ge_r", [P, RING, P], I32) as R, nc.sbuf_tensor("ge_id", [P, RING, 2], I32) as ID, \
            nc.sbuf_tensor("ge_e", [P, RING, 3, HEADS], F32) as E, nc.sbuf_tensor("ge_c", [P, RING, 4], F32) as CN, \
            nc.sbuf_tensor("ge_ix", [P, RING], I32) as IX, nc.Block() as block:
        @block.sync
        def _(sp):
            with sp.Fori(0, ROUNDS) as it:
                for k in ks:
                    sp.wait_ge(s_rf[k], it + 1)
                    sp.dma_start(R[:, k, :], row_bc(drow[bass.ds(it * RING + k, 1), :].rearrange("a n -> (a n)"))).then_inc(s_rin[k], 16)

        @block.gpsimd
        def _(pool):
            def gather(k, n):
                pool.wait_ge(s_id[k], n)
                pool.wait_ge(s_m[k], n)
                pool.sem_inc(s_taken, 1)
                pool.indirect_dma_start(out=G[:, k, :], out_offset=None, in_=T["gat_src"],
                                        in_offset=bass.IndirectOffsetOnAxis(ap=ID[:, k, 0:1], axis=0)).then_inc(s_g[k], 16)
                pool.indirect_dma_start(out=H[:, k, :], out_offset=None, in_=T["gat_dst"],
                                        in_offset=bass.IndirectOffsetOnAxis(ap=ID[:, k, 1:2], axis=0)).then_inc(s_h[k], 16)

            def scatter(k, n):
                pool.wait_ge(s_o[k], n)
                pool.sem_inc(s_taken, 1)
                pool.indirect_dma_start(out=T["acc1"][k], out_offset=bass.IndirectOffsetOnAxis(ap=IX[:, k:k + 1], axis=0),
                                        in_=O[:, k, :], in_offset=None, compute_op=ALU.add).then_inc(s_sc[k], 16)

            for k in ks:
                gather(k, 1)
            with pool.Fori(0, ROUNDS - 1) as it:
                for k in ks:
                    gather(k, it + 2)
                    scatter(k, it + 1)
            for k in ks:
                scatter(k, ROUNDS)
            for k in ks:
                pool.wait_ge(s_sc[k], 16 * (ROUNDS + 1))

        @block.vector
        def _(dve):
            ch = Chain(dve, s_self)
            for k in ks:
                ch(dve.tensor_copy(ID[:, k, 0:1], K["srci"][:, k:k + 1]))
                ch(dve.tensor_copy(ID[:, k, 1:2], K["dsti"][:, k:k + 1]))
                dve.sem_inc(s_id[k], 1)
                dve.sem_inc(s_m[k], 1)
                dve.sem_inc(s_rf[k], 1)
            ch.reset()
            with dve.Fori(0, ROUNDS) as it:
                for k in ks:
                    c = it * RING + k
                    dve.wait_ge(s_g[k], 16 * (it + 1))
                    dve.wait_ge(s_h[k], 16 * (it + 1))
                    dve.sem_inc(s_taken2, 1)
                    dve.tensor_copy(ID[:, k, 0:1], K["srci"][:, bass.ds(c + RING, 1)])
                    ch(dve.tensor_copy(CN[:, k, 0:1], K["dstf"][:, bass.ds(c, 1)]))
                    ch(dve.tensor_copy(ID[:, k, 1:2], K["dsti"][:, bass.ds(c + RING, 1)]))
                    dve.sem_inc(s_id[k], 1)
                    ch(dve.tensor_tensor(E[:, k, 0, :], G[:, k, GH:], H[:, k, 0:HEADS], ALU.add))
                    ch(dve.scalar_tensor_tensor(out=E[:, k, 1, :], in0=E[:, k, 0, :], scalar=0.2, in1=E[:, k, 0, :], op0=ALU.mult, op1=ALU.max))
                    ch(dve.tensor_tensor(E[:, k, 2, :], E[:, k, 1, :], H[:, k, HEADS:], ALU.subtract))
                    dve.sem_inc(s_e[k], 1)
                    same_target(dve, ch, K, R[:, k, :], S[:, k, :], J[:, k, :], CN[:, k, :], s_rin[k], it, s_sc[k], IX[:, k:k + 1])
                    dve.sem_inc(s_rf[k], 1)
                    dve.wait_ge(s_x[k], it + 1)
                    ch(dve.tensor_tensor(M[:, k, 0:GH].rearrange("p (h o) -> p h o", h=HEADS),
                                         G[:, k, 0:GH].rearrange("p (h o) -> p h o", h=HEADS),
                                         M[:, k, GH:].unsqueeze(2).broadcast_to([P, HEADS, HID]), ALU.mult))
                    dve.sem_inc(s_m[k], 1)
                ch.reset()

        @block.scalar
        def _(act):
            def exp(k, it):
                act.wait_ge(s_e[k], it + 1)
                act.activation(M[:, k, GH:], E[:, k, 2, :], ACT.Exp).then_inc(s_x[k], 1)

            def evacuate(k, it):
                act.wait_ge(s_pe[k], it + 1)
                act.activation(O[:, k, 0:GH], PS[k][:, 0:GH], ACT.Copy).then_inc(s_oh, 1)
                act.activation(O[:, k, GH:], PS[k][:, 512:512 + HEADS], ACT.Copy).then_inc(s_oh, 1)
                act.wait_ge(s_oh, 2 * (RING * it + k + 1))
                act.sem_inc(s_o[k], 1)

            with act.Fori(0, ROUNDS) as it:
                exp(0, it)
                for k in range(1, RING):
                    exp(k, it)
                    evacuate(k - 1, it)
                evacuate(RING - 1, it)

        @block.tensor
        def _(pe):
            with pe.Fori(0, ROUNDS) as it:
                for k in ks:
                    pe.wait_ge(s_m[k], it + 2)
                    merge_rows(pe, S[:, k, :], M[:, k, :], PS[k], GW).then_inc(s_pe[k], 1)
    sem.clear()


def same_target(dve, ch, K, row, S, J, CN, s_in, it, s_scattered, index):
    dve.wait_ge(s_in, 16 * (it + 1))
    dve.wait_ge(s_scattered, 16 * (it + 1))
    ch(dve.tensor_scalar(S, row, CN[:, 0:1], None, ALU.is_equal))
    e0 = (RING - 1) * P
    ch(dve.scalar_tensor_tensor(out=J, in0=S, scalar=1.0, in1=K["early"][:, e0:e0 + P], op0=ALU.mult, op1=ALU.mult,
                                accum_out=CN[:, 1:2]))
    ch(dve.tensor_scalar(CN[:, 2:3], CN[:, 1:2], 0.5, None, ALU.is_gt))
    ch(dve.tensor_tensor(CN[:, 3:4], K["trash_row"][:, :], CN[:, 0:1], ALU.subtract))
    ch(dve.scalar_tensor_tensor(out=index, in0=CN[:, 3:4], scalar=CN[:, 2:3], in1=CN[:, 0:1], op0=ALU.mult, op1=ALU.add))


def gat_out(nc, A, T, K, PS):
    sem = Semaphores(nc)
    n_ = lambda x: sem("go_" + x)
    s_w, s_in, s_free_in, s_self, s_o, s_xt, s_xth, s_y, s_x, s_taken = (n_(x) for x in (
        "w", "in", "in_free", "self", "o", "xt", "xth", "y", "exp", "taken"))
    s_full, s_free = [n_(f"full{k}") for k in range(4)], [n_(f"free{k}") for k in range(4)]
    with nc.sbuf_tensor("go_acc", [P, RING, ST, GW], F32) as AC, nc.sbuf_tensor("go_w", [P, 4, D], F32) as W, \
            nc.sbuf_tensor("go_b", [P, 1, D], F32) as B, nc.sbuf_tensor("go_o", [P, ST, GH], F32) as O, \
            nc.sbuf_tensor("go_d", [P, ST, HEADS], F32) as DN, nc.sbuf_tensor("go_xt", [P, 4, SW], F32) as XT, \
            nc.sbuf_tensor("go_y", [P, ST, D], F32) as Y, nc.sbuf_tensor("go_n", [P, ST, D], F32) as N, \
            nc.sbuf_tensor("go_e", [P, ST, D], F32) as E, nc.Block() as block:
        @block.sync
        def _(sp):
            sp.dma_start(W[:, :, :], A["L1_gnn_Wo"].rearrange("(k p) n -> p k n", p=P)).then_inc(s_w, 16)
            sp.dma_start(B[:, 0, :], row_bc(A["L1_gnn_bo"])).then_inc(s_w, 16)
            with sp.Fori(0, NST) as j:
                sp.wait_ge(s_free_in, j + 1)
                for k in range(RING):
                    v = T["acc1"][k][0:NP, :].rearrange("(j t p) w -> j p t w", t=ST, p=P)
                    sp.dma_start(AC[:, k, :, :], v[bass.ds(j, 1), :, :, :].rearrange("a p t w -> (a p) t w")).then_inc(s_in, 16)

        @block.vector
        def _(dve):
            ch = Chain(dve, s_self)
            dve.sem_inc(s_free_in, 1)
            dve.wait_ge(s_w, 32)
            ch(dve.memset(DN[:, :, :], 0.0))
            ch.reset()
            with dve.Fori(0, NST) as j:
                dve.wait_ge(s_in, 16 * RING * (j + 1))
                for k in range(1, RING):
                    ch(dve.tensor_tensor(AC[:, 0, :, :], AC[:, 0, :, :], AC[:, k, :, :], ALU.add))
                ch(dve.tensor_scalar(DN[:, :, :], AC[:, 0, :, GH:], 1e-16, None, ALU.add))
                ch(dve.reciprocal(DN[:, :, :], DN[:, :, :]))
                for i in range(ST):
                    ch(dve.tensor_tensor(O[:, i, :].rearrange("p (h o) -> p h o", h=HEADS),
                                         AC[:, 0, i, 0:GH].rearrange("p (h o) -> p h o", h=HEADS),
                                         DN[:, i, :].unsqueeze(2).broadcast_to([P, HEADS, HID]), ALU.mult))
                dve.sem_inc(s_free_in, 1)
                dve.sem_inc(s_o, 1)
                for i in range(ST):
                    k, per, nth = i % 2, 4 - i % 2, 1 + i // 2
                    dve.wait_ge(s_full[k], per * j + nth + 1)
                    ch(dve.tensor_tensor(Y[:, i, :], PS[k][:, 0:D], B[:, 0, :], ALU.add))
                    dve.sem_inc(s_free[k], 1)
                ch(dve.tensor_scalar(N[:, :, :], Y[:, :, :], 0.0, None, ALU.min))
                dve.sem_inc(s_y, 1)
                ch(dve.tensor_scalar(Y[:, :, :], Y[:, :, :], 0.0, -1.0, ALU.max, ALU.add))
                dve.wait_ge(s_x, j + 1)
                ch(dve.tensor_tensor(Y[:, :, :], Y[:, :, :], E[:, :, :], ALU.add))
                xs = K["X"][:, bass.ds(j * ST, ST), :]
                ch(dve.tensor_tensor(xs, xs, Y[:, :, :], ALU.add))
                ch.reset()

        @block.scalar
        def _(act):
            for k in range(4):
                act.sem_inc(s_free[k], 1)
            with act.Fori(0, NST) as j:
                for kb in range(4):
                    per = (4, 3, 1, 1)[kb]
                    act.wait_ge(s_full[kb], per * j + 1)
                    for a, b in HALVES:
                        act.activation(XT[:, kb, b], PS[kb][:, a], ACT.Copy).then_inc(s_xth, 1)
                    act.wait_ge(s_xth, 8 * j + 2 * kb + 2)
                    act.sem_inc(s_free[kb], 1)
                act.sem_inc(s_xt, 1)
                act.wait_ge(s_y, j + 1)
                act.activation(E[:, :, :], N[:, :, :], ACT.Exp).then_inc(s_x, 1)

        @block.tensor
        def _(pe):
            pe.wait_ge(s_w, 32)
            pe.sem_inc(s_taken, 1)
            with pe.Fori(0, NST) as j:
                pe.wait_ge(s_o, j + 1)
                for kb in range(4):
                    pe.wait_ge(s_free[kb], (4, 3, 1, 1)[kb] * j + 1)
                    transposed(pe, K["I32"][:, :], PS[kb], O, ST, kb * P).then_inc(s_full[kb], 1)
                pe.wait_ge(s_xt, j + 1)
                for i in range(ST):
                    k, per, nth = i % 2, 4 - i % 2, 1 + i // 2
                    pe.wait_ge(s_free[k], per * j + nth + 1)
                    for kb in range(4):
                        m = pe.matmul(PS[k][:, 0:D], XT[:, kb, i * P:(i + 1) * P], W[:, kb, :], start=kb == 0, stop=kb == 3)
                    m.then_inc(s_full[k], 1)
    final_norm(nc, K, "gat_ln", None)
    sem.clear()


def deep_gin(nc, A, T, K, PS):
    sem = Semaphores(nc)
    KB = F2 // P
    s_self = sem("dg_self")
    with nc.sbuf_tensor("dg_wf", [P, 2 + LAYERS * KB, D], F32) as WF, nc.sbuf_tensor("dg_ob", [P, D], F32) as OB:
        fold_output(nc, A, K, PS, WF, OB)
        n_ = lambda x: sem("dg_" + x)
        s_w, s_xs, s_xt, s_taken, s_hl, s_tabout, s_drain = (n_(x) for x in ("w", "xs", "xt", "taken", "split", "tab_out", "drained"))
        s_full, s_free = [n_(f"sfull{k}") for k in range(4)], [n_(f"sfree{k}") for k in range(4)]
        tab_d = T["tab2"].rearrange("(j t p) w -> j p t w", t=ST, p=P)

        def rows_out(dve, ch, ps, i, j, BR, HF, HL):
            ch(dve.tensor_tensor(HF[:, :], ps[:, 0:F2], BR[:, :], ALU.add))
            xs = K["X"][:, bass.ds(j * ST + i, 1), :]
            ch(dve.tensor_tensor(xs, xs, ps[:, 512:512 + D].unsqueeze(1), ALU.add))

        with nc.sbuf_tensor("dg_win", [P, 2, F2], F32) as W, nc.sbuf_tensor("dg_brow", [P, F2], F32) as BR, \
                nc.sbuf_tensor("dg_xs", [P, ST, D], F32) as XS, nc.sbuf_tensor("dg_xt", [P, 2, SW], F32) as XT, \
                nc.sbuf_tensor("dg_hf0", [P, F2], F32) as HF, nc.sbuf_tensor("dg_hl0", [P, ST, 2 * F2], F16) as HL, \
                nc.Block() as block:
            @block.sync
            def _(sp):
                sp.dma_start(W[:, :, :], A["L2_gnn_in_W"].rearrange("(k p) n -> p k n", p=P)).then_inc(s_w, 16)
                sp.dma_start(BR[:, :], row_bc(A["L2_gnn_in_b"])).then_inc(s_w, 16)
                with sp.Fori(0, NST) as j:
                    sp.wait_ge(s_hl, j + 1)
                    sp.dma_start(tab_d[bass.ds(j, 1), :, :, :].rearrange("a p t w -> (a p) t w"), HL[:, :, :]).then_inc(s_tabout, 16)
                    sp.wait_ge(s_tabout, 16 * (j + 1))
                    sp.sem_inc(s_drain, 1)

            @block.vector
            def _(dve):
                ch = Chain(dve, s_self)
                dve.sem_inc(s_drain, 1)
                dve.wait_ge(s_w, 32)
                with dve.Fori(0, NST) as j:
                    ch(dve.tensor_copy(XS[:, :, :], K["X"][:, bass.ds(j * ST, ST), :]))
                    dve.sem_inc(s_xs, 1)
                    mine = K["X"][:, bass.ds(j * ST, ST), :]
                    ch(dve.tensor_tensor(mine, mine, OB[:, :].unsqueeze(1).broadcast_to([P, ST, D]), ALU.add))
                    dve.wait_ge(s_drain, j + 1)
                    for i in range(ST):
                        k, per, nth = 2 + i % 2, 3 - i % 2, i // 2
                        dve.wait_ge(s_full[k], per * j + nth + 1)
                        rows_out(dve, ch, PS[k], i, j, BR, HF, HL)
                        dve.sem_inc(s_free[k], 1)
                        split16(ch, dve, HF[:, :], HL[:, i, 0:F2], HL[:, i, F2:])
                    dve.sem_inc(s_hl, 1)
                    ch.reset()

            @block.scalar
            def _(act):
                for k in range(4):
                    act.sem_inc(s_free[k], 1)
                with act.Fori(0, NST) as j:
                    for kb in range(2):
                        act.wait_ge(s_full[kb], j + 1)
                        for a, b in HALVES:
                            act.activation(XT[:, kb, b], PS[kb][:, a], ACT.Copy).then_inc(s_xt, 1)
                        act.wait_ge(s_xt, 4 * j + 2 * kb + 2)
                        act.sem_inc(s_free[kb], 1)

            @block.tensor
            def _(pe):
                pe.wait_ge(s_w, 32)
                pe.sem_inc(s_taken, 1)
                with pe.Fori(0, NST) as j:
                    pe.wait_ge(s_xs, j + 1)
                    for kb in range(2):
                        pe.wait_ge(s_free[kb], j + 1)
                        transposed(pe, K["I32"][:, :], PS[kb], XS, ST, kb * P).then_inc(s_full[kb], 1)
                    pe.wait_ge(s_xt, 4 * j + 4)
                    for i in range(ST):
                        k, per, nth = 2 + i % 2, 3 - i % 2, i // 2
                        pe.wait_ge(s_free[k], per * j + nth + 1)
                        for kb in range(2):
                            pe.matmul(PS[k][:, 0:F2], XT[:, kb, i * P:(i + 1) * P], W[:, kb, :], start=kb == 0, stop=kb == 1)
                        for kb in range(2):
                            m = pe.matmul(PS[k][:, 512:512 + D], XT[:, kb, i * P:(i + 1) * P], WF[:, kb, :], start=kb == 0, stop=kb == 1)
                        m.then_inc(s_full[k], 1)

        s_tab, s_w, s_taken, s_hl, s_tabout, s_zt, s_ut = (n_("l" + x) for x in ("tab_in", "w", "taken", "split", "tab_out", "zt", "ut"))
        s_drain = n_("ldrained")
        s_cin, s_cout = [n_(f"c_in{q}") for q in range(ST)], [n_(f"c_out{q}") for q in range(ST)]
        s_full, s_free = [n_(f"full{k}") for k in range(4)], [n_(f"free{k}") for k in range(4)]
        NW = 4
        with nc.sbuf_tensor("dg_tab", [P, TILES, 2 * F2], F16) as TAB, \
                nc.sbuf_tensor("dg_c", [P, ST, ST, SW], F16) as C, \
                nc.sbuf_tensor("dg_w1", [P, KB, F2], F32) as W1, nc.sbuf_tensor("dg_w2", [P, KB, F2], F32) as W2, \
                nc.sbuf_tensor("dg_b1", [P, KB], F32) as B1, nc.sbuf_tensor("dg_b2", [P, F2], F32) as BR, \
                nc.sbuf_tensor("dg_hf", [P, F2], F32) as HF, nc.sbuf_tensor("dg_hl", [P, ST, 2 * F2], F16) as HL, \
                nc.sbuf_tensor("dg_zt", [P, KB, SW], F32) as ZT, nc.sbuf_tensor("dg_ut", [P, KB, SW], F32) as UT, \
                nc.Block() as block:
            @block.sync
            def _(sp):
                with sp.Fori(0, LAYERS) as l:
                    one = bass.ds(l, 1)
                    sp.wait_ge(s_drain, NST * l + 1)
                    sp.dma_start(TAB[:, :, :], T["tab2"].rearrange("(t p) w -> p t w", p=P)).then_inc(s_tab, 16)
                    for dst, name in ((W1, "L2_gnn_conv_W1"), (W2, "L2_gnn_conv_W2")):
                        sp.dma_start(dst[:, :, :], A[name][one, :, :].rearrange("a (k p) n -> p (a k) n", p=P)).then_inc(s_w, 16)
                    sp.dma_start(B1[:, :], A["L2_gnn_conv_b1"][one, :, :].rearrange("a p k -> (a p) k")).then_inc(s_w, 16)
                    sp.dma_start(BR[:, :], row_bc(A["L2_gnn_conv_b2"][one, :].rearrange("a n -> (a n)"))).then_inc(s_w, 16)
                    with sp.Fori(0, NST) as j:
                        load_counts(sp, T, C, s_cin, s_cout, j, l * NST + j)

            @block.gpsimd
            def _(pool):
                pool.sem_inc(s_drain, 1)
                with pool.Fori(0, LAYERS) as l:
                    with pool.Fori(0, NST) as j:
                        g = l * NST + j
                        pool.wait_ge(s_hl, g + 1)
                        pool.sem_inc(s_taken, 1)
                        pool.dma_start(tab_d[bass.ds(j, 1), :, :, :].rearrange("a p t w -> (a p) t w"), HL[:, :, :]).then_inc(s_tabout, 16)
                        pool.wait_ge(s_tabout, 16 * (g + 1))
                        pool.sem_inc(s_drain, 1)

            @block.vector
            def _(dve):
                ch = Chain(dve, s_self)
                with dve.Fori(0, LAYERS) as l:
                    dve.wait_ge(s_w, 16 * NW * (l + 1))
                    dve.sem_inc(s_taken, 1)
                    with dve.Fori(0, NST) as j:
                        g = l * NST + j
                        dve.wait_ge(s_drain, g + 1)
                        for i in range(ST):
                            k = 2 + i % 2
                            per, nth = (5, 2 + i // 2) if k == 2 else (4, 2 + i // 2)
                            dve.wait_ge(s_full[k], per * g + nth + 1)
                            rows_out(dve, ch, PS[k], i, j, BR, HF, HL)
                            dve.sem_inc(s_free[k], 1)
                            split16(ch, dve, HF[:, :], HL[:, i, 0:F2], HL[:, i, F2:])
                        dve.sem_inc(s_hl, 1)
                        ch.reset()

            @block.scalar
            def _(act):
                for q in range(ST):
                    act.sem_inc(s_cout[q], 1)
                for k in range(4):
                    act.sem_inc(s_free[k], 1)
                with act.Fori(0, LAYERS) as l:
                    act.wait_ge(s_w, 16 * NW * (l + 1))
                    act.sem_inc(s_taken, 1)
                    with act.Fori(0, NST) as j:
                        g = l * NST + j
                        for fb in range(KB):
                            act.wait_ge(s_full[fb % 2], 2 * g + fb // 2 + 1)
                            for a, b in HALVES:
                                act.activation(ZT[:, fb, b], PS[fb % 2][:, a], ACT.Copy).then_inc(s_zt, 1)
                            act.wait_ge(s_zt, 2 * KB * g + 2 * fb + 2)
                            act.sem_inc(s_free[fb % 2], 1)
                        for hb in range(KB):
                            k = 2 + hb % 2
                            act.wait_ge(s_full[k], (5 - hb % 2) * g + hb // 2 + 1)
                            for a, b in HALVES:
                                act.activation(UT[:, hb, b], PS[k][:, a], ACT.Relu, bias=B1[:, hb:hb + 1]).then_inc(s_ut, 1)
                            act.wait_ge(s_ut, 2 * KB * g + 2 * hb + 2)
                            act.sem_inc(s_free[k], 1)

            @block.tensor
            def _(pe):
                with pe.Fori(0, LAYERS) as l:
                    pe.wait_ge(s_w, 16 * NW * (l + 1))
                    pe.wait_ge(s_tab, 16 * (l + 1))
                    pe.sem_inc(s_taken, 1)
                    with pe.Fori(0, NST) as j:
                        g = l * NST + j
                        for fb in range(KB):
                            ps = PS[fb % 2]

                            def own():
                                for i in range(ST):
                                    for part in range(2):
                                        a = part * F2 + fb * P
                                        w = TAB[:, bass.ds(j * ST + i, 1), a:a + P].rearrange("p a w -> p (a w)")
                                        pe.matmul(ps[:, cols(i)], w, K["I16"][:, :], start=False, stop=False, skip_group_check=True)
                            pe.wait_ge(s_free[fb % 2], 2 * g + fb // 2 + 1)
                            neighbour_sum(pe, TAB, C, ps, fb, F2, s_cin, s_cout, g, fb == KB - 1, own).then_inc(s_full[fb % 2], 1)
                        pe.wait_ge(s_zt, 2 * KB * (g + 1))
                        pe.sem_inc(s_cout[ST - 1], 1)
                        for hb in range(KB):
                            k = 2 + hb % 2
                            pe.wait_ge(s_free[k], (5 - hb % 2) * g + hb // 2 + 1)
                            for a, b in HALVES:
                                for kb in range(KB):
                                    m = pe.matmul(PS[k][:, a], W1[:, kb, hb * P:(hb + 1) * P], ZT[:, kb, b],
                                                  start=kb == 0, stop=kb == KB - 1)
                            m.then_inc(s_full[k], 1)
                        pe.wait_ge(s_ut, 2 * KB * (g + 1))
                        for i in range(ST):
                            k = 2 + i % 2
                            per, nth = (5, 2 + i // 2) if k == 2 else (4, 2 + i // 2)
                            pe.wait_ge(s_free[k], per * g + nth + 1)
                            for kb in range(KB):
                                pe.matmul(PS[k][:, 0:F2], UT[:, kb, i * P:(i + 1) * P], W2[:, kb, :], start=kb == 0, stop=kb == KB - 1)
                            for kb in range(KB):
                                wf = WF[:, bass.ds(2 + KB * l + kb, 1), :].rearrange("p a n -> p (a n)")
                                m = pe.matmul(PS[k][:, 512:512 + D], UT[:, kb, i * P:(i + 1) * P], wf, start=kb == 0, stop=kb == KB - 1)
                            m.then_inc(s_full[k], 1)
    final_norm(nc, K, "dg_ln", None)
    sem.clear()


def fold_output(nc, A, K, PS, WF, OB):
    sem = Semaphores(nc)
    n_ = lambda x: sem("fo_" + x)
    s_w, s_b, s_self, s_full, s_free, s_bb, s_bf = (n_(x) for x in ("w", "b", "self", "full", "free", "bias", "bias_full"))
    KB = F2 // P
    with nc.sbuf_tensor("fo_wt", [P, KB, F2], F32) as WT, nc.sbuf_tensor("fo_wo", [P, LAYERS + 1, KB, D], F32) as WO, \
            nc.sbuf_tensor("fo_b", [P, LAYERS + 1, KB], F32) as B, nc.sbuf_tensor("fo_bb", [P, LAYERS + 1, KB, P], F32) as BB, \
            nc.Block() as block:
        @block.sync
        def _(sp):
            sp.dma_start(WO[:, :, :, :].rearrange("p l k n -> p (l k) n"),
                         A["L2_gnn_out_W"].rearrange("(k p) n -> p k n", p=P)).then_inc(s_b, 16)
            sp.dma_start(B[:, 0, :], A["L2_gnn_in_bc"]).then_inc(s_b, 16)
            for l in range(LAYERS):
                sp.dma_start(B[:, l + 1, :], A["L2_gnn_conv_b2c"][l]).then_inc(s_b, 16)
            sp.dma_start(OB[:, :], row_bc(A["L2_gnn_out_b"])).then_inc(s_b, 16)
            sp.dma_start(WT[:, :, 0:D], A["L2_gnn_in_WT"].rearrange("(k p) n -> p k n", p=P)).then_inc(s_w, 16)
            for l in range(LAYERS):
                sp.wait_ge(s_free, 2 + KB * l)
                sp.dma_start(WT[:, :, :], A["L2_gnn_conv_W2T"][l].rearrange("(k p) n -> p k n", p=P)).then_inc(s_w, 16)

        @block.tensor
        def _(pe):
            pe.wait_ge(s_b, 16 * (LAYERS + 3))
            n = 0
            for l in range(LAYERS + 1):
                pe.wait_ge(s_w, 16 * (l + 1))
                for ib in range(2 if l == 0 else KB):
                    if n >= 2:
                        pe.wait_ge(s_free, n - 1)
                    for kb in range(KB):
                        m = pe.matmul(PS[n % 2][:, 0:D], WT[:, kb, ib * P:(ib + 1) * P], WO[:, l, kb, :], start=kb == 0, stop=kb == KB - 1)
                    m.then_inc(s_full, 1)
                    n += 1
            pe.wait_ge(s_bb, 1)
            for l in range(LAYERS + 1):
                for kb in range(KB):
                    m = pe.matmul(PS[2][:, 0:D], BB[:, l, kb, :], WO[:, l, kb, :], start=l + kb == 0, stop=l + kb == LAYERS + KB - 1)
            m.then_inc(s_bf, 1)

        @block.vector
        def _(dve):
            ch = Chain(dve, s_self)
            dve.wait_ge(s_b, 16 * (LAYERS + 3))
            for l in range(LAYERS + 1):
                for kb in range(KB):
                    ch(dve.tensor_scalar(BB[:, l, kb, :], K["ones"][:, :], B[:, l, kb:kb + 1], None, ALU.mult))
            dve.sem_inc(s_bb, 1)
            for n in range(2 + LAYERS * KB):
                dve.wait_ge(s_full, n + 1)
                dve.tensor_copy(WF[:, n, :], PS[n % 2][:, 0:D]).then_inc(s_free, 1)
            dve.wait_ge(s_bf, 1)
            ch(dve.tensor_tensor(OB[:, :], PS[2][:, 0:D], OB[:, :], ALU.add))
    sem.clear()


def att_nodes(nc, A, T, K, PS):
    sem = Semaphores(nc)
    n_ = lambda x: sem("an_" + x)
    s_w, s_self, s_taken, s_zero, s_xs, s_xt, s_ut, s_ft, s_rb, s_cb, s_cbh, s_out, s_drain = (n_(x) for x in (
        "w", "self", "taken", "zero", "xs", "xt", "ut", "ft", "rb", "cb", "cbh", "out", "drained"))
    s_full, s_free = [n_(f"full{k}") for k in range(4)], [n_(f"free{k}") for k in range(4)]
    HB = 2 * ATT
    with nc.sbuf_tensor("an_w1", [P, PH, 2, D], F32) as W1, nc.sbuf_tensor("an_w2", [P, PH, 2, P], F32) as W2, \
            nc.sbuf_tensor("an_b1", [P, PH, 2], F32) as B1, nc.sbuf_tensor("an_b2", [P, 2], F32) as B2, \
            nc.sbuf_tensor("an_a", [P, 2, 2, HB], F32) as AA, nc.sbuf_tensor("an_ab", [P, 2, HB], F32) as AB, \
            nc.sbuf_tensor("an_xs", [P, ST, D], F32) as XS, nc.sbuf_tensor("an_xt", [P, 2, SW], F32) as XT, \
            nc.sbuf_tensor("an_ut", [P, 4, SW], F32) as UT, nc.sbuf_tensor("an_ft", [P, 2, SW], F32) as FT, \
            nc.sbuf_tensor("an_rb", [P, ST, AW], F32) as RB, nc.sbuf_tensor("an_cb", [P, ST, AW + PF], F32) as CB, \
            nc.Block() as block:
        NLOAD = 2 + PH + PH + 2 * PH + 1

        @block.sync
        def _(sp):
            sp.wait_ge(s_zero, 2)
            sp.dma_start(W1[:, :, :, :].rearrange("p h k n -> p (h k) n"),
                         A["L3_gnn_W1"].rearrange("h (k p) n -> p (h k) n", p=P)).then_inc(s_w, 16)
            sp.dma_start(B2[:, :], A["L3_gnn_b2c"]).then_inc(s_w, 16)
            for h in range(PH):
                lo = h % 2 * PO
                sp.dma_start(B1[:, h, :], A["L3_gnn_b1"][h]).then_inc(s_w, 16)
                sp.dma_start(W2[:, h, :, lo:lo + PO], A["L3_gnn_W2"][h].rearrange("(k p) n -> p k n", p=P)).then_inc(s_w, 16)
                for side in range(2):
                    sp.dma_start(AA[lo:lo + PO, h // 2, side, h % 2 * ATT:(h % 2 + 1) * ATT],
                                 A["L3_gnn_A1"][h, side * PO:(side + 1) * PO, :]).then_inc(s_w, 16)
            sp.dma_start(AB[:, :, :].rearrange("p a b -> p (a b)"), row_bc(A["L3_gnn_ab1"].rearrange("h n -> (h n)"))).then_inc(s_w, 16)
            with sp.Fori(0, NST) as j:
                sp.wait_ge(s_rb, j + 1)
                v = T["att_row"].rearrange("(j t p) w -> j p t w", t=ST, p=P)
                sp.dma_start(v[bass.ds(j, 1), :, :, :].rearrange("a p t w -> (a p) t w"), RB[:, :, :]).then_inc(s_out, 16)
                sp.wait_ge(s_cb, j + 1)
                v = T["att_col"].rearrange("(j t p) w -> j p t w", t=ST, p=P)
                sp.dma_start(v[bass.ds(j, 1), :, :, :].rearrange("a p t w -> (a p) t w"), CB[:, :, :]).then_inc(s_out, 16)
                sp.wait_ge(s_out, 32 * (j + 1))
                sp.sem_inc(s_drain, 1)

        @block.vector
        def _(dve):
            ch = Chain(dve, s_self)
            dve.memset(W2[:, :, :, :], 0.0).then_inc(s_zero, 1)
            dve.memset(AA[:, :, :, :], 0.0).then_inc(s_zero, 1)
            dve.sem_inc(s_drain, 1)
            dve.wait_ge(s_w, 16 * NLOAD)
            dve.sem_inc(s_taken, 1)
            with dve.Fori(0, NST) as j:
                ch(dve.tensor_copy(XS[:, :, :], K["X"][:, bass.ds(j * ST, ST), :]))
                dve.sem_inc(s_xs, 1)
                dve.wait_ge(s_drain, j + 1)
                for i in range(ST):
                    dve.wait_ge(s_full[2], 9 * j + 4 + i + 1)
                    ch(dve.tensor_tensor(RB[:, i, :].rearrange("p (a b) -> p a b", a=2),
                                         PS[2][:, :].rearrange("p (a b) -> p a b", a=2)[:, :, 0:HB], AB[:, :, :], ALU.add))
                    dve.sem_inc(s_free[2], 1)
                dve.sem_inc(s_rb, 1)
                ch.reset()

        @block.scalar
        def _(act):
            for k in range(4):
                act.sem_inc(s_free[k], 1)
            act.wait_ge(s_w, 16 * NLOAD)
            act.sem_inc(s_taken, 1)
            with act.Fori(0, NST) as j:
                def copy(k, n, out, s_done, before, func=ACT.Copy, **kw):
                    act.wait_ge(s_full[k], n)
                    for a, b in HALVES:
                        act.activation(out[:, b], PS[k][:, a], func, **kw).then_inc(s_done, 1)
                    act.wait_ge(s_done, before + 2)
                    act.sem_inc(s_free[k], 1)
                for kb in range(2):
                    copy(kb, 2 * j + 1, XT[:, kb, :], s_xt, 4 * j + 2 * kb)
                for hp in range(2):
                    for u in range(4):
                        copy(2 + u % 2, 9 * j + 2 * hp + u // 2 + 1, UT[:, u, :], s_ut, 16 * j + 8 * hp + 2 * u,
                             ACT.Relu, bias=B1[:, 2 * hp + u // 2, u % 2:u % 2 + 1])
                    copy(hp, 2 * j + 2, FT[:, hp, :], s_ft, 4 * j + 2 * hp, ACT.Identity, bias=B2[:, hp:hp + 1])
                act.wait_ge(s_drain, j + 1)
                act.sem_inc(s_taken, 1)
                for i in range(ST):
                    act.wait_ge(s_full[3], 9 * j + 4 + i + 1)
                    pv = PS[3][:, :].rearrange("p (a b) -> p a b", a=2)
                    act.activation(CB[:, i, 0:AW].rearrange("p (a b) -> p a b", a=2), pv[:, :, 0:HB], ACT.Copy).then_inc(s_cbh, 1)
                    act.activation(CB[:, i, AW:].rearrange("p (a b) -> p a b", a=2), pv[:, :, HB:HB + P], ACT.Copy).then_inc(s_cbh, 1)
                    act.wait_ge(s_cbh, 2 * (ST * j + i + 1))
                    act.sem_inc(s_free[3], 1)
                act.sem_inc(s_cb, 1)

        @block.tensor
        def _(pe):
            pe.wait_ge(s_w, 16 * NLOAD)
            pe.sem_inc(s_taken, 1)
            with pe.Fori(0, NST) as j:
                pe.wait_ge(s_xs, j + 1)
                for kb in range(2):
                    pe.wait_ge(s_free[kb], 2 * j + 1)
                    transposed(pe, K["I32"][:, :], PS[kb], XS, ST, kb * P).then_inc(s_full[kb], 1)
                pe.wait_ge(s_xt, 4 * j + 4)
                for hp in range(2):
                    for u in range(4):
                        k = 2 + u % 2
                        pe.wait_ge(s_free[k], 9 * j + 2 * hp + u // 2 + 1)
                        for a, b in HALVES:
                            for kb in range(2):
                                m = pe.matmul(PS[k][:, a], W1[:, 2 * hp + u // 2, kb, u % 2 * P:(u % 2 + 1) * P],
                                              XT[:, kb, b], start=kb == 0, stop=kb == 1)
                        m.then_inc(s_full[k], 1)
                    pe.wait_ge(s_ut, 16 * j + 8 * hp + 8)
                    pe.wait_ge(s_free[hp], 2 * j + 2)
                    for a, b in HALVES:
                        for u in range(4):
                            m = pe.matmul(PS[hp][:, a], W2[:, 2 * hp + u // 2, u % 2, :], UT[:, u, b], start=u == 0, stop=u == 3)
                    m.then_inc(s_full[hp], 1)
                pe.wait_ge(s_ft, 4 * j + 4)
                for i in range(ST):
                    for side in range(2):
                        k = 2 + side
                        pe.wait_ge(s_free[k], 9 * j + 4 + i + 1)
                        for hp in range(2):
                            f = FT[:, hp, i * P:(i + 1) * P]
                            m = pe.matmul(PS[k][:, 512 * hp:512 * hp + HB], f, AA[:, hp, side, :], start=True, stop=True)
                            if side:
                                m = pe.matmul(PS[k][:, 512 * hp + HB:512 * hp + HB + P], f, K["I32"][:, :], start=True, stop=True)
                        m.then_inc(s_full[k], 1)
    sem.clear()


def att_edges(nc, A, T, K, PS):
    sem = Semaphores(nc)
    ks = range(RING)
    with nc.sbuf_tensor("ae_w", [P, CHUNKS, PH], F32) as WA:
        n_ = lambda x: [sem(f"ae_{x}{k}") for k in ks]
        s_r, s_c, s_id, s_used, s_spill = (n_(x) for x in ("row_in", "col_in", "ids", "used", "spilt"))
        s_w, s_self, s_taken, s_taken2 = (sem("ae_" + x) for x in ("w", "self", "taken", "taken2"))
        spill = T["spill"].rearrange("(c p) n -> c p n", p=P)
        with nc.sbuf_tensor("ae_r", [P, RING, AW], F32) as R, nc.sbuf_tensor("ae_c", [P, RING, AW + PF], F32) as C, \
                nc.sbuf_tensor("ae_rows", [P, 2, AW], F32) as RW, nc.sbuf_tensor("ae_id", [P, RING, 2], I32) as ID, \
                nc.sbuf_tensor("ae_ew", [P, CHUNKS], F32) as EW, nc.sbuf_tensor("ae_ewk", [P, RING], F32) as EWK, \
                nc.sbuf_tensor("ae_z", [P, RING, AW], F32) as Z, nc.sbuf_tensor("ae_y", [P, RING, AW], F32) as Y, \
                nc.Block() as block:
            @block.sync
            def _(sp):
                for h in range(PH):
                    sp.dma_start(RW[:, 0, h * ATT:(h + 1) * ATT], row_bc(A["L3_gnn_A1"][h, ATT - 1, :])).then_inc(s_w, 16)
                sp.dma_start(RW[:, 1, :], row_bc(A["L3_gnn_A2"].rearrange("h n a -> (h n a)"))).then_inc(s_w, 16)
                sp.dma_start(EW[:, :], A["ew_col"]).then_inc(s_w, 16)
                with sp.Fori(0, ROUNDS) as it:
                    for k in ks:
                        sp.wait_ge(s_c[k], 16 * (it + 1))
                        sp.dma_start(spill[bass.ds(it * RING + k, 1), :, :].rearrange("a p n -> (a p) n"), C[:, k, AW:]).then_inc(s_spill[k], 16)
                for k in ks:
                    sp.wait_ge(s_spill[k], 16 * ROUNDS)

            @block.gpsimd
            def _(pool):
                def gather(k, n, spilt):
                    pool.wait_ge(s_id[k], n)
                    pool.wait_ge(s_used[k], n)
                    if spilt is not None:
                        pool.wait_ge(s_spill[k], 16 * spilt)
                    pool.sem_inc(s_taken, 1)
                    pool.indirect_dma_start(out=R[:, k, :], out_offset=None, in_=T["att_row"],
                                            in_offset=bass.IndirectOffsetOnAxis(ap=ID[:, k, 0:1], axis=0)).then_inc(s_r[k], 16)
                    pool.indirect_dma_start(out=C[:, k, :], out_offset=None, in_=T["att_col"],
                                            in_offset=bass.IndirectOffsetOnAxis(ap=ID[:, k, 1:2], axis=0)).then_inc(s_c[k], 16)
                for k in ks:
                    gather(k, 1, None)
                with pool.Fori(1, ROUNDS) as it:
                    for k in ks:
                        gather(k, it + 1, it)

            @block.vector
            def _(dve):
                ch = Chain(dve, s_self)
                dve.wait_ge(s_w, 16 * (PH + 2))
                for k in ks:
                    ch(dve.tensor_copy(ID[:, k, 0:1], K["srci"][:, k:k + 1]))
                    ch(dve.tensor_copy(ID[:, k, 1:2], K["dsti"][:, k:k + 1]))
                    dve.sem_inc(s_id[k], 1)
                    dve.sem_inc(s_used[k], 1)
                ch.reset()
                with dve.Fori(0, ROUNDS) as it:
                    for k in ks:
                        c = it * RING + k
                        dve.wait_ge(s_r[k], 16 * (it + 1))
                        dve.wait_ge(s_c[k], 16 * (it + 1))
                        dve.sem_inc(s_taken2, 1)
                        dve.tensor_copy(ID[:, k, 0:1], K["srci"][:, bass.ds(c + RING, 1)])
                        ch(dve.tensor_copy(EWK[:, k:k + 1], EW[:, bass.ds(c, 1)]))
                        ch(dve.tensor_copy(ID[:, k, 1:2], K["dsti"][:, bass.ds(c + RING, 1)]))
                        dve.sem_inc(s_id[k], 1)
                        ch(dve.tensor_tensor(Z[:, k, :], R[:, k, :], C[:, k, 0:AW], ALU.add))
                        dve.sem_inc(s_used[k], 1)
                        ch(dve.scalar_tensor_tensor(out=Z[:, k, :], in0=RW[:, 0, :], scalar=EWK[:, k:k + 1], in1=Z[:, k, :],
                                                    op0=ALU.mult, op1=ALU.add))
                        ch(dve.scalar_tensor_tensor(out=Y[:, k, :], in0=Z[:, k, :], scalar=0.0, in1=RW[:, 1, :],
                                                    op0=ALU.max, op1=ALU.mult))
                        ch(dve.tensor_reduce(WA[:, bass.ds(c, 1), :], Y[:, k, :].rearrange("p (a h n) -> p a h n", a=1, h=PH),
                                             AX.X, ALU.add))
                    ch.reset()

        s_w, s_self, s_part, s_max, s_sub, s_e = (sem("am_" + x) for x in ("w", "self", "part", "max", "sub", "exp"))
        FULL, REM = EDGES // P, EDGES % P
        with nc.sbuf_tensor("am_b", [P, PH], F32) as B, nc.sbuf_tensor("am_m", [P, PH], F32) as MX, \
                nc.sbuf_tensor("am_a", [P, PH], F32) as MA, nc.sbuf_tensor("am_t", [P, CHUNKS, PH], F32) as TM, nc.Block() as block:
            @block.sync
            def _(sp):
                sp.dma_start(B[:, :], row_bc(A["L3_gnn_ab2"].rearrange("h a -> (h a)"))).then_inc(s_w, 16)

            @block.vector
            def _(dve):
                ch = Chain(dve, s_self)
                dve.wait_ge(s_w, 16)
                ch(dve.tensor_tensor(TM[:, :, :], WA[:, :, :], B[:, :].unsqueeze(1).broadcast_to([P, CHUNKS, PH]), ALU.add))
                ch(dve.scalar_tensor_tensor(out=WA[:, :, :], in0=TM[:, :, :], scalar=0.2, in1=TM[:, :, :], op0=ALU.mult, op1=ALU.max))
                ch(dve.tensor_reduce(MX[:, :], WA[:, 0:FULL, :].rearrange("p c h -> p h c"), AX.X, ALU.max))
                ch(dve.tensor_tensor(MX[0:REM, :], MX[0:REM, :], WA[0:REM, FULL, :], ALU.max))
                dve.sem_inc(s_part, 1)
                dve.wait_ge(s_max, 1)
                top = MA[:, :].unsqueeze(1).broadcast_to([P, CHUNKS, PH])
                ch(dve.tensor_tensor(WA[:, :, :], WA[:, :, :], top, ALU.min))
                ch(dve.tensor_tensor(TM[:, :, :], WA[:, :, :], top, ALU.subtract))
                dve.sem_inc(s_sub, 1)

            @block.gpsimd
            def _(pool):
                pool.wait_ge(s_part, 1)
                pool.partition_all_reduce(MA[:, :], MX[:, :], P, MAX_OF_ALL).then_inc(s_max, 1)

            @block.scalar
            def _(act):
                act.wait_ge(s_sub, 1)
                act.activation(WA[:, :, :], TM[:, :, :], ACT.Exp).then_inc(s_e, 1)

        n_ = lambda x: [sem(f"aw_{x}{k}") for k in ks]
        s_f, s_m, s_pe, s_o, s_rin, s_rf = (n_(x) for x in ("feats_in", "msg", "merged", "row", "rows_in", "free"))
        s_sc = T["scat3"]
        s_self, s_taken, s_taken2 = (sem("aw_" + x) for x in ("self", "taken", "taken2"))
        srow = A["src_row"].rearrange("(c n) -> c n", n=P)
        with nc.sbuf_tensor("aw_f", [P, RING, PF], F32) as F, nc.sbuf_tensor("aw_m", [P, RING, PW], F32) as M, \
                nc.sbuf_tensor("aw_o", [P, RING, PW], F32) as O, nc.sbuf_tensor("aw_s", [P, RING, P], F32) as S, \
                nc.sbuf_tensor("aw_j", [P, RING, P], F32) as J, nc.sbuf_tensor("aw_r", [P, RING, P], I32) as R, \
                nc.sbuf_tensor("aw_c", [P, RING, 4], F32) as CN, nc.sbuf_tensor("aw_ix", [P, RING], I32) as IX, \
                nc.Block() as block:
            @block.sync
            def _(sp):
                with sp.Fori(0, ROUNDS) as it:
                    for k in ks:
                        c = bass.ds(it * RING + k, 1)
                        sp.wait_ge(s_rf[k], it + 1)
                        sp.dma_start(R[:, k, :], row_bc(srow[c, :].rearrange("a n -> (a n)"))).then_inc(s_rin[k], 16)
                        sp.dma_start(F[:, k, :], spill[c, :, :].rearrange("a p n -> (a p) n")).then_inc(s_f[k], 16)

            @block.gpsimd
            def _(pool):
                with pool.Fori(0, ROUNDS) as it:
                    for k in ks:
                        pool.wait_ge(s_o[k], it + 1)
                        pool.sem_inc(s_taken, 1)
                        pool.indirect_dma_start(out=T["acc3"][k], out_offset=bass.IndirectOffsetOnAxis(ap=IX[:, k:k + 1], axis=0),
                                                in_=O[:, k, :], in_offset=None, compute_op=ALU.add).then_inc(s_sc[k], 16)
                for k in ks:
                    pool.wait_ge(s_sc[k], 16 * (ROUNDS + 1))

            @block.vector
            def _(dve):
                ch = Chain(dve, s_self)
                for k in ks:
                    dve.sem_inc(s_rf[k], 1)
                with dve.Fori(0, ROUNDS) as it:
                    for k in ks:
                        c = it * RING + k
                        ch(dve.tensor_copy(CN[:, k, 0:1], K["srcf"][:, bass.ds(c, 1)]))
                        same_target(dve, ch, K, R[:, k, :], S[:, k, :], J[:, k, :], CN[:, k, :], s_rin[k], it, s_sc[k], IX[:, k:k + 1])
                        ch(dve.tensor_copy(M[:, k, PF:].unsqueeze(1), WA[:, bass.ds(c, 1), :]))
                        dve.wait_ge(s_f[k], 16 * (it + 1))
                        ch(dve.tensor_tensor(M[:, k, 0:PF].rearrange("p (h o) -> p h o", h=PH),
                                             F[:, k, :].rearrange("p (h o) -> p h o", h=PH),
                                             M[:, k, PF:].unsqueeze(2).broadcast_to([P, PH, PO]), ALU.mult))
                        dve.sem_inc(s_m[k], 1)
                        dve.sem_inc(s_rf[k], 1)
                    ch.reset()

            @block.scalar
            def _(act):
                with act.Fori(0, ROUNDS) as it:
                    for k in ks:
                        act.wait_ge(s_pe[k], it + 1)
                        act.activation(O[:, k, :], PS[k][:, 0:PW], ACT.Copy).then_inc(s_o[k], 1)

            @block.tensor
            def _(pe):
                with pe.Fori(0, ROUNDS) as it:
                    for k in ks:
                        pe.wait_ge(s_m[k], it + 1)
                        merge_rows(pe, S[:, k, :], M[:, k, :], PS[k], PW).then_inc(s_pe[k], 1)
    sem.clear()


def att_out(nc, A, T, K, PS):
    sem = Semaphores(nc)
    s_in, s_free, s_self, s_taken = (sem("ao_" + x) for x in ("in", "free", "self", "taken"))
    with nc.sbuf_tensor("ao_acc", [P, RING, ST, PW], F32) as AC, nc.sbuf_tensor("ao_d", [P, ST, PH], F32) as DN, \
            nc.sbuf_tensor("ao_o", [P, ST, D], F32) as O, nc.Block() as block:
        @block.sync
        def _(sp):
            with sp.Fori(0, NST) as j:
                sp.wait_ge(s_free, j + 1)
                for k in range(RING):
                    v = T["acc3"][k][0:NP, :].rearrange("(j t p) w -> j p t w", t=ST, p=P)
                    sp.dma_start(AC[:, k, :, :], v[bass.ds(j, 1), :, :, :].rearrange("a p t w -> (a p) t w")).then_inc(s_in, 16)

        @block.vector
        def _(dve):
            ch = Chain(dve, s_self)
            dve.sem_inc(s_free, 1)
            with dve.Fori(0, NST) as j:
                dve.wait_ge(s_in, 16 * RING * (j + 1))
                for k in range(1, RING):
                    ch(dve.tensor_tensor(AC[:, 0, :, :], AC[:, 0, :, :], AC[:, k, :, :], ALU.add))
                ch(dve.tensor_scalar(DN[:, :, :], AC[:, 0, :, PF:], 1e-10, None, ALU.add))
                ch(dve.reciprocal(DN[:, :, :], DN[:, :, :]))
                for i in range(ST):
                    ch(dve.tensor_tensor(O[:, i, :].rearrange("p (h o) -> p h o", h=PH),
                                         AC[:, 0, i, 0:PF].rearrange("p (h o) -> p h o", h=PH),
                                         DN[:, i, :].unsqueeze(2).broadcast_to([P, PH, PO]), ALU.mult))
                dve.sem_inc(s_free, 1)
                xs = K["X"][:, bass.ds(j * ST, ST), :]
                ch(dve.tensor_tensor(xs, xs, O[:, :, :], ALU.add))
                ch.reset()
    final_norm(nc, K, "att_ln", None)
    sem.clear()


PHASES = 10


def kernel(**inputs):
    import numpy as np
    import concourse.bacc as bacc
    from concourse.bass_utils import run_bass_kernel_spmd

    nc = bacc.Bacc("TRN2", target_bir_lowering=False, num_devices=1)
    arrays = layout(inputs)
    A = {n: nc.dram_tensor(n, a.shape, mybir.dt.from_np(a.dtype), kind="ExternalInput").ap() for n, a in arrays.items()}
    out = nc.dram_tensor("out", (NODES, D), F32, kind="ExternalOutput").ap()
    gnn_kernel(nc, A, out)
    r = run_bass_kernel_spmd(nc, [arrays], core_ids=[0])
    return r.results[0]["out"]


def layout(inputs):
    import numpy as np

    a = {n: np.ascontiguousarray(v) for n, v in inputs.items()}
    pad = NODES + np.arange(EP - EDGES) % (NP - NODES)
    o = {"x": np.concatenate([a["x"], np.zeros((NP - NODES, D), a["x"].dtype)])}
    for n in ("src", "dst"):
        row = np.concatenate([a[n], pad.astype(a[n].dtype)])
        o[n + "_row"] = row
        o[n + "_col"] = np.ascontiguousarray(row.reshape(CHUNKS, P).T)
    ew = np.concatenate([a["edge_weight"], np.zeros(EP - EDGES, a["edge_weight"].dtype)])
    o["ew_col"] = np.ascontiguousarray(ew.reshape(CHUNKS, P).T)
    for n, v in a.items():
        if n[:2] in ("L0", "L1", "L2", "L3"):
            o[n] = v
    def columns(v, n):
        return np.ascontiguousarray(v.reshape(v.shape[:-1] + (n, P)).swapaxes(-1, -2))

    o["L0_gnn_b1"] = columns(a["L0_gnn_b1"], 2)
    o["L2_gnn_conv_b1"] = columns(a["L2_gnn_conv_b1"], 4)
    o["L2_gnn_conv_b2c"] = columns(a["L2_gnn_conv_b2"], 4)
    o["L2_gnn_in_bc"] = columns(a["L2_gnn_in_b"], 4)
    o["L3_gnn_b1"] = columns(a["L3_gnn_b1"], 2)
    o["L3_gnn_b2c"] = columns(a["L3_gnn_b2"].reshape(PF), 2)
    o["L1_gnn_W"] = np.ascontiguousarray(a["L1_gnn_W"].transpose(1, 0, 2).reshape(D, GH))
    o["L2_gnn_in_WT"] = np.ascontiguousarray(a["L2_gnn_in_W"].T)
    o["L2_gnn_conv_W2T"] = np.ascontiguousarray(a["L2_gnn_conv_W2"].transpose(0, 2, 1))
    return o
```

```python
import concourse.bass as bass
from concourse import mybir

F32 = mybir.dt.float32
F16 = mybir.dt.float16
BF16 = mybir.dt.bfloat16
I32 = mybir.dt.int32
ALU = mybir.AluOpType
ACT = mybir.ActivationFunctionType
AX = mybir.AxisListType
MAX_OF_ALL = bass.bass_isa.ReduceOp.max

P = 128
NODES = 3125
TILES = 25
NP = TILES * P
ST = 5
NST = TILES // ST
SW = ST * P
HALF = 3 * P
REST = SW - HALF
D = 256
EDGES = 50000
RING = 4
CHUNKS = 392
GROUPS = CHUNKS // RING
EP = CHUNKS * P
LAYERS = 3
HEADS, HID = 8, 64
GH = HEADS * HID
GW = GH + HEADS
F2 = 512
PH, PO = 4, 64
ATT = 2 * PO + 1
AW = PH * ATT
PF = PH * PO
PW = PF + PH
LN_EPS = 1e-5
ACC_ROWS = NP + P


class Chain:

    def __init__(self, eng, sem):
        self.eng, self.sem, self.n = eng, sem, 0

    def __call__(self, ins):
        self.n += 1
        ins.then_inc(self.sem, 1)
        self.eng.wait_ge(self.sem, self.n)

    def run(self, ins):
        self.n += 1
        ins.then_inc(self.sem, 1)

    def sync(self):
        self.eng.wait_ge(self.sem, self.n)

    def reset(self):
        self.eng.sem_clear(self.sem)
        self.n = 0


class Semaphores:

    def __init__(self, nc):
        self.nc, self.all = nc, []

    def __call__(self, name):
        self.all.append(self.nc.alloc_semaphore(name))
        return self.all[-1]

    def clear(self):
        self.nc.clear_and_free_semaphores(self.all)
        self.nc.all_engine_barrier(sem_only=True)


def row_bc(ap, parts=P):
    return ap.partition_broadcast(parts)


def gnn_kernel(nc, A, out):
    dram = lambda name, shape, dt: nc.dram_tensor(name, shape, dt, kind="Internal").ap()
    T = {
        "counts": dram("counts", [NP * NP + RING * P, 1], F16),
        "tab0": dram("tab0", [NP, 2 * D], F16),
        "tab2": dram("tab2", [NP, 2 * F2], F16),
        "gat_src": dram("gat_src", [NP, GW], F32),
        "gat_dst": dram("gat_dst", [NP, 2 * HEADS], F32),
        "gat_at": dram("gat_at", [HEADS, NP], F32),
        "acc1": [dram(f"acc1_{k}", [ACC_ROWS, GW], F32) for k in range(RING)],
        "att_row": dram("att_row", [NP, AW], F32),
        "att_col": dram("att_col", [NP, AW + PF], F32),
        "spill": dram("spill", [EP, PF], F32),
        "acc3": [dram(f"acc3_{k}", [ACC_ROWS, PW], F32) for k in range(RING)],
    }
    sb = lambda name, shape, dt=F32: nc.alloc_sbuf_tensor(name, shape, dt)
    K = {
        "X": sb("X", [P, TILES, D]),
        "I32": sb("ident", [P, P]), "I16": sb("ident16", [P, P], F16),
        "ones": sb("ones", [P, P]),
        "early": sb("early", [P, P]), "late": sb("late", [P, P], BF16),
        "trash": sb("trash", [P, RING]),
        "trash_row": sb("trash_row", [P, 1]),
        "eps": sb("eps", [P, 1]),
        "srci": sb("srci", [P, CHUNKS + 2 * RING], I32), "dsti": sb("dsti", [P, CHUNKS + 2 * RING], I32),
        "srcf": sb("srcf", [P, CHUNKS]), "dstf": sb("dstf", [P, CHUNKS]),
        "keyf": sb("keyf", [P, CHUNKS]),
    }
    PS = [nc.alloc_psum_tensor(f"ps{k}", [P, 1024], F32) for k in range(4)]
    setup(nc, A, T, K)
    if PHASES > 1:
        build_counts(nc, A, T, K, PS)
    if PHASES > 2:
        gin(nc, A, T, K, PS)
    if PHASES > 3:
        gat_nodes(nc, A, T, K, PS)
    if PHASES > 4:
        gat_edges(nc, A, T, K, PS)
    if PHASES > 5:
        gat_out(nc, A, T, K, PS)
    if PHASES > 6:
        deep_gin(nc, A, T, K, PS)
    if PHASES > 7:
        att_nodes(nc, A, T, K, PS)
    if PHASES > 8:
        att_edges(nc, A, T, K, PS)
    if PHASES > 9:
        att_out(nc, A, T, K, PS)
    s = nc.alloc_semaphore("out_done")
    with nc.Block() as block:
        @block.sync
        def _(sp):
            sp.dma_start(out[0:P * (TILES - 1), :].rearrange("(t p) d -> p t d", p=P),
                         K["X"][:, 0:TILES - 1, :]).then_inc(s, 16)
            sp.dma_start(out[P * (TILES - 1):NODES, :], K["X"][0:NODES - P * (TILES - 1), TILES - 1, :]).then_inc(s, 16)
            sp.wait_ge(s, 32)


def setup(nc, A, T, K):
    sem = Semaphores(nc)
    s_in, s_pad, s_zero, s_io = sem("su_in"), sem("su_pad"), sem("su_zero"), sem("su_iota")
    s_z, s_self = sem("su_zeroed"), sem("su_self")
    s_scat = [nc.alloc_semaphore(f"gat_scattered{k}") for k in range(RING)]
    s_scat3 = [nc.alloc_semaphore(f"att_scattered{k}") for k in range(RING)]
    T["scat"], T["scat3"] = s_scat, s_scat3
    with nc.sbuf_tensor("zeros", [P, 26 * 128], F32) as Z, nc.Block() as block:
        @block.vector
        def _(dve):
            ch = Chain(dve, s_self)
            dve.memset(Z[:, :], 0.0).then_inc(s_zero, 1)
            dve.memset(K["ones"][:, :], 1.0)
            dve.memset(K["eps"][:, :], LN_EPS)
            dve.memset(K["srci"][:, CHUNKS:], 0)
            dve.memset(K["dsti"][:, CHUNKS:], 0)
            dve.wait_ge(s_in, 16 * 3)
            ch(dve.tensor_copy(K["srcf"][:, :], K["srci"][:, 0:CHUNKS]))
            ch(dve.tensor_copy(K["dstf"][:, :], K["dsti"][:, 0:CHUNKS]))
            dve.scalar_tensor_tensor(out=K["keyf"][:, :], in0=K["srcf"][:, :], scalar=float(NP), in1=K["dstf"][:, :],
                                     op0=ALU.mult, op1=ALU.add)
            dve.wait_ge(s_io, 8)
            dve.tensor_copy(K["I16"][:, :], K["I32"][:, :])

        @block.gpsimd
        def _(pool):
            pool.memset(K["I32"][:, :], 0.0).then_inc(s_io, 1)
            pool.memset(K["early"][:, :], 1.0).then_inc(s_io, 1)
            pool.memset(K["late"][:, :], 1.0).then_inc(s_io, 1)
            pool.iota(K["trash"][:, :], [[P, RING]], base=NP * NP, channel_multiplier=1,
                      allow_small_or_imprecise_dtypes=True).then_inc(s_io, 1)
            pool.iota(K["trash_row"][:, :], [[0, 1]], base=NP, channel_multiplier=1,
                      allow_small_or_imprecise_dtypes=True).then_inc(s_io, 1)
            pool.wait_ge(s_io, 5)
            pool.affine_select(out=K["I32"][:, :], in_=K["I32"][:, :], compare_op=ALU.not_equal, fill=1.0,
                               base=0, pattern=[[-1, P]], channel_multiplier=1).then_inc(s_io, 1)
            pool.affine_select(out=K["early"][:, :], in_=K["early"][:, :], compare_op=ALU.is_gt, fill=0.0,
                               base=0, pattern=[[-1, P]], channel_multiplier=1).then_inc(s_io, 1)
            pool.affine_select(out=K["late"][:, :], in_=K["late"][:, :], compare_op=ALU.is_gt, fill=0.0,
                               base=0, pattern=[[1, P]], channel_multiplier=-1).then_inc(s_io, 1)
            pool.wait_ge(s_zero, 1)
            for k in range(RING):
                for a in range(2):
                    r = slice(NP + a * P // 2, NP + (a + 1) * P // 2)
                    pool.dma_start(T["acc1"][k][r, :], Z[0:P // 2, 0:GW]).then_inc(s_scat[k], 16)
                    pool.dma_start(T["acc3"][k][r, :], Z[0:P // 2, 0:PW]).then_inc(s_scat3[k], 16)
            for k in range(RING):
                pool.wait_ge(s_scat[k], 32)
                pool.wait_ge(s_scat3[k], 32)

        @block.sync
        def _(sp):
            sp.dma_start(K["srci"][:, 0:CHUNKS], A["src_col"]).then_inc(s_in, 16)
            sp.dma_start(K["dsti"][:, 0:CHUNKS], A["dst_col"]).then_inc(s_in, 16)
            sp.dma_start(K["X"][:, :, :], A["x"].rearrange("(t p) d -> p t d", p=P)).then_inc(s_in, 16)
            sp.wait_ge(s_in, 48)
            sp.wait_ge(s_zero, 1)
            n = 0
            cz = T["counts"][0:NP * NP, :].rearrange("(t p n) a -> t p (n a)", p=P, n=NP)
            zh = Z[:, :].bitcast(F16)
            with sp.Fori(0, TILES) as t:
                sp.dma_start(cz[bass.ds(t, 1), :, :].rearrange("a p n -> (a p) n"), zh[:, 0:NP]).then_inc(s_z, 16)
            n += TILES
            sp.dma_start(T["counts"][NP * NP:, :].rearrange("(p n) a -> p (n a)", p=P), zh[:, 0:RING]).then_inc(s_z, 16)
            n += 1
            sp.wait_ge(s_z, 16 * n)
    sem.clear()


def build_counts(nc, A, T, K, PS):
    sem = Semaphores(nc)
    s_row, s_idx, s_self = [sem("bc_row0"), sem("bc_row1")], [sem("bc_idx0"), sem("bc_idx1")], sem("bc_self")
    s_rfree, s_sc = [sem("bc_rfree0"), sem("bc_rfree1")], [sem("bc_scat0"), sem("bc_scat1")]
    s_one, s_same, s_sum, s_z = sem("bc_one"), sem("bc_same"), sem("bc_sums"), sem("bc_zeroed")
    GC = RING * P
    srow = A["src_row"].rearrange("(g n) -> g n", n=GC)
    drow = A["dst_row"].rearrange("(g n) -> g n", n=GC)
    with nc.sbuf_tensor("rows", [P, 2, 2, GC], I32) as R, nc.sbuf_tensor("keyrow", [P, 2, GC], F32) as KR, \
            nc.sbuf_tensor("same", [P, 2, RING, GC], BF16) as S, nc.sbuf_tensor("own", [P, 2, RING, P], BF16) as OW, \
            nc.sbuf_tensor("kcol", [P, 2, RING], F32) as KC, nc.sbuf_tensor("ones16", [P, 1], BF16) as ONE, \
            nc.sbuf_tensor("tmp", [P, 2, RING], F32) as TM, nc.sbuf_tensor("bc_zeros", [P, ST * GW], F32) as Z, \
            nc.sbuf_tensor("idx", [P, 2, RING], I32) as IX, nc.sbuf_tensor("val", [P, 2, RING], F16) as VA, \
            nc.Block() as block:
        @block.sync
        def _(sp):
            with sp.Fori(0, GROUPS // 2) as it:
                for h in range(2):
                    sp.wait_ge(s_rfree[h], it + 1)
                    sp.dma_start(R[:, h, 0, :], row_bc(srow[bass.ds(2 * it + h, 1), :].rearrange("a n -> (a n)"))).then_inc(s_row[h], 16)
                    sp.dma_start(R[:, h, 1, :], row_bc(drow[bass.ds(2 * it + h, 1), :].rearrange("a n -> (a n)"))).then_inc(s_row[h], 16)

        @block.scalar
        def _(act):
            act.wait_ge(s_one, 1)
            n = 0
            for k in range(RING):
                for acc, w in ((T["acc1"][k], GW), (T["acc3"][k], PW)):
                    for t in range(0, TILES, ST):
                        act.dma_start(acc[t * P:(t + ST) * P, :].rearrange("(t p) w -> p t w", p=P),
                                      Z[:, 0:ST * w].rearrange("p (t w) -> p t w", t=ST)).then_inc(s_z, 16)
                        n += 1
            act.wait_ge(s_z, 16 * n)

        @block.vector
        def _(dve):
            ch = Chain(dve, s_self)
            for h in range(2):
                dve.sem_inc(s_rfree[h], 1)
            ch(dve.memset(ONE[:, :], 1.0))
            dve.memset(Z[:, :], 0.0).then_inc(s_one, 1)
            ch.reset()
            with dve.Fori(0, GROUPS // 2) as it:
                for h in range(2):
                    dve.wait_ge(s_row[h], 32 * (it + 1))
                    ch.run(dve.scalar_tensor_tensor(out=KR[:, h, :], in0=R[:, h, 0, :], scalar=float(NP), in1=R[:, h, 1, :],
                                                    op0=ALU.mult, op1=ALU.add))
                    ch.run(dve.tensor_copy(KC[:, h, :], K["keyf"][:, bass.ds((2 * it + h) * RING, RING)]))
                    ch.sync()
                    dve.sem_inc(s_rfree[h], 1)
                    for k in range(RING):
                        ch.run(dve.tensor_scalar(S[:, h, k, :], KR[:, h, :], KC[:, h, k:k + 1], None, ALU.is_equal))
                    ch.sync()
                    own = S[:, h, :, :].rearrange("p k (c x) -> p (k c) x", x=P)[:, 0:RING * RING:RING + 1, :]
                    ch(dve.tensor_tensor(OW[:, h, :, :], own, K["late"][:, :].unsqueeze(1).broadcast_to([P, RING, P]), ALU.mult))
                    dve.sem_inc(s_same, 1)
                    ch(dve.tensor_tensor(TM[:, h, :], K["trash"][:, :], KC[:, h, :], ALU.subtract))
                    dve.wait_ge(s_sc[h], 16 * (RING * it + 1))
                    dve.wait_ge(s_sum, 2 * it + h + 1)
                    ch.run(dve.tensor_copy(VA[:, h, :], PS[h][:, 0:RING]))
                    ch(dve.scalar_tensor_tensor(out=TM[:, h, :], in0=PS[h][:, RING:2 * RING], scalar=1.0, in1=TM[:, h, :],
                                                op0=ALU.min, op1=ALU.mult))
                    ch(dve.tensor_tensor(IX[:, h, :], TM[:, h, :], KC[:, h, :], ALU.add))
                    dve.sem_inc(s_idx[h], 1)
                ch.reset()

        @block.tensor
        def _(pe):
            with pe.Fori(0, GROUPS // 2) as it:
                for h in range(2):
                    pe.wait_ge(s_same, 2 * it + h + 1)
                    for k in range(RING):
                        for c in range(RING):
                            pe.matmul(PS[h][:, k:k + 1], S[:, h, c, k * P:(k + 1) * P], ONE[:, :], start=c == 0, stop=c == RING - 1)
                        for c in range(k):
                            pe.matmul(PS[h][:, RING + k:RING + k + 1], S[:, h, c, k * P:(k + 1) * P], ONE[:, :], start=c == 0, stop=False)
                        m = pe.matmul(PS[h][:, RING + k:RING + k + 1], OW[:, h, k, :], ONE[:, :], start=k == 0, stop=True)
                    m.then_inc(s_sum, 1)

        @block.gpsimd
        def _(pool):
            for h in range(2):
                pool.dma_start(IX[:, h, :], A["src_col"][:, 0:RING]).then_inc(s_sc[h], 16)
            for h in range(2):
                pool.wait_ge(s_sc[h], 16)
            with pool.Fori(0, GROUPS // 2) as it:
                for h in range(2):
                    pool.wait_ge(s_idx[h], it + 1)
                    pool.wait_ge(s_sc[1 - h], 16 * (RING * (it + h) + 1))
                    pool.sem_inc(s_one, 1)
                    for k in range(RING):
                        pool.indirect_dma_start(
                            out=T["counts"], out_offset=bass.IndirectOffsetOnAxis(ap=IX[:, h, k:k + 1], axis=0),
                            in_=VA[:, h, k:k + 1], in_offset=None, compute_op=ALU.add).then_inc(s_sc[h], 16)
            for h in range(2):
                pool.wait_ge(s_sc[h], 16 * (RING * (GROUPS // 2) + 1))
    sem.clear()


def split16(ch, dve, x, hi, lo):
    ch(dve.tensor_copy(hi, x))
    ch(dve.tensor_tensor(lo, x, hi, ALU.subtract))


def norm_stats(ch, dve, x, stats, mv, n):
    for i in range(n):
        dve_i = dve.bn_stats(stats[:, i, :], x[:, i, :])
        ch(dve_i)
        ch(dve.bn_aggr(mv[:, i, :], stats[:, i, :]))


def final_norm(nc, K, name, add, width=ST):
    sem = Semaphores(nc)
    s_self, s_mv, s_sd = (sem(f"{name}_{x}") for x in ("self", "var", "sd"))
    X = K["X"]
    with nc.sbuf_tensor(name + "_st", [P, TILES, 6], F32) as S, nc.sbuf_tensor(name + "_mv", [P, TILES, 2], F32) as MV, \
            nc.sbuf_tensor(name + "_sd", [P, TILES], F32) as SD, nc.sbuf_tensor(name + "_rs", [P, TILES], F32) as RS, \
            nc.Block() as block:
        @block.vector
        def _(dve):
            ch = Chain(dve, s_self)
            if add is not None:
                ch(dve.tensor_tensor(X[:, :, :], X[:, :, :], add[:, :, :], ALU.add))
            for i in range(TILES):
                dve.bn_stats(S[:, i, :], X[:, i, :]).then_inc(s_self, 1)
            ch.n += TILES
            dve.wait_ge(s_self, ch.n)
            for i in range(TILES):
                dve.bn_aggr(MV[:, i, :], S[:, i, :]).then_inc(s_mv, 1)
            dve.wait_ge(s_sd, 1)
            ch(dve.reciprocal(RS[:, :], SD[:, :]))
            for i in range(TILES):
                dve.tensor_scalar(X[:, i, :], X[:, i, :], MV[:, i, 0:1], RS[:, i:i + 1], ALU.subtract, ALU.mult)

        @block.scalar
        def _(act):
            act.wait_ge(s_mv, TILES)
            act.activation(SD[:, :], MV[:, :, 1], ACT.Sqrt, bias=K["eps"][:, 0:1]).then_inc(s_sd, 1)
    sem.clear()


def load_counts(sp, T, C, s_in, s_out, j, round_):
    view = T["counts"][0:NP * NP, :].rearrange("(k s p t c) a -> k t p s (c a)", k=ST, s=ST, p=P, c=SW)
    for q in range(ST):
        sp.wait_ge(s_out[q], round_ + 1)
        sp.dma_start(C[:, q, :, :], view[q, bass.ds(j, 1), :, :, :].rearrange("a p s c -> (a p) s c")).then_inc(s_in[q], 16)


def neighbour_sum(pe, TAB, C, ps, fb, width, s_in, s_out, round_, last, own):
    for s in range(TILES):
        q = s // ST
        if fb == 0 and s % ST == 0:
            pe.wait_ge(s_in[q], 16 * (round_ + 1))
        for part in range(2):
            w = TAB[:, s, part * width + fb * P:part * width + (fb + 1) * P]
            first, end = s == 0 and part == 0, s == TILES - 1 and part == 1
            pe.matmul(ps[:, 0:HALF], w, C[:, q, s % ST, 0:HALF], start=first, stop=end, skip_group_check=True)
            m = pe.matmul(ps[:, 512:512 + REST], w, C[:, q, s % ST, HALF:SW], start=first, stop=end, skip_group_check=True)
        if last and s % ST == ST - 1 and q < ST - 1:
            m.then_inc(s_out[q], 1)
        if s == ST:
            own()
    return m


def cols(i):
    return slice(i * P, (i + 1) * P) if i < 3 else slice(512 + (i - 3) * P, 512 + (i - 2) * P)


HALVES = ((slice(0, HALF), slice(0, HALF)), (slice(512, 512 + REST), slice(HALF, SW)))


def gin(nc, A, T, K, PS):
    sem = Semaphores(nc)
    n_ = lambda x: sem("gin_" + x)
    s_tab, s_w, s_self, s_hl, s_taken = n_("tab_in"), n_("weights_in"), n_("self"), n_("split"), n_("taken")
    s_tabout, s_own, s_zt, s_ut = n_("tab_out"), n_("own"), n_("zt"), n_("ut")
    s_mv, s_sd = n_("var"), n_("sd")
    s_cin, s_cout = [n_(f"c_in{q}") for q in range(ST)], [n_(f"c_out{q}") for q in range(ST)]
    s_full, s_free = [n_(f"full{k}") for k in range(4)], [n_(f"free{k}") for k in range(4)]
    X = K["X"]
    NW = 7
    with nc.sbuf_tensor("gin_h", [P, TILES, D], F32) as H:
        with nc.sbuf_tensor("gin_tab", [P, TILES, 2 * D], F16) as TAB, \
                nc.sbuf_tensor("gin_c", [P, ST, ST, SW], F16) as C, \
                nc.sbuf_tensor("gin_w1", [P, 2, D], F32) as W1, nc.sbuf_tensor("gin_w2", [P, 2, D], F32) as W2, \
                nc.sbuf_tensor("gin_b1", [P, 2], F32) as B1, nc.sbuf_tensor("gin_rows", [P, 3, D], F32) as RW, \
                nc.sbuf_tensor("gin_eps", [P, 1], F32) as EPS, nc.sbuf_tensor("gin_eps1", [P, 1], F32) as EPS1, \
                nc.sbuf_tensor("gin_own", [P, ST, D], F32) as OWN, nc.sbuf_tensor("gin_hb", [P, ST, D], F32) as HB, \
                nc.sbuf_tensor("gin_r", [P, ST, D], F32) as R, nc.sbuf_tensor("gin_hl", [P, ST, 2 * D], F16) as HL, \
                nc.sbuf_tensor("gin_zt", [P, 2, SW], F32) as ZT, nc.sbuf_tensor("gin_ut", [P, 2, SW], F32) as UT, \
                nc.sbuf_tensor("gin_st", [P, ST, 6], F32) as S, nc.sbuf_tensor("gin_mv", [P, ST, 2], F32) as MV, \
                nc.sbuf_tensor("gin_sd", [P, ST], F32) as SD, nc.sbuf_tensor("gin_rs", [P, ST], F32) as RS, \
                nc.Block() as block:
            tab_d = T["tab0"].rearrange("(j t p) w -> j p t w", t=ST, p=P)

            @block.sync
            def _(sp):
                with sp.Fori(0, LAYERS) as l:
                    sp.wait_ge(s_tabout, 16 * NST * (l + 1))
                    one = bass.ds(l, 1)
                    sp.dma_start(TAB[:, :, :], T["tab0"].rearrange("(t p) w -> p t w", p=P)).then_inc(s_tab, 16)
                    for dst, name in ((W1, "L0_gnn_W1"), (W2, "L0_gnn_W2")):
                        sp.dma_start(dst[:, :, :], A[name][one, :, :].rearrange("a (k p) n -> p (a k) n", p=P)).then_inc(s_w, 16)
                    sp.dma_start(B1[:, :], A["L0_gnn_b1"][one, :, :].rearrange("a p k -> (a p) k")).then_inc(s_w, 16)
                    for n, name in enumerate(("L0_gnn_b2", "L0_gnn_gamma", "L0_gnn_beta")):
                        sp.dma_start(RW[:, n, :], row_bc(A[name][one, :].rearrange("a n -> (a n)"))).then_inc(s_w, 16)
                    sp.dma_start(EPS[:, :], row_bc(A["L0_gnn_eps"][one])).then_inc(s_w, 16)
                    with sp.Fori(0, NST) as j:
                        load_counts(sp, T, C, s_cin, s_cout, j, l * NST + j)

            @block.gpsimd
            def _(pool):
                def store(j, n):
                    pool.wait_ge(s_hl, n)
                    pool.sem_inc(s_taken, 1)
                    pool.dma_start(tab_d[bass.ds(j, 1), :, :, :].rearrange("a p t w -> (a p) t w"), HL[:, :, :]).then_inc(s_tabout, 16)
                with pool.Fori(0, NST) as j:
                    store(j, j + 1)
                with pool.Fori(0, LAYERS) as l:
                    with pool.Fori(0, NST) as j:
                        store(j, l * NST + j + NST + 1)
                pool.wait_ge(s_tabout, 16 * NST * (LAYERS + 1))

            @block.vector
            def _(dve):
                ch = Chain(dve, s_self)
                ch(dve.tensor_copy(H[:, :, :], X[:, :, :]))
                for j in range(NST):
                    if j:
                        dve.wait_ge(s_tabout, 16 * j)
                    split16(ch, dve, H[:, j * ST:(j + 1) * ST, :], HL[:, :, 0:D], HL[:, :, D:])
                    dve.sem_inc(s_hl, 1)
                ch.reset()
                with dve.Fori(0, LAYERS) as l:
                    dve.wait_ge(s_w, 16 * NW * (l + 1))
                    ch(dve.tensor_scalar(EPS1[:, :], EPS[:, :], 1.0, None, ALU.add))
                    ch.reset()
                    with dve.Fori(0, NST) as j:
                        g = l * NST + j
                        mine = H[:, bass.ds(j * ST, ST), :]
                        ch(dve.tensor_scalar(OWN[:, :, :], mine, EPS1[:, 0:1], None, ALU.mult))
                        dve.sem_inc(s_own, 1)
                        ch(dve.tensor_tensor(HB[:, :, :], mine, RW[:, 0:1, :].broadcast_to([P, ST, D]), ALU.add))
                        for i in range(ST):
                            k = 2 + i % 2
                            per, nth = (4, 1 + i // 2) if k == 2 else (3, 1 + i // 2)
                            dve.wait_ge(s_full[k], per * g + nth + 1)
                            ch(dve.tensor_tensor(R[:, i, :], HB[:, i, :], PS[k][:, 0:D], ALU.add))
                            dve.sem_inc(s_free[k], 1)
                        norm_stats(ch, dve, R, S, MV, ST)
                        dve.sem_inc(s_mv, 1)
                        dve.wait_ge(s_sd, g + 1)
                        ch(dve.reciprocal(RS[:, :], SD[:, :]))
                        for i in range(ST):
                            ch(dve.tensor_scalar(R[:, i, :], R[:, i, :], MV[:, i, 0:1], RS[:, i:i + 1], ALU.subtract, ALU.mult))
                        ch(dve.tensor_tensor(R[:, :, :], R[:, :, :], RW[:, 1:2, :].broadcast_to([P, ST, D]), ALU.mult))
                        ch(dve.tensor_tensor(R[:, :, :], R[:, :, :], RW[:, 2:3, :].broadcast_to([P, ST, D]), ALU.add))
                        ch(dve.tensor_scalar(R[:, :, :], R[:, :, :], 0.0, None, ALU.max))
                        ch(dve.tensor_copy(mine, R[:, :, :]))
                        dve.wait_ge(s_tabout, 16 * (g + NST))
                        split16(ch, dve, R[:, :, :], HL[:, :, 0:D], HL[:, :, D:])
                        dve.sem_inc(s_hl, 1)
                        ch.reset()

            @block.scalar
            def _(act):
                for q in range(ST):
                    act.sem_inc(s_cout[q], 1)
                for k in range(4):
                    act.sem_inc(s_free[k], 1)
                with act.Fori(0, LAYERS) as l:
                    act.wait_ge(s_w, 16 * NW * (l + 1))
                    act.sem_inc(s_taken, 1)
                    with act.Fori(0, NST) as j:
                        g = l * NST + j
                        for fb in range(2):
                            act.wait_ge(s_full[fb], g + 1)
                            for a, b in HALVES:
                                act.activation(ZT[:, fb, b], PS[fb][:, a], ACT.Copy).then_inc(s_zt, 1)
                            act.wait_ge(s_zt, 4 * g + 2 * fb + 2)
                            act.sem_inc(s_free[fb], 1)
                        for hb in range(2):
                            k = 2 + hb
                            act.wait_ge(s_full[k], (4 - hb) * g + 1)
                            for a, b in HALVES:
                                act.activation(UT[:, hb, b], PS[k][:, a], ACT.Relu, bias=B1[:, hb:hb + 1]).then_inc(s_ut, 1)
                            act.wait_ge(s_ut, 4 * g + 2 * hb + 2)
                            act.sem_inc(s_free[k], 1)
                        act.wait_ge(s_mv, g + 1)
                        act.activation(SD[:, :], MV[:, :, 1], ACT.Sqrt, bias=K["eps"][:, 0:1]).then_inc(s_sd, 1)

            @block.tensor
            def _(pe):
                with pe.Fori(0, LAYERS) as l:
                    pe.wait_ge(s_w, 16 * NW * (l + 1))
                    pe.wait_ge(s_tab, 16 * (l + 1))
                    pe.sem_inc(s_taken, 1)
                    with pe.Fori(0, NST) as j:
                        g = l * NST + j
                        for fb in range(2):
                            def own():
                                if fb == 0:
                                    pe.wait_ge(s_own, g + 1)
                                for i in range(ST):
                                    pe.matmul(PS[fb][:, cols(i)], OWN[:, i, fb * P:(fb + 1) * P], K["I32"][:, :],
                                              start=False, stop=False, skip_group_check=True)
                            pe.wait_ge(s_free[fb], g + 1)
                            neighbour_sum(pe, TAB, C, PS[fb], fb, D, s_cin, s_cout, g, fb == 1, own).then_inc(s_full[fb], 1)
                        pe.wait_ge(s_zt, 4 * g + 4)
                        pe.sem_inc(s_cout[ST - 1], 1)
                        for hb in range(2):
                            pe.wait_ge(s_free[2 + hb], (4 - hb) * g + 1)
                            for a, b in HALVES:
                                for kb in range(2):
                                    m = pe.matmul(PS[2 + hb][:, a], W1[:, kb, hb * P:(hb + 1) * P], ZT[:, kb, b],
                                                  start=kb == 0, stop=kb == 1)
                            m.then_inc(s_full[2 + hb], 1)
                        pe.wait_ge(s_ut, 4 * g + 4)
                        for i in range(ST):
                            k = 2 + i % 2
                            per, nth = (4, 1 + i // 2) if k == 2 else (3, 1 + i // 2)
                            pe.wait_ge(s_free[k], per * g + nth + 1)
                            for kb in range(2):
                                m = pe.matmul(PS[k][:, 0:D], UT[:, kb, i * P:(i + 1) * P], W2[:, kb, :], start=kb == 0, stop=kb == 1)
                            m.then_inc(s_full[k], 1)
        final_norm(nc, K, "gin_ln", H)
    sem.clear()


def transposed(pe, ident, ps, src, n, col):
    for i in range(n):
        m = pe.transpose(ps[:, cols(i)], src[:, i, col:col + P], ident)
    return m


def gat_nodes(nc, A, T, K, PS):
    sem = Semaphores(nc)
    n_ = lambda x: sem("gn_" + x)
    s_w, s_self, s_taken, s_xs, s_xt, s_row, s_sc = (n_(x) for x in ("w", "self", "taken", "xs", "xt", "row", "score"))
    s_as, s_as2, s_out, s_aout = n_("as"), n_("as_half"), n_("row_out"), n_("at_out")
    s_full, s_free = [n_(f"full{k}") for k in range(4)], [n_(f"free{k}") for k in range(4)]
    with nc.sbuf_tensor("gn_bm", [P, TILES, 2 * HEADS], F32) as BM:
        with nc.sbuf_tensor("gn_w", [P, 2, GH], F32) as W, nc.sbuf_tensor("gn_a", [P, HEADS, 2, HID], F32) as AV, \
                nc.sbuf_tensor("gn_xs", [P, ST, D], F32) as XS, nc.sbuf_tensor("gn_xt", [P, 2, SW], F32) as XT, \
                nc.sbuf_tensor("gn_row", [P, ST, GW], F32) as ROW, nc.sbuf_tensor("gn_p", [P, HEADS, HID], F32) as PR, \
                nc.sbuf_tensor("gn_as", [HEADS, SW], F32) as AS, nc.Block() as block:
            @block.sync
            def _(sp):
                sp.dma_start(W[:, :, :], A["L1_gnn_W"].rearrange("(k p) n -> p k n", p=P)).then_inc(s_w, 16)
                sp.dma_start(AV[:, :, :, :].rearrange("p h s o -> p (h s o)"),
                             row_bc(A["L1_gnn_a"].rearrange("h o -> (h o)"))).then_inc(s_w, 16)
                rows = T["gat_src"].rearrange("(j t p) w -> j p t w", t=ST, p=P)
                with sp.Fori(0, NST) as j:
                    sp.wait_ge(s_as, j + 1)
                    sp.dma_start(rows[bass.ds(j, 1), :, :, :].rearrange("a p t w -> (a p) t w"), ROW[:, :, :]).then_inc(s_out, 16)
                    sp.dma_start(T["gat_at"][:, bass.ds(j * SW, SW)], AS[:, :]).then_inc(s_out, 16)
                    sp.wait_ge(s_out, 32 * (j + 1))
                    sp.sem_inc(s_aout, 1)

            @block.vector
            def _(dve):
                ch = Chain(dve, s_self)
                dve.sem_inc(s_aout, 1)
                dve.wait_ge(s_w, 32)
                dve.sem_inc(s_taken, 1)
                with dve.Fori(0, NST) as j:
                    ch(dve.tensor_copy(XS[:, :, :], K["X"][:, bass.ds(j * ST, ST), :]))
                    dve.sem_inc(s_xs, 1)
                    for i in range(ST):
                        dve.wait_ge(s_row, ST * j + i + 1)
                        f = ROW[:, i, 0:GH].rearrange("p (h o) -> p h o", h=HEADS)
                        ch(dve.tensor_tensor(PR[:, :, :], f, AV[:, :, 0, :], ALU.mult))
                        ch(dve.tensor_reduce(ROW[:, i, GH:], PR[:, :, :], AX.X, ALU.add))
                        ch(dve.tensor_tensor(PR[:, :, :], f, AV[:, :, 1, :], ALU.mult))
                        ch(dve.tensor_reduce(BM[:, bass.ds(j * ST + i, 1), 0:HEADS], PR[:, :, :].unsqueeze(1), AX.X, ALU.add))
                    dve.sem_inc(s_sc, 1)
                    ch.reset()

            @block.scalar
            def _(act):
                for k in range(4):
                    act.sem_inc(s_free[k], 1)
                with act.Fori(0, NST) as j:
                    for kb in range(2):
                        act.wait_ge(s_full[kb], (2 - kb) * j + 1)
                        for a, b in HALVES:
                            act.activation(XT[:, kb, b], PS[kb][:, a], ACT.Copy).then_inc(s_xt, 1)
                        act.wait_ge(s_xt, 4 * j + 2 * kb + 2)
                        act.sem_inc(s_free[kb], 1)
                    act.wait_ge(s_aout, j + 1)
                    act.sem_inc(s_taken, 1)
                    for i in range(ST):
                        k, per, nth = 2 + i % 2, 3 - i % 2, i // 2
                        act.wait_ge(s_full[k], per * j + nth + 1)
                        act.activation(ROW[:, i, 0:GH], PS[k][:, 0:GH], ACT.Copy).then_inc(s_row, 1)
                        act.wait_ge(s_row, ST * j + i + 1)
                        act.sem_inc(s_free[k], 1)
                    act.wait_ge(s_full[0], 2 * j + 2)
                    for a, b in HALVES:
                        act.activation(AS[:, b], PS[0][0:HEADS, a], ACT.Copy).then_inc(s_as2, 1)
                    act.wait_ge(s_as2, 2 * j + 2)
                    act.sem_inc(s_free[0], 1)
                    act.sem_inc(s_as, 1)

            @block.tensor
            def _(pe):
                pe.wait_ge(s_w, 32)
                pe.sem_inc(s_taken, 1)
                with pe.Fori(0, NST) as j:
                    pe.wait_ge(s_xs, j + 1)
                    for kb in range(2):
                        pe.wait_ge(s_free[kb], (2 - kb) * j + 1)
                        transposed(pe, K["I32"][:, :], PS[kb], XS, ST, kb * P).then_inc(s_full[kb], 1)
                    pe.wait_ge(s_xt, 4 * j + 4)
                    for i in range(ST):
                        k, per, nth = 2 + i % 2, 3 - i % 2, i // 2
                        pe.wait_ge(s_free[k], per * j + nth + 1)
                        for kb in range(2):
                            m = pe.matmul(PS[k][:, 0:GH], XT[:, kb, i * P:(i + 1) * P], W[:, kb, :], start=kb == 0, stop=kb == 1)
                        m.then_inc(s_full[k], 1)
                    pe.wait_ge(s_sc, j + 1)
                    pe.wait_ge(s_free[0], 2 * j + 2)
                    for i in range(ST):
                        m = pe.transpose(PS[0][0:HEADS, cols(i)], ROW[:, i, GH:GW], K["I32"][:, :])
                    m.then_inc(s_full[0], 1)

        n_ = lambda x: sem("gm_" + x)
        s_ab, s_c, s_cf, s_ps, s_psf, s_self, s_bm, s_bo, s_taken = (n_(x) for x in (
            "scores_in", "c_in", "c_free", "ps", "ps_free", "self", "bm", "bm_out", "taken"))
        NEG = -1e30
        with nc.sbuf_tensor("gm_ab", [P, HEADS, NP], F32) as AB, nc.sbuf_tensor("gm_c", [P, 2, TILES, P], F16) as C, \
                nc.sbuf_tensor("gm_mask", [P, NP], BF16) as MK, nc.sbuf_tensor("gm_junk", [P, NP], BF16) as J, \
                nc.sbuf_tensor("gm_am", [P, HEADS], F32) as AM, nc.sbuf_tensor("gm_t", [P, TILES, HEADS], F32) as TM, \
                nc.Block() as block:
            @block.sync
            def _(sp):
                for h in range(HEADS):
                    sp.dma_start(AB[:, h, :], row_bc(T["gat_at"][h, :])).then_inc(s_ab, 16)
                cv = T["counts"][0:NP * NP, :].rearrange("(s p t c) a -> t p s (c a)", s=TILES, p=P, c=P)
                with sp.Fori(0, TILES) as t:
                    sp.wait_ge(s_cf, t + 1)
                    sp.dma_start(C[:, 0, :, :], cv[bass.ds(t, 1), :, :, :].rearrange("a p s c -> (a p) s c")).then_inc(s_c, 16)
                sp.wait_ge(s_bm, 1)
                sp.dma_start(T["gat_dst"].rearrange("(t p) w -> p t w", p=P), BM[:, :, :]).then_inc(s_bo, 16)
                sp.wait_ge(s_bo, 16)

            @block.tensor
            def _(pe):
                pe.sem_inc(s_cf, 1)
                pe.sem_inc(s_psf, 1)
                with pe.Fori(0, TILES) as t:
                    pe.wait_ge(s_c, 16 * (t + 1))
                    pe.wait_ge(s_psf, t + 1)
                    pe.sem_inc(s_taken, 1)
                    for s in range(TILES):
                        o = PS[s // 16][:, :].bitcast(F16)[:, (s % 16) * P:(s % 16 + 1) * P]
                        m = pe.transpose(o, C[:, 0, s, :], K["I16"][:, :])
                    m.then_inc(s_ps, 1)
                    pe.wait_ge(s_ps, t + 1)
                    pe.sem_inc(s_cf, 1)

            @block.vector
            def _(dve):
                ch = Chain(dve, s_self)
                dve.wait_ge(s_ab, 16 * HEADS)
                with dve.Fori(0, TILES) as t:
                    dve.wait_ge(s_ps, t + 1)
                    ch(dve.tensor_scalar(MK[:, 0:16 * P], PS[0][:, :].bitcast(F16), 0.0, NEG, ALU.is_equal, ALU.mult))
                    ch(dve.tensor_scalar(MK[:, 16 * P:], PS[1][:, :].bitcast(F16)[:, 0:NP - 16 * P], 0.0, NEG, ALU.is_equal, ALU.mult))
                    dve.sem_inc(s_psf, 1)
                    for h in range(HEADS):
                        ch(dve.tensor_tensor_reduce(out=J[:, :], in0=MK[:, :], in1=AB[:, h, :], scale=1.0, scalar=NEG,
                                                    op0=ALU.add, op1=ALU.max, accum_out=AM[:, h:h + 1]))
                    ch(dve.tensor_copy(BM[:, bass.ds(t, 1), HEADS:], AM[:, :].unsqueeze(1)))
                    ch.reset()
                ch(dve.tensor_tensor(TM[:, :, :], BM[:, :, 0:HEADS], BM[:, :, HEADS:], ALU.add))
                ch(dve.scalar_tensor_tensor(out=BM[:, :, HEADS:], in0=TM[:, :, :], scalar=0.2, in1=TM[:, :, :], op0=ALU.mult, op1=ALU.max))
                dve.sem_inc(s_bm, 1)
    sem.clear()


def same_targets(dve, ch, K, rows, tg, S, J, EC, index, s_scattered, n):
    ch.run(dve.tensor_tensor(S, rows, tg.unsqueeze(2).broadcast_to([P, RING, P]), ALU.is_equal))
    ch.run(dve.tensor_tensor(EC[:, 1, :], K["trash_row"][:, :].broadcast_to([P, RING]), tg, ALU.subtract))
    ch.sync()
    ch(dve.tensor_tensor(J, S, K["early"][:, :].unsqueeze(1).broadcast_to([P, RING, P]), ALU.mult))
    ch(dve.tensor_reduce(EC[:, 0, :], J, AX.X, ALU.add))
    ch(dve.scalar_tensor_tensor(out=EC[:, 2, :], in0=EC[:, 0, :], scalar=1.0, in1=EC[:, 1, :], op0=ALU.min, op1=ALU.mult))
    for k in range(RING):
        dve.wait_ge(s_scattered[k], 16 * (n + 1))
    ch(dve.tensor_tensor(index, EC[:, 2, :], tg, ALU.add))


def merge_group(pe, n, S, M, PS, width, s_m, s_copied, s_merged):
    pe.wait_ge(s_m, n)
    for k in range(RING):
        pe.wait_ge(s_copied, RING * n + k + 1)
        m = pe.matmul(PS[k][:, 0:min(width, 512)], S[:, k, :], M[:, k, 0:min(width, 512)], start=True, stop=True)
        if width > 512:
            m = pe.matmul(PS[k][:, 512:width], S[:, k, :], M[:, k, 512:width], start=True, stop=True)
        m.then_inc(s_merged, 1)


def gat_edges(nc, A, T, K, PS):
    sem = Semaphores(nc)
    ks = range(RING)
    n_ = lambda x: [sem(f"ge_{x}{h}") for h in range(2)]
    s_g, s_id, s_used, s_rin, s_rf, s_o = (n_(x) for x in ("in", "ids", "used", "targets_in", "targets_free", "rows"))
    s_sc = T["scat"]
    s_self, s_taken, s_taken2, s_e, s_x, s_m, s_mg, s_cp, s_cph = (sem("ge_" + x) for x in (
        "self", "taken", "taken2", "scores", "exp", "msg", "merged", "copied", "half"))
    drow = A["dst_row"].rearrange("(g n) -> g n", n=RING * P)
    with nc.sbuf_tensor("ge_g", [P, 2, RING, GW], F32) as G, nc.sbuf_tensor("ge_h", [P, 2, RING, 2 * HEADS], F32) as H, \
            nc.sbuf_tensor("ge_m", [P, 2, RING, GW], F32) as M, nc.sbuf_tensor("ge_o", [P, 2, RING, GW], F32) as O, \
            nc.sbuf_tensor("ge_s", [P, 2, RING, P], F32) as S, nc.sbuf_tensor("ge_j", [P, RING, P], F32) as J, \
            nc.sbuf_tensor("ge_r", [P, 2, RING * P], I32) as R, nc.sbuf_tensor("ge_id", [P, 2, 2, RING], I32) as ID, \
            nc.sbuf_tensor("ge_e", [P, 2, 3, RING, HEADS], F32) as E, nc.sbuf_tensor("ge_tg", [P, 2, RING], F32) as TG, \
            nc.sbuf_tensor("ge_c", [P, 3, RING], F32) as EC, nc.sbuf_tensor("ge_ix", [P, 2, RING], I32) as IX, \
            nc.Block() as block:
        @block.sync
        def _(sp):
            with sp.Fori(0, GROUPS // 2) as it:
                for h in range(2):
                    sp.wait_ge(s_rf[h], it + 1)
                    sp.dma_start(R[:, h, :], row_bc(drow[bass.ds(2 * it + h, 1), :].rearrange("a n -> (a n)"))).then_inc(s_rin[h], 16)

        @block.gpsimd
        def _(pool):
            def gather(h, k):
                pool.indirect_dma_start(out=G[:, h, k, :], out_offset=None, in_=T["gat_src"],
                                        in_offset=bass.IndirectOffsetOnAxis(ap=ID[:, h, 0, k:k + 1], axis=0)).then_inc(s_g[h], 16)
                pool.indirect_dma_start(out=H[:, h, k, :], out_offset=None, in_=T["gat_dst"],
                                        in_offset=bass.IndirectOffsetOnAxis(ap=ID[:, h, 1, k:k + 1], axis=0)).then_inc(s_g[h], 16)

            def scatter(h, k, n):
                pool.wait_ge(s_sc[k], 16 * (n + 2))
                pool.sem_inc(s_taken, 1)
                pool.indirect_dma_start(out=T["acc1"][k], out_offset=bass.IndirectOffsetOnAxis(ap=IX[:, h, k:k + 1], axis=0),
                                        in_=O[:, h, k, :], in_offset=None, compute_op=ALU.add).then_inc(s_sc[k], 16)

            for h in range(2):
                pool.wait_ge(s_id[h], 1)
                for k in ks:
                    gather(h, k)
            with pool.Fori(0, GROUPS // 2 - 1) as it:
                for h in range(2):
                    pool.wait_ge(s_id[h], it + 2)
                    pool.wait_ge(s_used[h], it + 1)
                    pool.sem_inc(s_taken, 1)
                    for k in ks:
                        gather(h, k)
                    pool.wait_ge(s_o[h], it + 1)
                    for k in ks:
                        scatter(h, k, 2 * it + h)
            for h in range(2):
                pool.wait_ge(s_o[h], GROUPS // 2)
                for k in ks:
                    scatter(h, k, GROUPS - 2 + h)
            for k in ks:
                pool.wait_ge(s_sc[k], 16 * (GROUPS + 2))

        @block.vector
        def _(dve):
            ch = Chain(dve, s_self)
            for h in range(2):
                ch.run(dve.tensor_copy(ID[:, h, 0, :], K["srci"][:, h * RING:(h + 1) * RING]))
                ch.run(dve.tensor_copy(ID[:, h, 1, :], K["dsti"][:, h * RING:(h + 1) * RING]))
                ch.sync()
                dve.sem_inc(s_id[h], 1)
                dve.sem_inc(s_rf[h], 1)
            ch.reset()
            with dve.Fori(0, GROUPS // 2) as it:
                for h in range(2):
                    n = 2 * it + h
                    dve.wait_ge(s_g[h], 16 * 2 * RING * (it + 1))
                    dve.sem_inc(s_taken2, 1)
                    ch.run(dve.tensor_copy(ID[:, h, 0, :], K["srci"][:, bass.ds((n + 2) * RING, RING)]))
                    ch.run(dve.tensor_copy(ID[:, h, 1, :], K["dsti"][:, bass.ds((n + 2) * RING, RING)]))
                    ch.run(dve.tensor_copy(TG[:, h, :], K["dstf"][:, bass.ds(n * RING, RING)]))
                    ch(dve.tensor_tensor(E[:, h, 0, :, :], G[:, h, :, GH:], H[:, h, :, 0:HEADS], ALU.add))
                    dve.sem_inc(s_id[h], 1)
                    ch(dve.scalar_tensor_tensor(out=E[:, h, 1, :, :], in0=E[:, h, 0, :, :], scalar=0.2, in1=E[:, h, 0, :, :],
                                                op0=ALU.mult, op1=ALU.max))
                    ch(dve.tensor_tensor(E[:, h, 2, :, :], E[:, h, 1, :, :], H[:, h, :, HEADS:], ALU.subtract))
                    dve.sem_inc(s_e, 1)
                    dve.wait_ge(s_cp, RING * (n + 1))
                    dve.wait_ge(s_rin[h], 16 * (it + 1))
                    dve.sem_inc(s_taken2, 1)
                    same_targets(dve, ch, K, R[:, h, :].rearrange("p (k x) -> p k x", k=RING), TG[:, h, :], S[:, h, :, :],
                                 J[:, :, :], EC, IX[:, h, :], s_sc, n)
                    dve.sem_inc(s_rf[h], 1)
                    dve.wait_ge(s_x, n + 1)
                    for k in ks:
                        ch.run(dve.tensor_tensor(M[:, h, k, 0:GH].rearrange("p (h o) -> p h o", h=HEADS),
                                                 G[:, h, k, 0:GH].rearrange("p (h o) -> p h o", h=HEADS),
                                                 M[:, h, k, GH:].unsqueeze(2).broadcast_to([P, HEADS, HID]), ALU.mult))
                    ch.sync()
                    dve.sem_inc(s_used[h], 1)
                    dve.sem_inc(s_m, 1)
                ch.reset()

        @block.scalar
        def _(act):
            def exp(h, n):
                act.wait_ge(s_e, n)
                act.activation(M[:, h, :, GH:], E[:, h, 2, :, :], ACT.Exp).then_inc(s_x, 1)

            def copy(h, n):
                for k in ks:
                    act.wait_ge(s_mg, RING * n + k + 1)
                    act.activation(O[:, h, k, 0:GH], PS[k][:, 0:GH], ACT.Copy).then_inc(s_cph, 1)
                    act.activation(O[:, h, k, GH:], PS[k][:, 512:512 + HEADS], ACT.Copy).then_inc(s_cph, 1)
                    act.wait_ge(s_cph, 2 * (RING * n + k + 1))
                    act.sem_inc(s_cp, 1)
                act.sem_inc(s_o[h], 1)

            act.sem_inc(s_cp, 2 * RING)
            exp(0, 1)
            with act.Fori(0, GROUPS // 2 - 1) as it:
                for h in range(2):
                    exp(1 - h, 2 * it + h + 2)
                    copy(h, 2 * it + h)
            exp(1, GROUPS)
            for h in range(2):
                copy(h, GROUPS - 2 + h)

        @block.tensor
        def _(pe):
            with pe.Fori(0, GROUPS // 2) as it:
                for h in range(2):
                    merge_group(pe, 2 * it + h + 1, S[:, h, :, :], M[:, h, :, :], PS, GW, s_m, s_cp, s_mg)
    sem.clear()


def gat_out(nc, A, T, K, PS):
    sem = Semaphores(nc)
    n_ = lambda x: sem("go_" + x)
    s_w, s_in, s_free_in, s_self, s_o, s_xt, s_xth, s_y, s_x, s_taken = (n_(x) for x in (
        "w", "in", "in_free", "self", "o", "xt", "xth", "y", "exp", "taken"))
    s_full, s_free = [n_(f"full{k}") for k in range(4)], [n_(f"free{k}") for k in range(4)]
    with nc.sbuf_tensor("go_acc", [P, RING, ST, GW], F32) as AC, nc.sbuf_tensor("go_w", [P, 4, D], F32) as W, \
            nc.sbuf_tensor("go_b", [P, 1, D], F32) as B, nc.sbuf_tensor("go_o", [P, ST, GH], F32) as O, \
            nc.sbuf_tensor("go_d", [P, ST, HEADS], F32) as DN, nc.sbuf_tensor("go_xt", [P, 4, SW], F32) as XT, \
            nc.sbuf_tensor("go_y", [P, ST, D], F32) as Y, nc.sbuf_tensor("go_n", [P, ST, D], F32) as N, \
            nc.sbuf_tensor("go_e", [P, ST, D], F32) as E, nc.Block() as block:
        @block.sync
        def _(sp):
            sp.dma_start(W[:, :, :], A["L1_gnn_Wo"].rearrange("(k p) n -> p k n", p=P)).then_inc(s_w, 16)
            sp.dma_start(B[:, 0, :], row_bc(A["L1_gnn_bo"])).then_inc(s_w, 16)
            with sp.Fori(0, NST) as j:
                sp.wait_ge(s_free_in, j + 1)
                for k in range(RING):
                    v = T["acc1"][k][0:NP, :].rearrange("(j t p) w -> j p t w", t=ST, p=P)
                    sp.dma_start(AC[:, k, :, :], v[bass.ds(j, 1), :, :, :].rearrange("a p t w -> (a p) t w")).then_inc(s_in, 16)

        @block.vector
        def _(dve):
            ch = Chain(dve, s_self)
            dve.sem_inc(s_free_in, 1)
            dve.wait_ge(s_w, 32)
            ch(dve.memset(DN[:, :, :], 0.0))
            ch.reset()
            with dve.Fori(0, NST) as j:
                dve.wait_ge(s_in, 16 * RING * (j + 1))
                for k in range(1, RING):
                    ch(dve.tensor_tensor(AC[:, 0, :, :], AC[:, 0, :, :], AC[:, k, :, :], ALU.add))
                ch(dve.tensor_scalar(DN[:, :, :], AC[:, 0, :, GH:], 1e-16, None, ALU.add))
                ch(dve.reciprocal(DN[:, :, :], DN[:, :, :]))
                for i in range(ST):
                    ch(dve.tensor_tensor(O[:, i, :].rearrange("p (h o) -> p h o", h=HEADS),
                                         AC[:, 0, i, 0:GH].rearrange("p (h o) -> p h o", h=HEADS),
                                         DN[:, i, :].unsqueeze(2).broadcast_to([P, HEADS, HID]), ALU.mult))
                dve.sem_inc(s_free_in, 1)
                dve.sem_inc(s_o, 1)
                for i in range(ST):
                    k, per, nth = i % 2, 4 - i % 2, 1 + i // 2
                    dve.wait_ge(s_full[k], per * j + nth + 1)
                    ch(dve.tensor_tensor(Y[:, i, :], PS[k][:, 0:D], B[:, 0, :], ALU.add))
                    dve.sem_inc(s_free[k], 1)
                ch(dve.tensor_scalar(N[:, :, :], Y[:, :, :], 0.0, None, ALU.min))
                dve.sem_inc(s_y, 1)
                ch(dve.tensor_scalar(Y[:, :, :], Y[:, :, :], 0.0, -1.0, ALU.max, ALU.add))
                dve.wait_ge(s_x, j + 1)
                ch(dve.tensor_tensor(Y[:, :, :], Y[:, :, :], E[:, :, :], ALU.add))
                xs = K["X"][:, bass.ds(j * ST, ST), :]
                ch(dve.tensor_tensor(xs, xs, Y[:, :, :], ALU.add))
                ch.reset()

        @block.scalar
        def _(act):
            for k in range(4):
                act.sem_inc(s_free[k], 1)
            with act.Fori(0, NST) as j:
                for kb in range(4):
                    per = (4, 3, 1, 1)[kb]
                    act.wait_ge(s_full[kb], per * j + 1)
                    for a, b in HALVES:
                        act.activation(XT[:, kb, b], PS[kb][:, a], ACT.Copy).then_inc(s_xth, 1)
                    act.wait_ge(s_xth, 8 * j + 2 * kb + 2)
                    act.sem_inc(s_free[kb], 1)
                act.sem_inc(s_xt, 1)
                act.wait_ge(s_y, j + 1)
                act.activation(E[:, :, :], N[:, :, :], ACT.Exp).then_inc(s_x, 1)

        @block.tensor
        def _(pe):
            pe.wait_ge(s_w, 32)
            pe.sem_inc(s_taken, 1)
            with pe.Fori(0, NST) as j:
                pe.wait_ge(s_o, j + 1)
                for kb in range(4):
                    pe.wait_ge(s_free[kb], (4, 3, 1, 1)[kb] * j + 1)
                    transposed(pe, K["I32"][:, :], PS[kb], O, ST, kb * P).then_inc(s_full[kb], 1)
                pe.wait_ge(s_xt, j + 1)
                for i in range(ST):
                    k, per, nth = i % 2, 4 - i % 2, 1 + i // 2
                    pe.wait_ge(s_free[k], per * j + nth + 1)
                    for kb in range(4):
                        m = pe.matmul(PS[k][:, 0:D], XT[:, kb, i * P:(i + 1) * P], W[:, kb, :], start=kb == 0, stop=kb == 3)
                    m.then_inc(s_full[k], 1)
    final_norm(nc, K, "gat_ln", None)
    sem.clear()


def deep_gin(nc, A, T, K, PS):
    sem = Semaphores(nc)
    KB = F2 // P
    s_self = sem("dg_self")
    with nc.sbuf_tensor("dg_wf", [P, 2 + LAYERS * KB, D], F32) as WF, nc.sbuf_tensor("dg_ob", [P, D], F32) as OB:
        fold_output(nc, A, K, PS, WF, OB)
        n_ = lambda x: sem("dg_" + x)
        s_w, s_xs, s_xt, s_taken, s_hl, s_tabout, s_drain = (n_(x) for x in ("w", "xs", "xt", "taken", "split", "tab_out", "drained"))
        s_full, s_free = [n_(f"sfull{k}") for k in range(4)], [n_(f"sfree{k}") for k in range(4)]
        tab_d = T["tab2"].rearrange("(j t p) w -> j p t w", t=ST, p=P)

        def rows_out(dve, ch, ps, i, j, BR, HF, HL):
            ch(dve.tensor_tensor(HF[:, :], ps[:, 0:F2], BR[:, :], ALU.add))
            xs = K["X"][:, bass.ds(j * ST + i, 1), :]
            ch(dve.tensor_tensor(xs, xs, ps[:, 512:512 + D].unsqueeze(1), ALU.add))

        with nc.sbuf_tensor("dg_win", [P, 2, F2], F32) as W, nc.sbuf_tensor("dg_brow", [P, F2], F32) as BR, \
                nc.sbuf_tensor("dg_xs", [P, ST, D], F32) as XS, nc.sbuf_tensor("dg_xt", [P, 2, SW], F32) as XT, \
                nc.sbuf_tensor("dg_hf0", [P, F2], F32) as HF, nc.sbuf_tensor("dg_hl0", [P, ST, 2 * F2], F16) as HL, \
                nc.Block() as block:
            @block.sync
            def _(sp):
                sp.dma_start(W[:, :, :], A["L2_gnn_in_W"].rearrange("(k p) n -> p k n", p=P)).then_inc(s_w, 16)
                sp.dma_start(BR[:, :], row_bc(A["L2_gnn_in_b"])).then_inc(s_w, 16)
                with sp.Fori(0, NST) as j:
                    sp.wait_ge(s_hl, j + 1)
                    sp.dma_start(tab_d[bass.ds(j, 1), :, :, :].rearrange("a p t w -> (a p) t w"), HL[:, :, :]).then_inc(s_tabout, 16)
                    sp.wait_ge(s_tabout, 16 * (j + 1))
                    sp.sem_inc(s_drain, 1)

            @block.vector
            def _(dve):
                ch = Chain(dve, s_self)
                dve.sem_inc(s_drain, 1)
                dve.wait_ge(s_w, 32)
                with dve.Fori(0, NST) as j:
                    ch(dve.tensor_copy(XS[:, :, :], K["X"][:, bass.ds(j * ST, ST), :]))
                    dve.sem_inc(s_xs, 1)
                    mine = K["X"][:, bass.ds(j * ST, ST), :]
                    ch(dve.tensor_tensor(mine, mine, OB[:, :].unsqueeze(1).broadcast_to([P, ST, D]), ALU.add))
                    dve.wait_ge(s_drain, j + 1)
                    for i in range(ST):
                        k, per, nth = 2 + i % 2, 3 - i % 2, i // 2
                        dve.wait_ge(s_full[k], per * j + nth + 1)
                        rows_out(dve, ch, PS[k], i, j, BR, HF, HL)
                        dve.sem_inc(s_free[k], 1)
                        split16(ch, dve, HF[:, :], HL[:, i, 0:F2], HL[:, i, F2:])
                    dve.sem_inc(s_hl, 1)
                    ch.reset()

            @block.scalar
            def _(act):
                for k in range(4):
                    act.sem_inc(s_free[k], 1)
                with act.Fori(0, NST) as j:
                    for kb in range(2):
                        act.wait_ge(s_full[kb], j + 1)
                        for a, b in HALVES:
                            act.activation(XT[:, kb, b], PS[kb][:, a], ACT.Copy).then_inc(s_xt, 1)
                        act.wait_ge(s_xt, 4 * j + 2 * kb + 2)
                        act.sem_inc(s_free[kb], 1)

            @block.tensor
            def _(pe):
                pe.wait_ge(s_w, 32)
                pe.sem_inc(s_taken, 1)
                with pe.Fori(0, NST) as j:
                    pe.wait_ge(s_xs, j + 1)
                    for kb in range(2):
                        pe.wait_ge(s_free[kb], j + 1)
                        transposed(pe, K["I32"][:, :], PS[kb], XS, ST, kb * P).then_inc(s_full[kb], 1)
                    pe.wait_ge(s_xt, 4 * j + 4)
                    for i in range(ST):
                        k, per, nth = 2 + i % 2, 3 - i % 2, i // 2
                        pe.wait_ge(s_free[k], per * j + nth + 1)
                        for kb in range(2):
                            pe.matmul(PS[k][:, 0:F2], XT[:, kb, i * P:(i + 1) * P], W[:, kb, :], start=kb == 0, stop=kb == 1)
                        for kb in range(2):
                            m = pe.matmul(PS[k][:, 512:512 + D], XT[:, kb, i * P:(i + 1) * P], WF[:, kb, :], start=kb == 0, stop=kb == 1)
                        m.then_inc(s_full[k], 1)

        s_tab, s_w, s_taken, s_hl, s_tabout, s_zt, s_ut = (n_("l" + x) for x in ("tab_in", "w", "taken", "split", "tab_out", "zt", "ut"))
        s_drain = n_("ldrained")
        s_cin, s_cout = [n_(f"c_in{q}") for q in range(ST)], [n_(f"c_out{q}") for q in range(ST)]
        s_full, s_free = [n_(f"full{k}") for k in range(4)], [n_(f"free{k}") for k in range(4)]
        NW = 4
        with nc.sbuf_tensor("dg_tab", [P, TILES, 2 * F2], F16) as TAB, \
                nc.sbuf_tensor("dg_c", [P, ST, ST, SW], F16) as C, \
                nc.sbuf_tensor("dg_w1", [P, KB, F2], F32) as W1, nc.sbuf_tensor("dg_w2", [P, KB, F2], F32) as W2, \
                nc.sbuf_tensor("dg_b1", [P, KB], F32) as B1, nc.sbuf_tensor("dg_b2", [P, F2], F32) as BR, \
                nc.sbuf_tensor("dg_hf", [P, F2], F32) as HF, nc.sbuf_tensor("dg_hl", [P, ST, 2 * F2], F16) as HL, \
                nc.sbuf_tensor("dg_zt", [P, KB, SW], F32) as ZT, nc.sbuf_tensor("dg_ut", [P, KB, SW], F32) as UT, \
                nc.Block() as block:
            @block.sync
            def _(sp):
                with sp.Fori(0, LAYERS) as l:
                    one = bass.ds(l, 1)
                    sp.wait_ge(s_drain, NST * l + 1)
                    sp.dma_start(TAB[:, :, :], T["tab2"].rearrange("(t p) w -> p t w", p=P)).then_inc(s_tab, 16)
                    for dst, name in ((W1, "L2_gnn_conv_W1"), (W2, "L2_gnn_conv_W2")):
                        sp.dma_start(dst[:, :, :], A[name][one, :, :].rearrange("a (k p) n -> p (a k) n", p=P)).then_inc(s_w, 16)
                    sp.dma_start(B1[:, :], A["L2_gnn_conv_b1"][one, :, :].rearrange("a p k -> (a p) k")).then_inc(s_w, 16)
                    sp.dma_start(BR[:, :], row_bc(A["L2_gnn_conv_b2"][one, :].rearrange("a n -> (a n)"))).then_inc(s_w, 16)
                    with sp.Fori(0, NST) as j:
                        load_counts(sp, T, C, s_cin, s_cout, j, l * NST + j)

            @block.gpsimd
            def _(pool):
                pool.sem_inc(s_drain, 1)
                with pool.Fori(0, LAYERS) as l:
                    with pool.Fori(0, NST) as j:
                        g = l * NST + j
                        pool.wait_ge(s_hl, g + 1)
                        pool.sem_inc(s_taken, 1)
                        pool.dma_start(tab_d[bass.ds(j, 1), :, :, :].rearrange("a p t w -> (a p) t w"), HL[:, :, :]).then_inc(s_tabout, 16)
                        pool.wait_ge(s_tabout, 16 * (g + 1))
                        pool.sem_inc(s_drain, 1)

            @block.vector
            def _(dve):
                ch = Chain(dve, s_self)
                with dve.Fori(0, LAYERS) as l:
                    dve.wait_ge(s_w, 16 * NW * (l + 1))
                    dve.sem_inc(s_taken, 1)
                    with dve.Fori(0, NST) as j:
                        g = l * NST + j
                        dve.wait_ge(s_drain, g + 1)
                        for i in range(ST):
                            k = 2 + i % 2
                            per, nth = (5, 2 + i // 2) if k == 2 else (4, 2 + i // 2)
                            dve.wait_ge(s_full[k], per * g + nth + 1)
                            rows_out(dve, ch, PS[k], i, j, BR, HF, HL)
                            dve.sem_inc(s_free[k], 1)
                            split16(ch, dve, HF[:, :], HL[:, i, 0:F2], HL[:, i, F2:])
                        dve.sem_inc(s_hl, 1)
                        ch.reset()

            @block.scalar
            def _(act):
                for q in range(ST):
                    act.sem_inc(s_cout[q], 1)
                for k in range(4):
                    act.sem_inc(s_free[k], 1)
                with act.Fori(0, LAYERS) as l:
                    act.wait_ge(s_w, 16 * NW * (l + 1))
                    act.sem_inc(s_taken, 1)
                    with act.Fori(0, NST) as j:
                        g = l * NST + j
                        for fb in range(KB):
                            act.wait_ge(s_full[fb % 2], 2 * g + fb // 2 + 1)
                            for a, b in HALVES:
                                act.activation(ZT[:, fb, b], PS[fb % 2][:, a], ACT.Copy).then_inc(s_zt, 1)
                            act.wait_ge(s_zt, 2 * KB * g + 2 * fb + 2)
                            act.sem_inc(s_free[fb % 2], 1)
                        for hb in range(KB):
                            k = 2 + hb % 2
                            act.wait_ge(s_full[k], (5 - hb % 2) * g + hb // 2 + 1)
                            for a, b in HALVES:
                                act.activation(UT[:, hb, b], PS[k][:, a], ACT.Relu, bias=B1[:, hb:hb + 1]).then_inc(s_ut, 1)
                            act.wait_ge(s_ut, 2 * KB * g + 2 * hb + 2)
                            act.sem_inc(s_free[k], 1)

            @block.tensor
            def _(pe):
                with pe.Fori(0, LAYERS) as l:
                    pe.wait_ge(s_w, 16 * NW * (l + 1))
                    pe.wait_ge(s_tab, 16 * (l + 1))
                    pe.sem_inc(s_taken, 1)
                    with pe.Fori(0, NST) as j:
                        g = l * NST + j
                        for fb in range(KB):
                            ps = PS[fb % 2]

                            def own():
                                for i in range(ST):
                                    for part in range(2):
                                        a = part * F2 + fb * P
                                        w = TAB[:, bass.ds(j * ST + i, 1), a:a + P].rearrange("p a w -> p (a w)")
                                        pe.matmul(ps[:, cols(i)], w, K["I16"][:, :], start=False, stop=False, skip_group_check=True)
                            pe.wait_ge(s_free[fb % 2], 2 * g + fb // 2 + 1)
                            neighbour_sum(pe, TAB, C, ps, fb, F2, s_cin, s_cout, g, fb == KB - 1, own).then_inc(s_full[fb % 2], 1)
                        pe.wait_ge(s_zt, 2 * KB * (g + 1))
                        pe.sem_inc(s_cout[ST - 1], 1)
                        for hb in range(KB):
                            k = 2 + hb % 2
                            pe.wait_ge(s_free[k], (5 - hb % 2) * g + hb // 2 + 1)
                            for a, b in HALVES:
                                for kb in range(KB):
                                    m = pe.matmul(PS[k][:, a], W1[:, kb, hb * P:(hb + 1) * P], ZT[:, kb, b],
                                                  start=kb == 0, stop=kb == KB - 1)
                            m.then_inc(s_full[k], 1)
                        pe.wait_ge(s_ut, 2 * KB * (g + 1))
                        for i in range(ST):
                            k = 2 + i % 2
                            per, nth = (5, 2 + i // 2) if k == 2 else (4, 2 + i // 2)
                            pe.wait_ge(s_free[k], per * g + nth + 1)
                            for kb in range(KB):
                                pe.matmul(PS[k][:, 0:F2], UT[:, kb, i * P:(i + 1) * P], W2[:, kb, :], start=kb == 0, stop=kb == KB - 1)
                            for kb in range(KB):
                                wf = WF[:, bass.ds(2 + KB * l + kb, 1), :].rearrange("p a n -> p (a n)")
                                m = pe.matmul(PS[k][:, 512:512 + D], UT[:, kb, i * P:(i + 1) * P], wf, start=kb == 0, stop=kb == KB - 1)
                            m.then_inc(s_full[k], 1)
    final_norm(nc, K, "dg_ln", None)
    sem.clear()


def fold_output(nc, A, K, PS, WF, OB):
    sem = Semaphores(nc)
    n_ = lambda x: sem("fo_" + x)
    s_w, s_b, s_self, s_full, s_free, s_bb, s_bf = (n_(x) for x in ("w", "b", "self", "full", "free", "bias", "bias_full"))
    KB = F2 // P
    with nc.sbuf_tensor("fo_wt", [P, KB, F2], F32) as WT, nc.sbuf_tensor("fo_wo", [P, LAYERS + 1, KB, D], F32) as WO, \
            nc.sbuf_tensor("fo_b", [P, LAYERS + 1, KB], F32) as B, nc.sbuf_tensor("fo_bb", [P, LAYERS + 1, KB, P], F32) as BB, \
            nc.Block() as block:
        @block.sync
        def _(sp):
            sp.dma_start(WO[:, :, :, :].rearrange("p l k n -> p (l k) n"),
                         A["L2_gnn_out_W"].rearrange("(k p) n -> p k n", p=P)).then_inc(s_b, 16)
            sp.dma_start(B[:, 0, :], A["L2_gnn_in_bc"]).then_inc(s_b, 16)
            for l in range(LAYERS):
                sp.dma_start(B[:, l + 1, :], A["L2_gnn_conv_b2c"][l]).then_inc(s_b, 16)
            sp.dma_start(OB[:, :], row_bc(A["L2_gnn_out_b"])).then_inc(s_b, 16)
            sp.dma_start(WT[:, :, 0:D], A["L2_gnn_in_WT"].rearrange("(k p) n -> p k n", p=P)).then_inc(s_w, 16)
            for l in range(LAYERS):
                sp.wait_ge(s_free, 2 + KB * l)
                sp.dma_start(WT[:, :, :], A["L2_gnn_conv_W2T"][l].rearrange("(k p) n -> p k n", p=P)).then_inc(s_w, 16)

        @block.tensor
        def _(pe):
            pe.wait_ge(s_b, 16 * (LAYERS + 3))
            n = 0
            for l in range(LAYERS + 1):
                pe.wait_ge(s_w, 16 * (l + 1))
                for ib in range(2 if l == 0 else KB):
                    if n >= 2:
                        pe.wait_ge(s_free, n - 1)
                    for kb in range(KB):
                        m = pe.matmul(PS[n % 2][:, 0:D], WT[:, kb, ib * P:(ib + 1) * P], WO[:, l, kb, :], start=kb == 0, stop=kb == KB - 1)
                    m.then_inc(s_full, 1)
                    n += 1
            pe.wait_ge(s_bb, 1)
            for l in range(LAYERS + 1):
                for kb in range(KB):
                    m = pe.matmul(PS[2][:, 0:D], BB[:, l, kb, :], WO[:, l, kb, :], start=l + kb == 0, stop=l + kb == LAYERS + KB - 1)
            m.then_inc(s_bf, 1)

        @block.vector
        def _(dve):
            ch = Chain(dve, s_self)
            dve.wait_ge(s_b, 16 * (LAYERS + 3))
            for l in range(LAYERS + 1):
                for kb in range(KB):
                    ch(dve.tensor_scalar(BB[:, l, kb, :], K["ones"][:, :], B[:, l, kb:kb + 1], None, ALU.mult))
            dve.sem_inc(s_bb, 1)
            for n in range(2 + LAYERS * KB):
                dve.wait_ge(s_full, n + 1)
                dve.tensor_copy(WF[:, n, :], PS[n % 2][:, 0:D]).then_inc(s_free, 1)
            dve.wait_ge(s_bf, 1)
            ch(dve.tensor_tensor(OB[:, :], PS[2][:, 0:D], OB[:, :], ALU.add))
    sem.clear()


def att_nodes(nc, A, T, K, PS):
    sem = Semaphores(nc)
    n_ = lambda x: sem("an_" + x)
    s_w, s_self, s_taken, s_zero, s_xs, s_xt, s_ut, s_ft, s_rb, s_cb, s_cbh, s_out, s_drain = (n_(x) for x in (
        "w", "self", "taken", "zero", "xs", "xt", "ut", "ft", "rb", "cb", "cbh", "out", "drained"))
    s_full, s_free = [n_(f"full{k}") for k in range(4)], [n_(f"free{k}") for k in range(4)]
    HB = 2 * ATT
    with nc.sbuf_tensor("an_w1", [P, PH, 2, D], F32) as W1, nc.sbuf_tensor("an_w2", [P, PH, 2, P], F32) as W2, \
            nc.sbuf_tensor("an_b1", [P, PH, 2], F32) as B1, nc.sbuf_tensor("an_b2", [P, 2], F32) as B2, \
            nc.sbuf_tensor("an_a", [P, 2, 2, HB], F32) as AA, nc.sbuf_tensor("an_ab", [P, 2, HB], F32) as AB, \
            nc.sbuf_tensor("an_xs", [P, ST, D], F32) as XS, nc.sbuf_tensor("an_xt", [P, 2, SW], F32) as XT, \
            nc.sbuf_tensor("an_ut", [P, 4, SW], F32) as UT, nc.sbuf_tensor("an_ft", [P, 2, SW], F32) as FT, \
            nc.sbuf_tensor("an_rb", [P, ST, AW], F32) as RB, nc.sbuf_tensor("an_cb", [P, ST, AW + PF], F32) as CB, \
            nc.Block() as block:
        NLOAD = 2 + PH + PH + 2 * PH + 1

        @block.sync
        def _(sp):
            sp.wait_ge(s_zero, 2)
            sp.dma_start(W1[:, :, :, :].rearrange("p h k n -> p (h k) n"),
                         A["L3_gnn_W1"].rearrange("h (k p) n -> p (h k) n", p=P)).then_inc(s_w, 16)
            sp.dma_start(B2[:, :], A["L3_gnn_b2c"]).then_inc(s_w, 16)
            for h in range(PH):
                lo = h % 2 * PO
                sp.dma_start(B1[:, h, :], A["L3_gnn_b1"][h]).then_inc(s_w, 16)
                sp.dma_start(W2[:, h, :, lo:lo + PO], A["L3_gnn_W2"][h].rearrange("(k p) n -> p k n", p=P)).then_inc(s_w, 16)
                for side in range(2):
                    sp.dma_start(AA[lo:lo + PO, h // 2, side, h % 2 * ATT:(h % 2 + 1) * ATT],
                                 A["L3_gnn_A1"][h, side * PO:(side + 1) * PO, :]).then_inc(s_w, 16)
            sp.dma_start(AB[:, :, :].rearrange("p a b -> p (a b)"), row_bc(A["L3_gnn_ab1"].rearrange("h n -> (h n)"))).then_inc(s_w, 16)
            with sp.Fori(0, NST) as j:
                sp.wait_ge(s_rb, j + 1)
                v = T["att_row"].rearrange("(j t p) w -> j p t w", t=ST, p=P)
                sp.dma_start(v[bass.ds(j, 1), :, :, :].rearrange("a p t w -> (a p) t w"), RB[:, :, :]).then_inc(s_out, 16)
                sp.wait_ge(s_cb, j + 1)
                v = T["att_col"].rearrange("(j t p) w -> j p t w", t=ST, p=P)
                sp.dma_start(v[bass.ds(j, 1), :, :, :].rearrange("a p t w -> (a p) t w"), CB[:, :, :]).then_inc(s_out, 16)
                sp.wait_ge(s_out, 32 * (j + 1))
                sp.sem_inc(s_drain, 1)

        @block.vector
        def _(dve):
            ch = Chain(dve, s_self)
            dve.memset(W2[:, :, :, :], 0.0).then_inc(s_zero, 1)
            dve.memset(AA[:, :, :, :], 0.0).then_inc(s_zero, 1)
            dve.sem_inc(s_drain, 1)
            dve.wait_ge(s_w, 16 * NLOAD)
            dve.sem_inc(s_taken, 1)
            with dve.Fori(0, NST) as j:
                ch(dve.tensor_copy(XS[:, :, :], K["X"][:, bass.ds(j * ST, ST), :]))
                dve.sem_inc(s_xs, 1)
                dve.wait_ge(s_drain, j + 1)
                for i in range(ST):
                    dve.wait_ge(s_full[2], 9 * j + 4 + i + 1)
                    ch(dve.tensor_tensor(RB[:, i, :].rearrange("p (a b) -> p a b", a=2),
                                         PS[2][:, :].rearrange("p (a b) -> p a b", a=2)[:, :, 0:HB], AB[:, :, :], ALU.add))
                    dve.sem_inc(s_free[2], 1)
                dve.sem_inc(s_rb, 1)
                ch.reset()

        @block.scalar
        def _(act):
            for k in range(4):
                act.sem_inc(s_free[k], 1)
            act.wait_ge(s_w, 16 * NLOAD)
            act.sem_inc(s_taken, 1)
            with act.Fori(0, NST) as j:
                def copy(k, n, out, s_done, before, func=ACT.Copy, **kw):
                    act.wait_ge(s_full[k], n)
                    for a, b in HALVES:
                        act.activation(out[:, b], PS[k][:, a], func, **kw).then_inc(s_done, 1)
                    act.wait_ge(s_done, before + 2)
                    act.sem_inc(s_free[k], 1)
                for kb in range(2):
                    copy(kb, 2 * j + 1, XT[:, kb, :], s_xt, 4 * j + 2 * kb)
                for hp in range(2):
                    for u in range(4):
                        copy(2 + u % 2, 9 * j + 2 * hp + u // 2 + 1, UT[:, u, :], s_ut, 16 * j + 8 * hp + 2 * u,
                             ACT.Relu, bias=B1[:, 2 * hp + u // 2, u % 2:u % 2 + 1])
                    copy(hp, 2 * j + 2, FT[:, hp, :], s_ft, 4 * j + 2 * hp, ACT.Identity, bias=B2[:, hp:hp + 1])
                act.wait_ge(s_drain, j + 1)
                act.sem_inc(s_taken, 1)
                for i in range(ST):
                    act.wait_ge(s_full[3], 9 * j + 4 + i + 1)
                    pv = PS[3][:, :].rearrange("p (a b) -> p a b", a=2)
                    act.activation(CB[:, i, 0:AW].rearrange("p (a b) -> p a b", a=2), pv[:, :, 0:HB], ACT.Copy).then_inc(s_cbh, 1)
                    act.activation(CB[:, i, AW:].rearrange("p (a b) -> p a b", a=2), pv[:, :, HB:HB + P], ACT.Copy).then_inc(s_cbh, 1)
                    act.wait_ge(s_cbh, 2 * (ST * j + i + 1))
                    act.sem_inc(s_free[3], 1)
                act.sem_inc(s_cb, 1)

        @block.tensor
        def _(pe):
            pe.wait_ge(s_w, 16 * NLOAD)
            pe.sem_inc(s_taken, 1)
            with pe.Fori(0, NST) as j:
                pe.wait_ge(s_xs, j + 1)
                for kb in range(2):
                    pe.wait_ge(s_free[kb], 2 * j + 1)
                    transposed(pe, K["I32"][:, :], PS[kb], XS, ST, kb * P).then_inc(s_full[kb], 1)
                pe.wait_ge(s_xt, 4 * j + 4)
                for hp in range(2):
                    for u in range(4):
                        k = 2 + u % 2
                        pe.wait_ge(s_free[k], 9 * j + 2 * hp + u // 2 + 1)
                        for a, b in HALVES:
                            for kb in range(2):
                                m = pe.matmul(PS[k][:, a], W1[:, 2 * hp + u // 2, kb, u % 2 * P:(u % 2 + 1) * P],
                                              XT[:, kb, b], start=kb == 0, stop=kb == 1)
                        m.then_inc(s_full[k], 1)
                    pe.wait_ge(s_ut, 16 * j + 8 * hp + 8)
                    pe.wait_ge(s_free[hp], 2 * j + 2)
                    for a, b in HALVES:
                        for u in range(4):
                            m = pe.matmul(PS[hp][:, a], W2[:, 2 * hp + u // 2, u % 2, :], UT[:, u, b], start=u == 0, stop=u == 3)
                    m.then_inc(s_full[hp], 1)
                pe.wait_ge(s_ft, 4 * j + 4)
                for i in range(ST):
                    for side in range(2):
                        k = 2 + side
                        pe.wait_ge(s_free[k], 9 * j + 4 + i + 1)
                        for hp in range(2):
                            f = FT[:, hp, i * P:(i + 1) * P]
                            m = pe.matmul(PS[k][:, 512 * hp:512 * hp + HB], f, AA[:, hp, side, :], start=True, stop=True)
                            if side:
                                m = pe.matmul(PS[k][:, 512 * hp + HB:512 * hp + HB + P], f, K["I32"][:, :], start=True, stop=True)
                        m.then_inc(s_full[k], 1)
    sem.clear()


def att_edges(nc, A, T, K, PS):
    sem = Semaphores(nc)
    ks = range(RING)
    with nc.sbuf_tensor("ae_w", [P, CHUNKS, PH], F32) as WA:
        n_ = lambda x: [sem(f"ae_{x}{h}") for h in range(2)]
        s_r, s_c, s_id, s_used, s_spill = (n_(x) for x in ("row_in", "col_in", "ids", "used", "spilt"))
        s_w, s_self, s_taken, s_taken2 = (sem("ae_" + x) for x in ("w", "self", "taken", "taken2"))
        spill = T["spill"].rearrange("(g k p) n -> g p k n", p=P, k=RING)
        with nc.sbuf_tensor("ae_r", [P, 2, RING, AW], F32) as R, nc.sbuf_tensor("ae_c", [P, 2, RING, AW + PF], F32) as C, \
                nc.sbuf_tensor("ae_rows", [P, 2, AW], F32) as RW, nc.sbuf_tensor("ae_id", [P, 2, 2, RING], I32) as ID, \
                nc.sbuf_tensor("ae_ew", [P, CHUNKS], F32) as EW, nc.sbuf_tensor("ae_ewk", [P, RING], F32) as EWK, \
                nc.sbuf_tensor("ae_z", [P, RING, AW], F32) as Z, nc.sbuf_tensor("ae_y", [P, RING, AW], F32) as Y, \
                nc.sbuf_tensor("ae_e", [P, RING * PH], F32) as E, nc.Block() as block:
            @block.sync
            def _(sp):
                for h in range(PH):
                    sp.dma_start(RW[:, 0, h * ATT:(h + 1) * ATT], row_bc(A["L3_gnn_A1"][h, ATT - 1, :])).then_inc(s_w, 16)
                sp.dma_start(RW[:, 1, :], row_bc(A["L3_gnn_A2"].rearrange("h n a -> (h n a)"))).then_inc(s_w, 16)
                sp.dma_start(EW[:, :], A["ew_col"]).then_inc(s_w, 16)
                with sp.Fori(0, GROUPS // 2) as it:
                    for h in range(2):
                        sp.wait_ge(s_c[h], 16 * RING * (it + 1))
                        sp.dma_start(spill[bass.ds(2 * it + h, 1), :, :, :].rearrange("a p k n -> (a p) k n"),
                                     C[:, h, :, AW:]).then_inc(s_spill[h], 16)
                for h in range(2):
                    sp.wait_ge(s_spill[h], 16 * (GROUPS // 2))

            @block.gpsimd
            def _(pool):
                def gathers(h):
                    for k in ks:
                        pool.indirect_dma_start(out=R[:, h, k, :], out_offset=None, in_=T["att_row"],
                                                in_offset=bass.IndirectOffsetOnAxis(ap=ID[:, h, 0, k:k + 1], axis=0)).then_inc(s_r[h], 16)
                        pool.indirect_dma_start(out=C[:, h, k, :], out_offset=None, in_=T["att_col"],
                                                in_offset=bass.IndirectOffsetOnAxis(ap=ID[:, h, 1, k:k + 1], axis=0)).then_inc(s_c[h], 16)
                for h in range(2):
                    pool.wait_ge(s_id[h], 1)
                    gathers(h)
                with pool.Fori(1, GROUPS // 2) as it:
                    for h in range(2):
                        pool.wait_ge(s_id[h], it + 1)
                        pool.wait_ge(s_used[h], it)
                        pool.wait_ge(s_spill[h], 16 * it)
                        pool.sem_inc(s_taken, 1)
                        gathers(h)

            @block.vector
            def _(dve):
                ch = Chain(dve, s_self)
                dve.wait_ge(s_w, 16 * (PH + 2))
                for h in range(2):
                    ch.run(dve.tensor_copy(ID[:, h, 0, :], K["srci"][:, h * RING:(h + 1) * RING]))
                    ch.run(dve.tensor_copy(ID[:, h, 1, :], K["dsti"][:, h * RING:(h + 1) * RING]))
                    ch.sync()
                    dve.sem_inc(s_id[h], 1)
                ch.reset()
                with dve.Fori(0, GROUPS // 2) as it:
                    for h in range(2):
                        n = 2 * it + h
                        dve.wait_ge(s_r[h], 16 * RING * (it + 1))
                        dve.wait_ge(s_c[h], 16 * RING * (it + 1))
                        dve.sem_inc(s_taken2, 1)
                        ch.run(dve.tensor_copy(ID[:, h, 0, :], K["srci"][:, bass.ds((n + 2) * RING, RING)]))
                        ch.run(dve.tensor_copy(ID[:, h, 1, :], K["dsti"][:, bass.ds((n + 2) * RING, RING)]))
                        ch.run(dve.tensor_copy(EWK[:, :], EW[:, bass.ds(n * RING, RING)]))
                        ch(dve.tensor_tensor(Z[:, :, :], R[:, h, :, :], C[:, h, :, 0:AW], ALU.add))
                        dve.sem_inc(s_id[h], 1)
                        dve.sem_inc(s_used[h], 1)
                        for k in ks:
                            ch.run(dve.scalar_tensor_tensor(out=Z[:, k, :], in0=RW[:, 0, :], scalar=EWK[:, k:k + 1], in1=Z[:, k, :],
                                                            op0=ALU.mult, op1=ALU.add))
                        ch.sync()
                        for k in ks:
                            for q in range(PH):
                                u = slice(q * ATT, (q + 1) * ATT)
                                ch.run(dve.scalar_tensor_tensor(out=Y[:, k, u], in0=Z[:, k, u], scalar=0.0, in1=RW[:, 1, u], op0=ALU.max,
                                                                op1=ALU.mult, accum_out=E[:, k * PH + q:k * PH + q + 1]))
                        ch.sync()
                        ch(dve.tensor_copy(WA[:, bass.ds(n * RING, RING), :].rearrange("p k h -> p (k h)"), E[:, :]))
                    ch.reset()

        s_w, s_self, s_part, s_max, s_sub, s_e = (sem("am_" + x) for x in ("w", "self", "part", "max", "sub", "exp"))
        FULL, REM = EDGES // P, EDGES % P
        with nc.sbuf_tensor("am_b", [P, PH], F32) as B, nc.sbuf_tensor("am_m", [P, PH], F32) as MX, \
                nc.sbuf_tensor("am_a", [P, PH], F32) as MA, nc.sbuf_tensor("am_t", [P, CHUNKS, PH], F32) as TM, nc.Block() as block:
            @block.sync
            def _(sp):
                sp.dma_start(B[:, :], row_bc(A["L3_gnn_ab2"].rearrange("h a -> (h a)"))).then_inc(s_w, 16)

            @block.vector
            def _(dve):
                ch = Chain(dve, s_self)
                dve.wait_ge(s_w, 16)
                ch(dve.tensor_tensor(TM[:, :, :], WA[:, :, :], B[:, :].unsqueeze(1).broadcast_to([P, CHUNKS, PH]), ALU.add))
                ch(dve.scalar_tensor_tensor(out=WA[:, :, :], in0=TM[:, :, :], scalar=0.2, in1=TM[:, :, :], op0=ALU.mult, op1=ALU.max))
                ch(dve.tensor_reduce(MX[:, :], WA[:, 0:FULL, :].rearrange("p c h -> p h c"), AX.X, ALU.max))
                ch(dve.tensor_tensor(MX[0:REM, :], MX[0:REM, :], WA[0:REM, FULL, :], ALU.max))
                dve.sem_inc(s_part, 1)
                dve.wait_ge(s_max, 1)
                top = MA[:, :].unsqueeze(1).broadcast_to([P, CHUNKS, PH])
                ch(dve.tensor_tensor(WA[:, :, :], WA[:, :, :], top, ALU.min))
                ch(dve.tensor_tensor(TM[:, :, :], WA[:, :, :], top, ALU.subtract))
                dve.sem_inc(s_sub, 1)

            @block.gpsimd
            def _(pool):
                pool.wait_ge(s_part, 1)
                pool.partition_all_reduce(MA[:, :], MX[:, :], P, MAX_OF_ALL).then_inc(s_max, 1)

            @block.scalar
            def _(act):
                act.wait_ge(s_sub, 1)
                act.activation(WA[:, :, :], TM[:, :, :], ACT.Exp).then_inc(s_e, 1)

        n_ = lambda x: [sem(f"aw_{x}{h}") for h in range(2)]
        s_f, s_rin, s_rf, s_o = (n_(x) for x in ("feats_in", "rows_in", "free", "rows"))
        s_sc = T["scat3"]
        s_self, s_taken, s_taken2, s_m, s_mg, s_cp = (sem("aw_" + x) for x in ("self", "taken", "taken2", "msg", "merged", "copied"))
        srow = A["src_row"].rearrange("(g n) -> g n", n=RING * P)
        with nc.sbuf_tensor("aw_f", [P, 2, RING, PF], F32) as F, nc.sbuf_tensor("aw_m", [P, 2, RING, PW], F32) as M, \
                nc.sbuf_tensor("aw_o", [P, 2, RING, PW], F32) as O, nc.sbuf_tensor("aw_s", [P, 2, RING, P], F32) as S, \
                nc.sbuf_tensor("aw_j", [P, RING, P], F32) as J, nc.sbuf_tensor("aw_r", [P, 2, RING * P], I32) as R, \
                nc.sbuf_tensor("aw_c", [P, 3, RING], F32) as EC, nc.sbuf_tensor("aw_tg", [P, RING], F32) as TG, \
                nc.sbuf_tensor("aw_ix", [P, 2, RING], I32) as IX, nc.Block() as block:
            @block.sync
            def _(sp):
                with sp.Fori(0, GROUPS // 2) as it:
                    for h in range(2):
                        g = bass.ds(2 * it + h, 1)
                        sp.wait_ge(s_rf[h], it + 1)
                        sp.dma_start(R[:, h, :], row_bc(srow[g, :].rearrange("a n -> (a n)"))).then_inc(s_rin[h], 16)
                        sp.dma_start(F[:, h, :, :], spill[g, :, :, :].rearrange("a p k n -> (a p) k n")).then_inc(s_f[h], 16)

            @block.gpsimd
            def _(pool):
                with pool.Fori(0, GROUPS // 2) as it:
                    for h in range(2):
                        pool.wait_ge(s_o[h], it + 1)
                        for k in ks:
                            pool.wait_ge(s_sc[k], 16 * (2 * it + h + 2))
                            pool.sem_inc(s_taken, 1)
                            pool.indirect_dma_start(out=T["acc3"][k], out_offset=bass.IndirectOffsetOnAxis(ap=IX[:, h, k:k + 1], axis=0),
                                                    in_=O[:, h, k, :], in_offset=None, compute_op=ALU.add).then_inc(s_sc[k], 16)
                for k in ks:
                    pool.wait_ge(s_sc[k], 16 * (GROUPS + 2))

            @block.vector
            def _(dve):
                ch = Chain(dve, s_self)
                for h in range(2):
                    dve.sem_inc(s_rf[h], 1)
                with dve.Fori(0, GROUPS // 2) as it:
                    for h in range(2):
                        n = 2 * it + h
                        ch.run(dve.tensor_copy(TG[:, :], K["srcf"][:, bass.ds(n * RING, RING)]))
                        ch.sync()
                        dve.wait_ge(s_cp, RING * (n + 1))
                        dve.wait_ge(s_rin[h], 16 * (it + 1))
                        dve.sem_inc(s_taken2, 1)
                        same_targets(dve, ch, K, R[:, h, :].rearrange("p (k x) -> p k x", k=RING), TG[:, :], S[:, h, :, :],
                                     J[:, :, :], EC, IX[:, h, :], s_sc, n)
                        ch(dve.tensor_copy(M[:, h, :, PF:], WA[:, bass.ds(n * RING, RING), :]))
                        dve.wait_ge(s_f[h], 16 * (it + 1))
                        for k in ks:
                            ch.run(dve.tensor_tensor(M[:, h, k, 0:PF].rearrange("p (h o) -> p h o", h=PH),
                                                     F[:, h, k, :].rearrange("p (h o) -> p h o", h=PH),
                                                     M[:, h, k, PF:].unsqueeze(2).broadcast_to([P, PH, PO]), ALU.mult))
                        ch.sync()
                        dve.sem_inc(s_m, 1)
                        dve.sem_inc(s_rf[h], 1)
                    ch.reset()

            @block.scalar
            def _(act):
                act.sem_inc(s_cp, 2 * RING)
                with act.Fori(0, GROUPS // 2) as it:
                    for h in range(2):
                        for k in ks:
                            n = RING * (2 * it + h) + k + 1
                            act.wait_ge(s_mg, n)
                            act.activation(O[:, h, k, :], PS[k][:, 0:PW], ACT.Copy).then_inc(s_cp, 1)
                        act.wait_ge(s_cp, n + 2 * RING)
                        act.sem_inc(s_o[h], 1)

            @block.tensor
            def _(pe):
                with pe.Fori(0, GROUPS // 2) as it:
                    for h in range(2):
                        merge_group(pe, 2 * it + h + 1, S[:, h, :, :], M[:, h, :, :], PS, PW, s_m, s_cp, s_mg)
    sem.clear()



def att_out(nc, A, T, K, PS):
    sem = Semaphores(nc)
    s_in, s_free, s_self, s_taken = (sem("ao_" + x) for x in ("in", "free", "self", "taken"))
    with nc.sbuf_tensor("ao_acc", [P, RING, ST, PW], F32) as AC, nc.sbuf_tensor("ao_d", [P, ST, PH], F32) as DN, \
            nc.sbuf_tensor("ao_o", [P, ST, D], F32) as O, nc.Block() as block:
        @block.sync
        def _(sp):
            with sp.Fori(0, NST) as j:
                sp.wait_ge(s_free, j + 1)
                for k in range(RING):
                    v = T["acc3"][k][0:NP, :].rearrange("(j t p) w -> j p t w", t=ST, p=P)
                    sp.dma_start(AC[:, k, :, :], v[bass.ds(j, 1), :, :, :].rearrange("a p t w -> (a p) t w")).then_inc(s_in, 16)

        @block.vector
        def _(dve):
            ch = Chain(dve, s_self)
            dve.sem_inc(s_free, 1)
            with dve.Fori(0, NST) as j:
                dve.wait_ge(s_in, 16 * RING * (j + 1))
                for k in range(1, RING):
                    ch(dve.tensor_tensor(AC[:, 0, :, :], AC[:, 0, :, :], AC[:, k, :, :], ALU.add))
                ch(dve.tensor_scalar(DN[:, :, :], AC[:, 0, :, PF:], 1e-10, None, ALU.add))
                ch(dve.reciprocal(DN[:, :, :], DN[:, :, :]))
                for i in range(ST):
                    ch(dve.tensor_tensor(O[:, i, :].rearrange("p (h o) -> p h o", h=PH),
                                         AC[:, 0, i, 0:PF].rearrange("p (h o) -> p h o", h=PH),
                                         DN[:, i, :].unsqueeze(2).broadcast_to([P, PH, PO]), ALU.mult))
                dve.sem_inc(s_free, 1)
                xs = K["X"][:, bass.ds(j * ST, ST), :]
                ch(dve.tensor_tensor(xs, xs, O[:, :, :], ALU.add))
                ch.reset()
    final_norm(nc, K, "att_ln", None)
    sem.clear()


PHASES = 10


def kernel(**inputs):
    import numpy as np
    import concourse.bacc as bacc
    from concourse.bass_utils import run_bass_kernel_spmd

    nc = bacc.Bacc("TRN2", target_bir_lowering=False, num_devices=1)
    arrays = layout(inputs)
    A = {n: nc.dram_tensor(n, a.shape, mybir.dt.from_np(a.dtype), kind="ExternalInput").ap() for n, a in arrays.items()}
    out = nc.dram_tensor("out", (NODES, D), F32, kind="ExternalOutput").ap()
    gnn_kernel(nc, A, out)
    r = run_bass_kernel_spmd(nc, [arrays], core_ids=[0])
    return r.results[0]["out"]


def layout(inputs):
    import numpy as np

    a = {n: np.ascontiguousarray(v) for n, v in inputs.items()}
    pad = NODES + np.arange(EP - EDGES) % (NP - NODES)
    o = {"x": np.concatenate([a["x"], np.zeros((NP - NODES, D), a["x"].dtype)])}
    for n in ("src", "dst"):
        row = np.concatenate([a[n], pad.astype(a[n].dtype)])
        o[n + "_row"] = row
        o[n + "_col"] = np.ascontiguousarray(row.reshape(CHUNKS, P).T)
    ew = np.concatenate([a["edge_weight"], np.zeros(EP - EDGES, a["edge_weight"].dtype)])
    o["ew_col"] = np.ascontiguousarray(ew.reshape(CHUNKS, P).T)
    for n, v in a.items():
        if n[:2] in ("L0", "L1", "L2", "L3"):
            o[n] = v
    def columns(v, n):
        return np.ascontiguousarray(v.reshape(v.shape[:-1] + (n, P)).swapaxes(-1, -2))

    o["L0_gnn_b1"] = columns(a["L0_gnn_b1"], 2)
    o["L2_gnn_conv_b1"] = columns(a["L2_gnn_conv_b1"], 4)
    o["L2_gnn_conv_b2c"] = columns(a["L2_gnn_conv_b2"], 4)
    o["L2_gnn_in_bc"] = columns(a["L2_gnn_in_b"], 4)
    o["L3_gnn_b1"] = columns(a["L3_gnn_b1"], 2)
    o["L3_gnn_b2c"] = columns(a["L3_gnn_b2"].reshape(PF), 2)
    o["L1_gnn_W"] = np.ascontiguousarray(a["L1_gnn_W"].transpose(1, 0, 2).reshape(D, GH))
    o["L2_gnn_in_WT"] = np.ascontiguousarray(a["L2_gnn_in_W"].T)
    o["L2_gnn_conv_W2T"] = np.ascontiguousarray(a["L2_gnn_conv_W2"].transpose(0, 2, 1))
    return o
```

```python
import concourse.bass as bass
from concourse import mybir

F32 = mybir.dt.float32
F16 = mybir.dt.float16
BF16 = mybir.dt.bfloat16
I32 = mybir.dt.int32
ALU = mybir.AluOpType
ACT = mybir.ActivationFunctionType
AX = mybir.AxisListType
MAX_OF_ALL = bass.bass_isa.ReduceOp.max

P = 128
NODES = 3125
TILES = 25
NP = TILES * P
ST = 5
NST = TILES // ST
SW = ST * P
HALF = 3 * P
REST = SW - HALF
D = 256
EDGES = 50000
RING = 4
CHUNKS = 392
CRING = 7
CGROUPS = CHUNKS // CRING
GROUPS = CHUNKS // RING
EP = CHUNKS * P
LAYERS = 3
HEADS, HID = 8, 64
GH = HEADS * HID
GW = GH + HEADS
F2 = 512
KB2 = F2 // P
PH, PO = 4, 64
ATT = 2 * PO + 1
AW = PH * ATT
PF = PH * PO
PW = PF + PH
LN_EPS = 1e-5
ACC_ROWS = NP + P


class Chain:

    def __init__(self, eng, sem):
        self.eng, self.sem, self.n = eng, sem, 0

    def __call__(self, ins):
        self.n += 1
        ins.then_inc(self.sem, 1)
        self.eng.wait_ge(self.sem, self.n)

    def run(self, ins):
        self.n += 1
        ins.then_inc(self.sem, 1)

    def sync(self):
        self.eng.wait_ge(self.sem, self.n)

    def reset(self):
        self.eng.sem_clear(self.sem)
        self.n = 0


def in_turn(eng, body):
    with eng.Fori(0, NST // 2) as it:
        for h in range(2):
            body(2 * it + h, h, it)
    body(NST - 1, 0, NST // 2)


class Semaphores:

    def __init__(self, nc):
        self.nc, self.all = nc, []

    def __call__(self, name):
        self.all.append(self.nc.alloc_semaphore(name))
        return self.all[-1]

    def clear(self):
        self.nc.clear_and_free_semaphores(self.all)
        self.nc.all_engine_barrier(sem_only=True)


def row_bc(ap, parts=P):
    return ap.partition_broadcast(parts)


def gnn_kernel(nc, A, out):
    dram = lambda name, shape, dt: nc.dram_tensor(name, shape, dt, kind="Internal").ap()
    T = {
        "counts": dram("counts", [NP * NP + CRING * P, 1], F16),
        "tab0": dram("tab0", [NP, 2 * D], F16),
        "tab2": dram("tab2", [NP, 2 * F2], F16),
        "gat_src": dram("gat_src", [NP, GW], F32),
        "gat_dst": dram("gat_dst", [NP, 2 * HEADS], F32),
        "gat_at": dram("gat_at", [HEADS, NP], F32),
        "acc1": [dram(f"acc1_{k}", [ACC_ROWS, GW], F32) for k in range(RING)],
        "att_row": dram("att_row", [NP, AW], F32),
        "att_col": dram("att_col", [NP, AW + PF], F32),
        "spill": dram("spill", [EP, PF], F32),
        "acc3": [dram(f"acc3_{k}", [ACC_ROWS, PW], F32) for k in range(RING)],
    }
    sb = lambda name, shape, dt=F32: nc.alloc_sbuf_tensor(name, shape, dt)
    K = {
        "X": sb("X", [P, TILES, D]),
        "I32": sb("ident", [P, P]), "I16": sb("ident16", [P, P], F16),
        "ones": sb("ones", [P, P]), "one16": sb("one16", [P, 1], F16),
        "deg1": sb("deg1", [P, TILES]),
        "early": sb("early", [P, P]), "late": sb("late", [P, P], BF16),
        "trash": sb("trash", [P, CRING]),
        "trash_row": sb("trash_row", [P, 1]),
        "eps": sb("eps", [P, 1]),
        "srci": sb("srci", [P, CHUNKS + 2 * RING], I32), "dsti": sb("dsti", [P, CHUNKS + 2 * RING], I32),
        "srcf": sb("srcf", [P, CHUNKS]), "dstf": sb("dstf", [P, CHUNKS]),
        "keyf": sb("keyf", [P, CHUNKS]),
    }
    PS = [nc.alloc_psum_tensor(f"ps{k}", [P, 1024], F32) for k in range(4)]
    setup(nc, A, T, K)
    if PHASES > 1:
        build_counts(nc, A, T, K, PS)
    if PHASES > 2:
        gin(nc, A, T, K, PS)
    if PHASES > 3:
        gat_nodes(nc, A, T, K, PS)
    if PHASES > 4:
        gat_edges(nc, A, T, K, PS)
    if PHASES > 5:
        gat_out(nc, A, T, K, PS)
    if PHASES > 6:
        deep_gin(nc, A, T, K, PS)
    if PHASES > 7:
        att_nodes(nc, A, T, K, PS)
    if PHASES > 8:
        att_edges(nc, A, T, K, PS)
    if PHASES > 9:
        att_out(nc, A, T, K, PS)
    s = nc.alloc_semaphore("out_done")
    with nc.Block() as block:
        @block.sync
        def _(sp):
            sp.dma_start(out[0:P * (TILES - 1), :].rearrange("(t p) d -> p t d", p=P),
                         K["X"][:, 0:TILES - 1, :]).then_inc(s, 16)
            sp.dma_start(out[P * (TILES - 1):NODES, :], K["X"][0:NODES - P * (TILES - 1), TILES - 1, :]).then_inc(s, 16)
            sp.wait_ge(s, 32)


def setup(nc, A, T, K):
    sem = Semaphores(nc)
    s_in, s_pad, s_zero, s_io = sem("su_in"), sem("su_pad"), sem("su_zero"), sem("su_iota")
    s_z, s_self = sem("su_zeroed"), sem("su_self")
    s_scat = [nc.alloc_semaphore(f"gat_scattered{k}") for k in range(RING)]
    s_scat3 = [nc.alloc_semaphore(f"att_scattered{k}") for k in range(RING)]
    T["scat"], T["scat3"] = s_scat, s_scat3
    with nc.sbuf_tensor("zeros", [P, 26 * 128], F32) as Z, nc.Block() as block:
        @block.vector
        def _(dve):
            ch = Chain(dve, s_self)
            dve.memset(Z[:, :], 0.0).then_inc(s_zero, 1)
            dve.memset(K["ones"][:, :], 1.0)
            dve.memset(K["one16"][:, :], 1.0)
            dve.memset(K["eps"][:, :], LN_EPS)
            dve.memset(K["srci"][:, CHUNKS:], 0)
            dve.memset(K["dsti"][:, CHUNKS:], 0)
            dve.wait_ge(s_in, 16 * 3)
            ch(dve.tensor_copy(K["srcf"][:, :], K["srci"][:, 0:CHUNKS]))
            ch(dve.tensor_copy(K["dstf"][:, :], K["dsti"][:, 0:CHUNKS]))
            dve.scalar_tensor_tensor(out=K["keyf"][:, :], in0=K["srcf"][:, :], scalar=float(NP), in1=K["dstf"][:, :],
                                     op0=ALU.mult, op1=ALU.add)
            dve.wait_ge(s_io, 8)
            dve.tensor_copy(K["I16"][:, :], K["I32"][:, :])

        @block.gpsimd
        def _(pool):
            pool.memset(K["I32"][:, :], 0.0).then_inc(s_io, 1)
            pool.memset(K["early"][:, :], 1.0).then_inc(s_io, 1)
            pool.memset(K["late"][:, :], 1.0).then_inc(s_io, 1)
            pool.iota(K["trash"][:, :], [[P, CRING]], base=NP * NP, channel_multiplier=1,
                      allow_small_or_imprecise_dtypes=True).then_inc(s_io, 1)
            pool.iota(K["trash_row"][:, :], [[0, 1]], base=NP, channel_multiplier=1,
                      allow_small_or_imprecise_dtypes=True).then_inc(s_io, 1)
            pool.wait_ge(s_io, 5)
            pool.affine_select(out=K["I32"][:, :], in_=K["I32"][:, :], compare_op=ALU.not_equal, fill=1.0,
                               base=0, pattern=[[-1, P]], channel_multiplier=1).then_inc(s_io, 1)
            pool.affine_select(out=K["early"][:, :], in_=K["early"][:, :], compare_op=ALU.is_gt, fill=0.0,
                               base=0, pattern=[[-1, P]], channel_multiplier=1).then_inc(s_io, 1)
            pool.affine_select(out=K["late"][:, :], in_=K["late"][:, :], compare_op=ALU.is_gt, fill=0.0,
                               base=0, pattern=[[1, P]], channel_multiplier=-1).then_inc(s_io, 1)
            pool.wait_ge(s_zero, 1)
            for k in range(RING):
                for a in range(2):
                    r = slice(NP + a * P // 2, NP + (a + 1) * P // 2)
                    pool.dma_start(T["acc1"][k][r, :], Z[0:P // 2, 0:GW]).then_inc(s_scat[k], 16)
                    pool.dma_start(T["acc3"][k][r, :], Z[0:P // 2, 0:PW]).then_inc(s_scat3[k], 16)
            for k in range(RING):
                pool.wait_ge(s_scat[k], 32)
                pool.wait_ge(s_scat3[k], 32)

        @block.sync
        def _(sp):
            sp.dma_start(K["srci"][:, 0:CHUNKS], A["src_col"]).then_inc(s_in, 16)
            sp.dma_start(K["dsti"][:, 0:CHUNKS], A["dst_col"]).then_inc(s_in, 16)
            sp.dma_start(K["X"][:, :, :], A["x"].rearrange("(t p) d -> p t d", p=P)).then_inc(s_in, 16)
            sp.wait_ge(s_in, 48)
            sp.wait_ge(s_zero, 1)
            n = 0
            cz = T["counts"][0:NP * NP, :].rearrange("(t p n) a -> t p (n a)", p=P, n=NP)
            zh = Z[:, :].bitcast(F16)
            with sp.Fori(0, TILES) as t:
                sp.dma_start(cz[bass.ds(t, 1), :, :].rearrange("a p n -> (a p) n"), zh[:, 0:NP]).then_inc(s_z, 16)
            n += TILES
            sp.dma_start(T["counts"][NP * NP:, :].rearrange("(p n) a -> p (n a)", p=P), zh[:, 0:CRING]).then_inc(s_z, 16)
            n += 1
            sp.wait_ge(s_z, 16 * n)
    sem.clear()


def build_counts(nc, A, T, K, PS):
    sem = Semaphores(nc)
    s_row, s_idx, s_self = [sem("bc_row0"), sem("bc_row1")], [sem("bc_idx0"), sem("bc_idx1")], sem("bc_self")
    s_rfree, s_sc = [sem("bc_rfree0"), sem("bc_rfree1")], [sem("bc_scat0"), sem("bc_scat1")]
    s_one, s_same, s_sum, s_z = sem("bc_one"), sem("bc_same"), sem("bc_sums"), sem("bc_zeroed")
    GC = CRING * P
    srow = A["src_row"].rearrange("(g n) -> g n", n=GC)
    drow = A["dst_row"].rearrange("(g n) -> g n", n=GC)
    with nc.sbuf_tensor("rows", [P, 2, 2, GC], I32) as R, nc.sbuf_tensor("keyrow", [P, 2, GC], F32) as KR, \
            nc.sbuf_tensor("same", [P, 2, CRING, GC], BF16) as S, nc.sbuf_tensor("own", [P, 2, CRING, P], BF16) as OW, \
            nc.sbuf_tensor("kcol", [P, 2, CRING], F32) as KC, nc.sbuf_tensor("ones16", [P, 1], BF16) as ONE, \
            nc.sbuf_tensor("tmp", [P, 2, CRING], F32) as TM, nc.sbuf_tensor("bc_zeros", [P, ST * GW], F32) as Z, \
            nc.sbuf_tensor("idx", [P, 2, CRING], I32) as IX, nc.sbuf_tensor("val", [P, 2, CRING], F16) as VA, \
            nc.Block() as block:
        @block.sync
        def _(sp):
            with sp.Fori(0, CGROUPS // 2) as it:
                for h in range(2):
                    sp.wait_ge(s_rfree[h], it + 1)
                    sp.dma_start(R[:, h, 0, :], row_bc(srow[bass.ds(2 * it + h, 1), :].rearrange("a n -> (a n)"))).then_inc(s_row[h], 16)
                    sp.dma_start(R[:, h, 1, :], row_bc(drow[bass.ds(2 * it + h, 1), :].rearrange("a n -> (a n)"))).then_inc(s_row[h], 16)

        @block.scalar
        def _(act):
            act.wait_ge(s_one, 1)
            n = 0
            for k in range(RING):
                for acc, w in ((T["acc1"][k], GW), (T["acc3"][k], PW)):
                    for t in range(0, TILES, ST):
                        act.dma_start(acc[t * P:(t + ST) * P, :].rearrange("(t p) w -> p t w", p=P),
                                      Z[:, 0:ST * w].rearrange("p (t w) -> p t w", t=ST)).then_inc(s_z, 16)
                        n += 1
            act.wait_ge(s_z, 16 * n)

        @block.vector
        def _(dve):
            ch = Chain(dve, s_self)
            for h in range(2):
                dve.sem_inc(s_rfree[h], 1)
            ch(dve.memset(ONE[:, :], 1.0))
            dve.memset(Z[:, :], 0.0).then_inc(s_one, 1)
            ch.reset()
            with dve.Fori(0, CGROUPS // 2) as it:
                for h in range(2):
                    dve.wait_ge(s_row[h], 32 * (it + 1))
                    ch.run(dve.scalar_tensor_tensor(out=KR[:, h, :], in0=R[:, h, 0, :], scalar=float(NP), in1=R[:, h, 1, :],
                                                    op0=ALU.mult, op1=ALU.add))
                    ch.run(dve.tensor_copy(KC[:, h, :], K["keyf"][:, bass.ds((2 * it + h) * CRING, CRING)]))
                    ch.sync()
                    dve.sem_inc(s_rfree[h], 1)
                    for k in range(CRING):
                        ch.run(dve.tensor_scalar(S[:, h, k, :], KR[:, h, :], KC[:, h, k:k + 1], None, ALU.is_equal))
                    ch.sync()
                    own = S[:, h, :, :].rearrange("p k (c x) -> p (k c) x", x=P)[:, 0:CRING * CRING:CRING + 1, :]
                    ch(dve.tensor_tensor(OW[:, h, :, :], own, K["late"][:, :].unsqueeze(1).broadcast_to([P, CRING, P]), ALU.mult))
                    dve.sem_inc(s_same, 1)
                    ch(dve.tensor_tensor(TM[:, h, :], K["trash"][:, :], KC[:, h, :], ALU.subtract))
                    dve.wait_ge(s_sc[h], 16 * (CRING * it + 1))
                    dve.wait_ge(s_sum, 2 * it + h + 1)
                    ch.run(dve.tensor_copy(VA[:, h, :], PS[h][:, 0:CRING]))
                    ch(dve.scalar_tensor_tensor(out=TM[:, h, :], in0=PS[h][:, CRING:2 * CRING], scalar=1.0, in1=TM[:, h, :],
                                                op0=ALU.min, op1=ALU.mult))
                    ch(dve.tensor_tensor(IX[:, h, :], TM[:, h, :], KC[:, h, :], ALU.add))
                    dve.sem_inc(s_idx[h], 1)
                ch.reset()

        @block.tensor
        def _(pe):
            with pe.Fori(0, CGROUPS // 2) as it:
                for h in range(2):
                    pe.wait_ge(s_same, 2 * it + h + 1)
                    for k in range(CRING):
                        for c in range(CRING):
                            pe.matmul(PS[h][:, k:k + 1], S[:, h, c, k * P:(k + 1) * P], ONE[:, :], start=c == 0, stop=c == CRING - 1)
                        for c in range(k):
                            pe.matmul(PS[h][:, CRING + k:CRING + k + 1], S[:, h, c, k * P:(k + 1) * P], ONE[:, :], start=c == 0, stop=False)
                        m = pe.matmul(PS[h][:, CRING + k:CRING + k + 1], OW[:, h, k, :], ONE[:, :], start=k == 0, stop=True)
                    m.then_inc(s_sum, 1)

        @block.gpsimd
        def _(pool):
            for h in range(2):
                pool.dma_start(IX[:, h, :], A["src_col"][:, 0:CRING]).then_inc(s_sc[h], 16)
            for h in range(2):
                pool.wait_ge(s_sc[h], 16)
            with pool.Fori(0, CGROUPS // 2) as it:
                for h in range(2):
                    pool.wait_ge(s_idx[h], it + 1)
                    pool.wait_ge(s_sc[1 - h], 16 * (CRING * (it + h) + 1))
                    pool.sem_inc(s_one, 1)
                    for k in range(CRING):
                        pool.indirect_dma_start(
                            out=T["counts"], out_offset=bass.IndirectOffsetOnAxis(ap=IX[:, h, k:k + 1], axis=0),
                            in_=VA[:, h, k:k + 1], in_offset=None, compute_op=ALU.add).then_inc(s_sc[h], 16)
            for h in range(2):
                pool.wait_ge(s_sc[h], 16 * (CRING * (CGROUPS // 2) + 1))
    sem.clear()


def split16(ch, dve, x, hi, lo):
    ch(dve.tensor_copy(hi, x))
    ch(dve.tensor_tensor(lo, x, hi, ALU.subtract))


def norm_stats(ch, dve, x, stats, mv, n):
    for i in range(n):
        ch.run(dve.bn_stats(stats[:, i, :], x[:, i, :]))
    ch.sync()
    for i in range(n):
        ch.run(dve.bn_aggr(mv[:, i, :], stats[:, i, :]))
    ch.sync()


def final_norm(nc, K, name, add, width=ST):
    sem = Semaphores(nc)
    s_self, s_mv, s_sd = (sem(f"{name}_{x}") for x in ("self", "var", "sd"))
    s_rs, s_act = sem(f"{name}_rs"), sem(f"{name}_act")
    X = K["X"]
    with nc.sbuf_tensor(name + "_st", [P, TILES, 6], F32) as S, nc.sbuf_tensor(name + "_mv", [P, TILES, 2], F32) as MV, \
            nc.sbuf_tensor(name + "_sd", [P, TILES], F32) as SD, nc.sbuf_tensor(name + "_rs", [P, TILES], F32) as RS, \
            nc.sbuf_tensor(name + "_mr", [P, TILES], F32) as MR, nc.Block() as block:
        @block.vector
        def _(dve):
            ch = Chain(dve, s_self)
            if add is not None:
                for a in range(0, TILES, ST):
                    ch.run(dve.tensor_tensor(X[:, a:a + ST, :], X[:, a:a + ST, :], add[:, a:a + ST, :], ALU.add))
                ch.sync()
            for i in range(TILES):
                ch.run(dve.bn_stats(S[:, i, :], X[:, i, :]))
            ch.sync()
            for i in range(TILES):
                dve.bn_aggr(MV[:, i, :], S[:, i, :]).then_inc(s_mv, 1)
            dve.wait_ge(s_sd, 1)
            ch(dve.reciprocal(RS[:, :], SD[:, :]))
            ch(dve.scalar_tensor_tensor(out=MR[:, :], in0=MV[:, :, 0], scalar=-1.0, in1=RS[:, :], op0=ALU.mult, op1=ALU.mult))
            dve.sem_inc(s_rs, 1)
            for i in range(0, TILES, 2):
                dve.tensor_scalar(X[:, i, :], X[:, i, :], RS[:, i:i + 1], MR[:, i:i + 1], ALU.mult, ALU.add)

        @block.scalar
        def _(act):
            act.wait_ge(s_mv, TILES)
            act.activation(SD[:, :], MV[:, :, 1], ACT.Sqrt, bias=K["eps"][:, 0:1]).then_inc(s_sd, 1)
            act.wait_ge(s_rs, 1)
            for i in range(1, TILES, 2):
                act.activation(X[:, i, :], X[:, i, :], ACT.Identity, scale=RS[:, i:i + 1], bias=MR[:, i:i + 1])
    sem.clear()


def load_counts(sp, T, C, s_in, s_out, j, round_):
    view = T["counts"][0:NP * NP, :].rearrange("(k s p t c) a -> k t p s (c a)", k=ST, s=ST, p=P, c=SW)
    for q in range(ST):
        sp.wait_ge(s_out[q], round_ + 1)
        sp.dma_start(C[:, q, :, :], view[q, bass.ds(j, 1), :, :, :].rearrange("a p s c -> (a p) s c")).then_inc(s_in[q], 16)


def neighbour_sum(pe, TAB, C, ps, fb, width, s_in, s_out, round_, last, own, ready=None):
    for s in range(TILES):
        q = s // ST
        if fb == 0 and s % ST == 0:
            pe.wait_ge(s_in[q], 16 * (round_ + 1))
            if ready:
                ready(q)
        for part in range(2):
            w = TAB[:, s, part * width + fb * P:part * width + (fb + 1) * P]
            first, end = s == 0 and part == 0, s == TILES - 1 and part == 1
            pe.matmul(ps[:, 0:HALF], w, C[:, q, s % ST, 0:HALF], start=first, stop=end, skip_group_check=True)
            m = pe.matmul(ps[:, 512:512 + REST], w, C[:, q, s % ST, HALF:SW], start=first, stop=end, skip_group_check=True)
        if last and s % ST == ST - 1 and q < ST - 1:
            m.then_inc(s_out[q], 1)
        if s == ST:
            own()
    return m


def cols(i):
    return slice(i * P, (i + 1) * P) if i < 3 else slice(512 + (i - 3) * P, 512 + (i - 2) * P)


HALVES = ((slice(0, HALF), slice(0, HALF)), (slice(512, 512 + REST), slice(HALF, SW)))


def gin(nc, A, T, K, PS):
    sem = Semaphores(nc)
    n_ = lambda x: sem("gin_" + x)
    s_tab, s_w, s_self, s_layer, s_taken = n_("tab"), n_("weights_in"), n_("self"), n_("layer"), n_("taken")
    s_own, s_zt, s_ut = n_("own"), n_("zt"), n_("ut")
    s_mv, s_sd, s_h = n_("var"), n_("sd"), n_("h")
    s_cin, s_cout = [n_(f"c_in{q}") for q in range(ST)], [n_(f"c_out{q}") for q in range(ST)]
    s_full, s_free = [n_(f"full{k}") for k in range(4)], [n_(f"free{k}") for k in range(4)]
    X = K["X"]
    NW = 7

    def second(i):
        return (2, 4, 1 + i // 2) if i % 2 == 0 else (3, 3, 1 + i // 2)

    with nc.sbuf_tensor("gin_h", [P, TILES, D], F32) as H:
        with nc.sbuf_tensor("gin_tab", [P, TILES, 2 * D], F16) as TAB, \
                nc.sbuf_tensor("gin_next", [P, TILES, 2 * D], F16) as NEXT, \
                nc.sbuf_tensor("gin_c", [P, ST, ST, SW], F16) as C, \
                nc.sbuf_tensor("gin_w1", [P, 2, D], F32) as W1, nc.sbuf_tensor("gin_w2", [P, 2, D], F32) as W2, \
                nc.sbuf_tensor("gin_b1", [P, 2], F32) as B1, nc.sbuf_tensor("gin_rows", [P, 3, D], F32) as RW, \
                nc.sbuf_tensor("gin_eps", [P, 1], F32) as EPS, nc.sbuf_tensor("gin_eps1", [P, 1], F32) as EPS1, \
                nc.sbuf_tensor("gin_own", [P, ST, D], F32) as OWN, nc.sbuf_tensor("gin_hb", [P, ST, D], F32) as HB, \
                nc.sbuf_tensor("gin_r", [P, ST, D], F32) as R, \
                nc.sbuf_tensor("gin_zt", [P, 2, SW], F32) as ZT, nc.sbuf_tensor("gin_ut", [P, 2, SW], F32) as UT, \
                nc.sbuf_tensor("gin_st", [P, ST, 6], F32) as S, nc.sbuf_tensor("gin_mv", [P, ST, 2], F32) as MV, \
                nc.sbuf_tensor("gin_sd", [P, ST], F32) as SD, nc.sbuf_tensor("gin_rs", [P, ST], F32) as RS, \
                nc.Block() as block:
            @block.sync
            def _(sp):
                with sp.Fori(0, LAYERS) as l:
                    with sp.Fori(0, NST) as j:
                        load_counts(sp, T, C, s_cin, s_cout, j, l * NST + j)

            @block.gpsimd
            def _(pool):
                with pool.Fori(0, LAYERS) as l:
                    pool.wait_ge(s_layer, l + 1)
                    pool.sem_inc(s_taken, 1)
                    one = bass.ds(l, 1)
                    pool.dma_start(EPS[:, :], row_bc(A["L0_gnn_eps"][one])).then_inc(s_w, 16)
                    for dst, name in ((W1, "L0_gnn_W1"), (W2, "L0_gnn_W2")):
                        pool.dma_start(dst[:, :, :], A[name][one, :, :].rearrange("a (k p) n -> p (a k) n", p=P)).then_inc(s_w, 16)
                    pool.dma_start(B1[:, :], A["L0_gnn_b1"][one, :, :].rearrange("a p k -> (a p) k")).then_inc(s_w, 16)
                    for n, name in enumerate(("L0_gnn_b2", "L0_gnn_gamma", "L0_gnn_beta")):
                        pool.dma_start(RW[:, n, :], row_bc(A[name][one, :].rearrange("a n -> (a n)"))).then_inc(s_w, 16)
                pool.wait_ge(s_w, 16 * NW * LAYERS)

            @block.vector
            def _(dve):
                ch = Chain(dve, s_self)

                def own(j):
                    ch(dve.tensor_scalar(OWN[:, :, :], H[:, bass.ds(j * ST, ST), :], EPS1[:, 0:1], None, ALU.mult))
                    dve.sem_inc(s_own, 1)

                def rest(j, g):
                    tiles = bass.ds(j * ST, ST)
                    mine = H[:, tiles, :]
                    ch(dve.tensor_tensor(HB[:, :, :], mine, RW[:, 0:1, :].broadcast_to([P, ST, D]), ALU.add))
                    for i in range(ST):
                        k, per, nth = second(i)
                        dve.wait_ge(s_full[k], per * g + nth + 1)
                        ch(dve.tensor_tensor(R[:, i, :], HB[:, i, :], PS[k][:, 0:D], ALU.add))
                        dve.sem_inc(s_free[k], 1)
                    norm_stats(ch, dve, R, S, MV, ST)
                    dve.sem_inc(s_mv, 1)
                    dve.wait_ge(s_sd, g + 1)
                    ch(dve.reciprocal(RS[:, :], SD[:, :]))
                    for i in range(ST):
                        ch.run(dve.tensor_scalar(R[:, i, :], R[:, i, :], MV[:, i, 0:1], RS[:, i:i + 1], ALU.subtract, ALU.mult))
                    ch.sync()
                    ch(dve.tensor_tensor(R[:, :, :], R[:, :, :], RW[:, 1:2, :].broadcast_to([P, ST, D]), ALU.mult))
                    ch(dve.tensor_tensor(R[:, :, :], R[:, :, :], RW[:, 2:3, :].broadcast_to([P, ST, D]), ALU.add))
                    ch(dve.tensor_scalar(R[:, :, :], R[:, :, :], 0.0, None, ALU.max))
                    ch.run(dve.tensor_copy(mine, R[:, :, :]))
                    split16(ch, dve, R[:, :, :], NEXT[:, tiles, 0:D], NEXT[:, tiles, D:])

                dve.sem_inc(s_layer, 1)
                split16(ch, dve, X[:, :, :], NEXT[:, :, 0:D], NEXT[:, :, D:])
                dve.wait_ge(s_h, 1)
                ch.reset()
                with dve.Fori(0, LAYERS) as l:
                    for q in range(ST):
                        ch(dve.tensor_copy(TAB[:, q * ST:(q + 1) * ST, :], NEXT[:, q * ST:(q + 1) * ST, :]))
                        dve.sem_inc(s_tab, 1)
                    dve.wait_ge(s_w, 16 * NW * (l + 1))
                    dve.sem_inc(s_taken, 1)
                    ch(dve.tensor_scalar(EPS1[:, :], EPS[:, :], 1.0, None, ALU.add))
                    own(0)
                    dve.wait_ge(s_full[1], l * NST + 1)
                    dve.sem_inc(s_taken, 1)
                    own(1)
                    ch.reset()
                    with dve.Fori(0, NST - 2) as j:
                        g = l * NST + j
                        dve.wait_ge(s_full[1], g + 2)
                        dve.sem_inc(s_taken, 1)
                        own(j + 2)
                        rest(j, g)
                        ch.reset()
                    for j in (NST - 2, NST - 1):
                        rest(j, l * NST + j)
                    dve.sem_inc(s_layer, 1)
                    ch.reset()

            @block.scalar
            def _(act):
                for q in range(ST):
                    act.sem_inc(s_cout[q], 1)
                for k in range(4):
                    act.sem_inc(s_free[k], 1)

                act.activation(H[:, :, :], X[:, :, :], ACT.Copy).then_inc(s_h, 1)

                def sums(g):
                    for fb in range(2):
                        act.wait_ge(s_full[fb], g + 1)
                        if fb == 1:
                            act.sem_inc(s_cout[ST - 1], 1)
                        for a, b in HALVES:
                            act.activation(ZT[:, fb, b], PS[fb][:, a], ACT.Copy).then_inc(s_zt, 1)
                        act.wait_ge(s_zt, 4 * g + 2 * fb + 2)
                        act.sem_inc(s_free[fb], 1)

                def hidden(g):
                    for hb in range(2):
                        k = 2 + hb
                        act.wait_ge(s_full[k], (4 - hb) * g + 1)
                        for a, b in HALVES:
                            act.activation(UT[:, hb, b], PS[k][:, a], ACT.Relu, bias=B1[:, hb:hb + 1]).then_inc(s_ut, 1)
                        act.wait_ge(s_ut, 4 * g + 2 * hb + 2)
                        act.sem_inc(s_free[k], 1)

                def roots(g):
                    act.wait_ge(s_mv, g + 1)
                    act.activation(SD[:, :], MV[:, :, 1], ACT.Sqrt, bias=K["eps"][:, 0:1]).then_inc(s_sd, 1)

                with act.Fori(0, LAYERS) as l:
                    sums(l * NST)
                    act.wait_ge(s_w, 16 * NW * (l + 1))
                    act.sem_inc(s_taken, 1)
                    with act.Fori(0, NST - 2) as j:
                        g = l * NST + j
                        hidden(g)
                        sums(g + 1)
                        roots(g)
                    g = l * NST + NST - 2
                    hidden(g)
                    sums(g + 1)
                    hidden(g + 1)
                    roots(g)
                    roots(g + 1)

            @block.tensor
            def _(pe):
                def sums(l, g, fb):
                    def own():
                        if fb == 0:
                            pe.wait_ge(s_own, g + 1)
                        for i in range(ST):
                            pe.matmul(PS[fb][:, cols(i)], OWN[:, i, fb * P:(fb + 1) * P], K["I32"][:, :],
                                      start=False, stop=False, skip_group_check=True)

                    def ready(q):
                        pe.wait_ge(s_tab, ST * l + q + 1)
                    pe.wait_ge(s_free[fb], g + 1)
                    neighbour_sum(pe, TAB, C, PS[fb], fb, D, s_cin, s_cout, g, fb == 1, own, ready).then_inc(s_full[fb], 1)

                def first(g):
                    pe.wait_ge(s_zt, 4 * g + 4)
                    for hb in range(2):
                        pe.wait_ge(s_free[2 + hb], (4 - hb) * g + 1)
                        for a, b in HALVES:
                            for kb in range(2):
                                m = pe.matmul(PS[2 + hb][:, a], W1[:, kb, hb * P:(hb + 1) * P], ZT[:, kb, b],
                                              start=kb == 0, stop=kb == 1)
                        m.then_inc(s_full[2 + hb], 1)

                def last(g):
                    pe.wait_ge(s_ut, 4 * g + 4)
                    for i in range(ST):
                        k, per, nth = second(i)
                        pe.wait_ge(s_free[k], per * g + nth + 1)
                        for kb in range(2):
                            m = pe.matmul(PS[k][:, 0:D], UT[:, kb, i * P:(i + 1) * P], W2[:, kb, :], start=kb == 0, stop=kb == 1)
                        m.then_inc(s_full[k], 1)

                with pe.Fori(0, LAYERS) as l:
                    for fb in range(2):
                        sums(l, l * NST, fb)
                    pe.wait_ge(s_w, 16 * NW * (l + 1))
                    pe.sem_inc(s_taken, 1)
                    with pe.Fori(0, NST - 1) as j:
                        g = l * NST + j
                        sums(l, g + 1, 0)
                        first(g)
                        sums(l, g + 1, 1)
                        last(g)
                    first(l * NST + NST - 1)
                    last(l * NST + NST - 1)
        final_norm(nc, K, "gin_ln", H)
    sem.clear()


def transposed(pe, ident, ps, src, n, col):
    for i in range(n):
        m = pe.transpose(ps[:, cols(i)], src[:, i, col:col + P], ident)
    return m


def gat_nodes(nc, A, T, K, PS):
    sem = Semaphores(nc)
    n_ = lambda x: sem("gn_" + x)
    s_w, s_self, s_taken, s_taken2, s_xs, s_xt, s_row, s_wa, s_dst, s_dfree = (n_(x) for x in (
        "w", "self", "taken", "taken2", "xs", "xt", "row", "wa", "dst", "dst_free"))
    s_as, s_as2, s_out, s_aout = n_("as"), n_("as_half"), n_("row_out"), n_("at_out")
    s_full, s_free = [n_(f"full{k}") for k in range(4)], [n_(f"free{k}") for k in range(4)]
    with nc.sbuf_tensor("gn_bm", [P, TILES, 2 * HEADS], F32) as BM:
        with nc.sbuf_tensor("gn_w", [P, 2, GH], F32) as W, nc.sbuf_tensor("gn_a", [P, HEADS, 2, HID], F32) as AV, \
                nc.sbuf_tensor("gn_xs", [P, ST, D], F32) as XS, nc.sbuf_tensor("gn_xt", [P, 2, SW], F32) as XT, \
                nc.sbuf_tensor("gn_row", [P, 2, ST, GW], F32) as ROW, nc.sbuf_tensor("gn_p", [P, 2, 2, HEADS, HID], F32) as PR, \
                nc.sbuf_tensor("gn_wa", [P, 2, 2 * HEADS], F32) as WA, nc.sbuf_tensor("gn_ds", [P, ST, HEADS], F32) as DS, \
                nc.sbuf_tensor("gn_as", [HEADS, 2, SW], F32) as AS, nc.Block() as block:
            @block.sync
            def _(sp):
                sp.dma_start(W[:, :, :], A["L1_gnn_W"].rearrange("(k p) n -> p k n", p=P)).then_inc(s_w, 16)
                sp.dma_start(AV[:, :, :, :].rearrange("p h s o -> p (h s o)"),
                             row_bc(A["L1_gnn_a"].rearrange("h o -> (h o)"))).then_inc(s_w, 16)
                rows = T["gat_src"].rearrange("(j t p) w -> j p t w", t=ST, p=P)

                def store(j, h, turn):
                    sp.wait_ge(s_as, j + 1)
                    sp.dma_start(rows[bass.ds(j, 1), :, :, :].rearrange("a p t w -> (a p) t w"), ROW[:, h, :, :]).then_inc(s_out, 16)
                    sp.dma_start(T["gat_at"][:, bass.ds(j * SW, SW)], AS[:, h, :]).then_inc(s_out, 16)
                    sp.wait_ge(s_out, 32 * (j + 1))
                    sp.sem_inc(s_aout, 1)
                in_turn(sp, store)

            @block.vector
            def _(dve):
                ch = Chain(dve, s_self)
                dve.sem_inc(s_dfree, 1)
                ch(dve.tensor_copy(XS[:, :, :], K["X"][:, 0:ST, :]))
                dve.sem_inc(s_xs, 1)
                dve.wait_ge(s_w, 32)
                for kb in range(2):
                    for side in range(2):
                        ch.run(dve.tensor_tensor(PR[:, kb, side, :, :], W[:, kb, :].rearrange("p (h o) -> p h o", h=HEADS),
                                                 AV[:, :, side, :], ALU.mult))
                ch.sync()
                for kb in range(2):
                    for side in range(2):
                        ch.run(dve.tensor_reduce(WA[:, kb, side * HEADS:(side + 1) * HEADS], PR[:, kb, side, :, :], AX.X, ALU.add))
                ch.sync()
                dve.sem_inc(s_wa, 1)
                ch.reset()
                with dve.Fori(0, NST - 1) as j:
                    dve.wait_ge(s_full[1], j + 1)
                    ch(dve.tensor_copy(XS[:, :, :], K["X"][:, bass.ds((j + 1) * ST, ST), :]))
                    dve.sem_inc(s_xs, 1)
                    dve.wait_ge(s_dst, j + 1)
                    dve.sem_inc(s_taken2, 1)
                    ch(dve.tensor_copy(BM[:, bass.ds(j * ST, ST), 0:HEADS], DS[:, :, :]))
                    dve.sem_inc(s_dfree, 1)
                    ch.reset()
                dve.wait_ge(s_dst, NST)
                dve.tensor_copy(BM[:, (NST - 1) * ST:, 0:HEADS], DS[:, :, :])

            @block.scalar
            def _(act):
                for k in range(4):
                    act.sem_inc(s_free[k], 1)
                act.sem_inc(s_aout, 2)

                def copies(j, h, turn):
                    for kb in range(2):
                        act.wait_ge(s_full[kb], (2 - kb) * j + 1)
                        for a, b in HALVES:
                            act.activation(XT[:, kb, b], PS[kb][:, a], ACT.Copy).then_inc(s_xt, 1)
                        act.wait_ge(s_xt, 4 * j + 2 * kb + 2)
                        act.sem_inc(s_free[kb], 1)
                    act.wait_ge(s_aout, j + 1)
                    act.wait_ge(s_dfree, j + 1)
                    act.sem_inc(s_taken, 1)
                    for i in range(ST):
                        k, per, nth = 2 + i % 2, 3 - i % 2, i // 2
                        act.wait_ge(s_full[k], per * j + nth + 1)
                        act.activation(ROW[:, h, i, 0:GH], PS[k][:, 0:GH], ACT.Copy).then_inc(s_row, 1)
                        act.activation(ROW[:, h, i, GH:], PS[k][:, 512:512 + HEADS], ACT.Copy).then_inc(s_row, 1)
                        act.activation(DS[:, i, :], PS[k][:, 512 + HEADS:512 + 2 * HEADS], ACT.Copy).then_inc(s_row, 1)
                        act.wait_ge(s_row, 3 * (ST * j + i + 1))
                        act.sem_inc(s_free[k], 1)
                    act.sem_inc(s_dst, 1)
                    act.wait_ge(s_full[0], 2 * j + 2)
                    for a, b in HALVES:
                        act.activation(AS[:, h, b], PS[0][0:HEADS, a], ACT.Copy).then_inc(s_as2, 1)
                    act.wait_ge(s_as2, 2 * j + 2)
                    act.sem_inc(s_free[0], 1)
                    act.sem_inc(s_as, 1)
                in_turn(act, copies)

            @block.tensor
            def _(pe):
                def rows(j):
                    pe.wait_ge(s_xs, j + 1)
                    for kb in range(2):
                        pe.wait_ge(s_free[kb], (2 - kb) * j + 1)
                        transposed(pe, K["I32"][:, :], PS[kb], XS, ST, kb * P).then_inc(s_full[kb], 1)

                def product(j):
                    pe.wait_ge(s_xt, 4 * j + 4)
                    for i in range(ST):
                        k, per, nth = 2 + i % 2, 3 - i % 2, i // 2
                        pe.wait_ge(s_free[k], per * j + nth + 1)
                        for kb in range(2):
                            pe.matmul(PS[k][:, 0:GH], XT[:, kb, i * P:(i + 1) * P], W[:, kb, :], start=kb == 0, stop=kb == 1)
                        for kb in range(2):
                            m = pe.matmul(PS[k][:, 512:512 + 2 * HEADS], XT[:, kb, i * P:(i + 1) * P], WA[:, kb, :],
                                          start=kb == 0, stop=kb == 1)
                        m.then_inc(s_full[k], 1)
                    pe.wait_ge(s_free[0], 2 * j + 2)
                    for a, b in HALVES:
                        for kb in range(2):
                            m = pe.matmul(PS[0][0:HEADS, a], WA[:, kb, 0:HEADS], XT[:, kb, b], start=kb == 0, stop=kb == 1)
                    m.then_inc(s_full[0], 1)

                rows(0)
                pe.wait_ge(s_wa, 1)
                with pe.Fori(0, NST - 1) as j:
                    product(j)
                    rows(j + 1)
                product(NST - 1)

        n_ = lambda x: sem("gm_" + x)
        s_c, s_cf, s_ps, s_psf, s_self, s_bm, s_bo, s_taken = (n_(x) for x in (
            "c_in", "c_free", "ps", "ps_free", "self", "bm", "bm_out", "taken"))
        NEG = -1e30
        s_ab = [n_(f"scores_in{h}") for h in range(HEADS)]
        with nc.sbuf_tensor("gm_ab", [P, HEADS, NP], F32) as AB, nc.sbuf_tensor("gm_c", [P, TILES, P], F16) as C, \
                nc.sbuf_tensor("gm_mask", [P, NP], BF16) as MK, nc.sbuf_tensor("gm_junk", [P, NP], BF16) as J, \
                nc.sbuf_tensor("gm_am", [P, HEADS], F32) as AM, nc.sbuf_tensor("gm_t", [P, TILES, HEADS], F32) as TM, \
                nc.Block() as block:
            @block.sync
            def _(sp):
                for h in range(HEADS):
                    sp.dma_start(AB[:, h, :], row_bc(T["gat_at"][h, :])).then_inc(s_ab[h], 16)
                sp.wait_ge(s_bm, 1)
                sp.dma_start(T["gat_dst"].rearrange("(t p) w -> p t w", p=P), BM[:, :, :]).then_inc(s_bo, 16)
                sp.wait_ge(s_bo, 16)

            @block.scalar
            def _(act):
                cv = T["counts"][0:NP * NP, :].rearrange("(s p t c) a -> t p s (c a)", s=TILES, p=P, c=P)
                with act.Fori(0, TILES) as t:
                    act.wait_ge(s_cf, t + 1)
                    act.dma_start(C[:, :, :], cv[bass.ds(t, 1), :, :, :].rearrange("a p s c -> (a p) s c")).then_inc(s_c, 16)

            @block.tensor
            def _(pe):
                pe.sem_inc(s_cf, 1)
                pe.sem_inc(s_psf, 1)
                with pe.Fori(0, TILES) as t:
                    pe.wait_ge(s_c, 16 * (t + 1))
                    pe.wait_ge(s_psf, t + 1)
                    pe.sem_inc(s_taken, 1)
                    for s in range(TILES):
                        o = PS[s // 16][:, :].bitcast(F16)[:, (s % 16) * P:(s % 16 + 1) * P]
                        pe.transpose(o, C[:, s, :], K["I16"][:, :])
                    for s in range(TILES):
                        m = pe.matmul(PS[2][:, 0:1], C[:, s, :], K["one16"][:, :], start=s == 0, stop=s == TILES - 1)
                    m.then_inc(s_ps, 1)
                    pe.wait_ge(s_ps, t + 1)
                    pe.sem_inc(s_cf, 1)

            @block.vector
            def _(dve):
                ch = Chain(dve, s_self)
                with dve.Fori(0, TILES) as t:
                    dve.wait_ge(s_ps, t + 1)
                    ch(dve.tensor_scalar(MK[:, 0:16 * P], PS[0][:, :].bitcast(F16), 0.0, NEG, ALU.is_equal, ALU.mult))
                    ch.run(dve.tensor_copy(K["deg1"][:, bass.ds(t, 1)], PS[2][:, 0:1]))
                    ch(dve.tensor_scalar(MK[:, 16 * P:], PS[1][:, :].bitcast(F16)[:, 0:NP - 16 * P], 0.0, NEG, ALU.is_equal, ALU.mult))
                    dve.sem_inc(s_psf, 1)
                    for h in range(HEADS):
                        dve.wait_ge(s_ab[h], 16)
                        ch(dve.tensor_tensor_reduce(out=J[:, :], in0=MK[:, :], in1=AB[:, h, :], scale=1.0, scalar=NEG,
                                                    op0=ALU.add, op1=ALU.max, accum_out=AM[:, h:h + 1]))
                    ch(dve.tensor_copy(BM[:, bass.ds(t, 1), HEADS:], AM[:, :].unsqueeze(1)))
                    ch.reset()
                ch(dve.tensor_scalar(K["deg1"][:, :], K["deg1"][:, :], 1.0, None, ALU.add))
                ch(dve.tensor_tensor(TM[:, :, :], BM[:, :, 0:HEADS], BM[:, :, HEADS:], ALU.add))
                ch(dve.scalar_tensor_tensor(out=BM[:, :, HEADS:], in0=TM[:, :, :], scalar=0.2, in1=TM[:, :, :], op0=ALU.mult, op1=ALU.max))
                dve.sem_inc(s_bm, 1)
    sem.clear()


def same_targets(dve, ch, K, rows, tg, S, J, EC):
    ch.run(dve.tensor_tensor(S, rows, tg.unsqueeze(2).broadcast_to([P, RING, P]), ALU.is_equal))
    ch.run(dve.tensor_tensor(EC[:, 1, :], K["trash_row"][:, :].broadcast_to([P, RING]), tg, ALU.subtract))
    ch.sync()
    ch(dve.tensor_tensor(J, S, K["early"][:, :].unsqueeze(1).broadcast_to([P, RING, P]), ALU.mult))
    ch(dve.tensor_reduce(EC[:, 0, :], J, AX.X, ALU.add))
    ch(dve.scalar_tensor_tensor(out=EC[:, 2, :], in0=EC[:, 0, :], scalar=1.0, in1=EC[:, 1, :], op0=ALU.min, op1=ALU.mult))


def target_index(dve, ch, tg, EC, index, s_scattered, n):
    for k in range(RING):
        dve.wait_ge(s_scattered[k], 16 * (n + 1))
    ch(dve.tensor_tensor(index, EC[:, 2, :], tg, ALU.add))


def merge_group(pe, n, S, M, PS, width, s_m, s_copied, s_merged):
    for k in range(RING):
        pe.wait_ge(s_m, RING * (n - 1) + k + 1)
        pe.wait_ge(s_copied, RING * n + k + 1)
        m = pe.matmul(PS[k][:, 0:min(width, 512)], S[:, k, :], M[:, k, 0:min(width, 512)], start=True, stop=True)
        if width > 512:
            m = pe.matmul(PS[k][:, 512:width], S[:, k, :], M[:, k, 512:width], start=True, stop=True)
        m.then_inc(s_merged, 1)


def gat_edges(nc, A, T, K, PS):
    sem = Semaphores(nc)
    ks = range(RING)
    n_ = lambda x: [sem(f"ge_{x}{h}") for h in range(2)]
    s_g, s_id, s_used, s_rin, s_rf, s_o = (n_(x) for x in ("in", "ids", "used", "targets_in", "targets_free", "rows"))
    s_sc = T["scat"]
    s_self, s_taken, s_taken2, s_e, s_x, s_m, s_mg, s_cp, s_cph = (sem("ge_" + x) for x in (
        "self", "taken", "taken2", "scores", "exp", "msg", "merged", "copied", "half"))
    drow = A["dst_row"].rearrange("(g n) -> g n", n=RING * P)
    with nc.sbuf_tensor("ge_g", [P, 2, RING, GW], F32) as G, nc.sbuf_tensor("ge_h", [P, 2, RING, 2 * HEADS], F32) as H, \
            nc.sbuf_tensor("ge_m", [P, 2, RING, GW], F32) as M, nc.sbuf_tensor("ge_o", [P, 2, RING, GW], F32) as O, \
            nc.sbuf_tensor("ge_s", [P, 2, RING, P], F32) as S, nc.sbuf_tensor("ge_j", [P, RING, P], F32) as J, \
            nc.sbuf_tensor("ge_r", [P, 2, RING * P], I32) as R, nc.sbuf_tensor("ge_id", [P, 2, 2, RING], I32) as ID, \
            nc.sbuf_tensor("ge_e", [P, 2, 3, RING, HEADS], F32) as E, nc.sbuf_tensor("ge_tg", [P, 2, RING], F32) as TG, \
            nc.sbuf_tensor("ge_c", [P, 3, RING], F32) as EC, nc.sbuf_tensor("ge_ix", [P, 2, RING], I32) as IX, \
            nc.Block() as block:
        @block.sync
        def _(sp):
            with sp.Fori(0, GROUPS // 2) as it:
                for h in range(2):
                    sp.wait_ge(s_rf[h], it + 1)
                    sp.dma_start(R[:, h, :], row_bc(drow[bass.ds(2 * it + h, 1), :].rearrange("a n -> (a n)"))).then_inc(s_rin[h], 16)

        @block.gpsimd
        def _(pool):
            def gather(h, k):
                pool.indirect_dma_start(out=G[:, h, k, :], out_offset=None, in_=T["gat_src"],
                                        in_offset=bass.IndirectOffsetOnAxis(ap=ID[:, h, 0, k:k + 1], axis=0)).then_inc(s_g[h], 16)
                pool.indirect_dma_start(out=H[:, h, k, :], out_offset=None, in_=T["gat_dst"],
                                        in_offset=bass.IndirectOffsetOnAxis(ap=ID[:, h, 1, k:k + 1], axis=0)).then_inc(s_g[h], 16)

            def scatter(h, k, n):
                pool.wait_ge(s_sc[k], 16 * (n + 2))
                pool.sem_inc(s_taken, 1)
                pool.indirect_dma_start(out=T["acc1"][k], out_offset=bass.IndirectOffsetOnAxis(ap=IX[:, h, k:k + 1], axis=0),
                                        in_=O[:, h, k, :], in_offset=None, compute_op=ALU.add).then_inc(s_sc[k], 16)

            for h in range(2):
                pool.wait_ge(s_id[h], 1)
                for k in ks:
                    gather(h, k)
            with pool.Fori(0, GROUPS // 2 - 1) as it:
                for h in range(2):
                    pool.wait_ge(s_id[h], it + 2)
                    pool.wait_ge(s_used[h], it + 1)
                    pool.sem_inc(s_taken, 1)
                    for k in ks:
                        gather(h, k)
                    pool.wait_ge(s_o[h], it + 1)
                    for k in ks:
                        scatter(h, k, 2 * it + h)
            for h in range(2):
                pool.wait_ge(s_o[h], GROUPS // 2)
                for k in ks:
                    scatter(h, k, GROUPS - 2 + h)
            for k in ks:
                pool.wait_ge(s_sc[k], 16 * (GROUPS + 2))

        @block.vector
        def _(dve):
            ch = Chain(dve, s_self)
            for h in range(2):
                ch.run(dve.tensor_copy(ID[:, h, 0, :], K["srci"][:, h * RING:(h + 1) * RING]))
                ch.run(dve.tensor_copy(ID[:, h, 1, :], K["dsti"][:, h * RING:(h + 1) * RING]))
                ch.sync()
                dve.sem_inc(s_id[h], 1)
                dve.sem_inc(s_rf[h], 1)
            ch.reset()
            with dve.Fori(0, GROUPS // 2) as it:
                for h in range(2):
                    n = 2 * it + h
                    dve.wait_ge(s_g[h], 16 * 2 * RING * (it + 1))
                    dve.sem_inc(s_taken2, 1)
                    ch.run(dve.tensor_copy(ID[:, h, 0, :], K["srci"][:, bass.ds((n + 2) * RING, RING)]))
                    ch.run(dve.tensor_copy(ID[:, h, 1, :], K["dsti"][:, bass.ds((n + 2) * RING, RING)]))
                    ch.run(dve.tensor_copy(TG[:, h, :], K["dstf"][:, bass.ds(n * RING, RING)]))
                    ch(dve.tensor_tensor(E[:, h, 0, :, :], G[:, h, :, GH:], H[:, h, :, 0:HEADS], ALU.add))
                    dve.sem_inc(s_id[h], 1)
                    ch(dve.scalar_tensor_tensor(out=E[:, h, 1, :, :], in0=E[:, h, 0, :, :], scalar=0.2, in1=E[:, h, 0, :, :],
                                                op0=ALU.mult, op1=ALU.max))
                    ch(dve.tensor_tensor(E[:, h, 2, :, :], E[:, h, 1, :, :], H[:, h, :, HEADS:], ALU.subtract))
                    dve.sem_inc(s_e, 1)
                    dve.wait_ge(s_cp, RING * (n + 1))
                    dve.wait_ge(s_rin[h], 16 * (it + 1))
                    dve.sem_inc(s_taken2, 1)
                    same_targets(dve, ch, K, R[:, h, :].rearrange("p (k x) -> p k x", k=RING), TG[:, h, :], S[:, h, :, :],
                                 J[:, :, :], EC)
                    target_index(dve, ch, TG[:, h, :], EC, IX[:, h, :], s_sc, n)
                    dve.sem_inc(s_rf[h], 1)
                    dve.wait_ge(s_x, n + 1)
                    for k in ks:
                        dve.tensor_tensor(M[:, h, k, 0:GH].rearrange("p (h o) -> p h o", h=HEADS),
                                          G[:, h, k, 0:GH].rearrange("p (h o) -> p h o", h=HEADS),
                                          M[:, h, k, GH:].unsqueeze(2).broadcast_to([P, HEADS, HID]), ALU.mult).then_inc(s_m, 1)
                    dve.wait_ge(s_m, RING * (n + 1))
                    dve.sem_inc(s_used[h], 1)
                ch.reset()

        @block.scalar
        def _(act):
            def exp(h, n):
                act.wait_ge(s_e, n)
                act.activation(M[:, h, :, GH:], E[:, h, 2, :, :], ACT.Exp).then_inc(s_x, 1)

            def copy(h, n):
                for k in ks:
                    act.wait_ge(s_mg, RING * n + k + 1)
                    act.activation(O[:, h, k, 0:GH], PS[k][:, 0:GH], ACT.Copy).then_inc(s_cph, 1)
                    act.activation(O[:, h, k, GH:], PS[k][:, 512:512 + HEADS], ACT.Copy).then_inc(s_cph, 1)
                    act.wait_ge(s_cph, 2 * (RING * n + k + 1))
                    act.sem_inc(s_cp, 1)
                act.sem_inc(s_o[h], 1)

            act.sem_inc(s_cp, 2 * RING)
            exp(0, 1)
            with act.Fori(0, GROUPS // 2 - 1) as it:
                for h in range(2):
                    exp(1 - h, 2 * it + h + 2)
                    copy(h, 2 * it + h)
            exp(1, GROUPS)
            for h in range(2):
                copy(h, GROUPS - 2 + h)

        @block.tensor
        def _(pe):
            with pe.Fori(0, GROUPS // 2) as it:
                for h in range(2):
                    merge_group(pe, 2 * it + h + 1, S[:, h, :, :], M[:, h, :, :], PS, GW, s_m, s_cp, s_mg)
    sem.clear()


def gat_out(nc, A, T, K, PS):
    sem = Semaphores(nc)
    n_ = lambda x: sem("go_" + x)
    s_in, s_free_in = [n_(f"in{h}") for h in range(2)], [n_(f"in_free{h}") for h in range(2)]
    s_w, s_taken2, s_self, s_o, s_xt, s_xth, s_y, s_x, s_taken = (n_(x) for x in (
        "w", "taken2", "self", "o", "xt", "xth", "y", "exp", "taken"))
    s_full, s_free = [n_(f"full{k}") for k in range(4)], [n_(f"free{k}") for k in range(4)]
    with nc.sbuf_tensor("go_acc", [P, 2, RING, ST, GW], F32) as AC, nc.sbuf_tensor("go_s", [P, ST, GW], F32) as SM, nc.sbuf_tensor("go_w", [P, 4, D], F32) as W, \
            nc.sbuf_tensor("go_b", [P, 1, D], F32) as B, nc.sbuf_tensor("go_o", [P, ST, GH], F32) as O, \
            nc.sbuf_tensor("go_d", [P, ST, HEADS], F32) as DN, nc.sbuf_tensor("go_xt", [P, 4, SW], F32) as XT, \
            nc.sbuf_tensor("go_y", [P, ST, D], F32) as Y, nc.sbuf_tensor("go_n", [P, ST, D], F32) as N, \
            nc.sbuf_tensor("go_e", [P, ST, D], F32) as E, nc.Block() as block:
        @block.sync
        def _(sp):
            sp.dma_start(W[:, :, :], A["L1_gnn_Wo"].rearrange("(k p) n -> p k n", p=P)).then_inc(s_w, 16)
            sp.dma_start(B[:, 0, :], row_bc(A["L1_gnn_bo"])).then_inc(s_w, 16)
            def load(j, h, turn):
                sp.wait_ge(s_free_in[h], turn + 1)
                for k in range(RING):
                    v = T["acc1"][k][0:NP, :].rearrange("(j t p) w -> j p t w", t=ST, p=P)
                    sp.dma_start(AC[:, h, k, :, :], v[bass.ds(j, 1), :, :, :].rearrange("a p t w -> (a p) t w")).then_inc(s_in[h], 16)
            in_turn(sp, load)

        @block.vector
        def _(dve):
            ch = Chain(dve, s_self)
            for h in range(2):
                dve.sem_inc(s_free_in[h], 1)

            def divide(j, h, turn):
                dve.wait_ge(s_in[h], 16 * RING * (turn + 1))
                dve.sem_inc(s_taken2, 1)
                ch.run(dve.tensor_tensor(AC[:, h, 0, :, :], AC[:, h, 0, :, :], AC[:, h, 1, :, :], ALU.add))
                ch(dve.tensor_tensor(AC[:, h, 2, :, :], AC[:, h, 2, :, :], AC[:, h, 3, :, :], ALU.add))
                ch(dve.tensor_tensor(SM[:, :, :], AC[:, h, 0, :, :], AC[:, h, 2, :, :], ALU.add))
                dve.sem_inc(s_free_in[h], 1)
                ch(dve.tensor_scalar(DN[:, :, :], SM[:, :, GH:], 1e-16, None, ALU.add))
                ch(dve.reciprocal(DN[:, :, :], DN[:, :, :]))
                for i in range(ST):
                    ch.run(dve.tensor_tensor(O[:, i, :].rearrange("p (h o) -> p h o", h=HEADS),
                                             SM[:, i, 0:GH].rearrange("p (h o) -> p h o", h=HEADS),
                                             DN[:, i, :].unsqueeze(2).broadcast_to([P, HEADS, HID]), ALU.mult))
                ch.sync()
                dve.sem_inc(s_o, 1)

            def finish(j):
                for i in range(ST):
                    k, per, nth = i % 2, 4 - i % 2, 1 + i // 2
                    dve.wait_ge(s_full[k], per * j + nth + 1)
                    dve.sem_inc(s_taken2, 1)
                    ch(dve.tensor_tensor(Y[:, i, :], PS[k][:, 0:D], B[:, 0, :], ALU.add))
                    dve.sem_inc(s_free[k], 1)
                ch(dve.tensor_scalar(N[:, :, :], Y[:, :, :], 0.0, None, ALU.min))
                dve.sem_inc(s_y, 1)
                ch(dve.tensor_scalar(Y[:, :, :], Y[:, :, :], 0.0, -1.0, ALU.max, ALU.add))
                dve.wait_ge(s_x, j + 1)
                dve.sem_inc(s_taken2, 1)
                ch(dve.tensor_tensor(Y[:, :, :], Y[:, :, :], E[:, :, :], ALU.add))
                xs = K["X"][:, bass.ds(j * ST, ST), :]
                ch(dve.tensor_tensor(xs, xs, Y[:, :, :], ALU.add))

            divide(0, 0, 0)
            ch.reset()
            dve.wait_ge(s_w, 32)
            with dve.Fori(0, NST // 2) as it:
                for h in range(2):
                    dve.wait_ge(s_xt, 2 * it + h + 1)
                    divide(2 * it + h + 1, 1 - h, it + h)
                    finish(2 * it + h)
                    ch.reset()
            finish(NST - 1)

        @block.scalar
        def _(act):
            for k in range(4):
                act.sem_inc(s_free[k], 1)
            with act.Fori(0, NST) as j:
                for kb in range(4):
                    per = (4, 3, 1, 1)[kb]
                    act.wait_ge(s_full[kb], per * j + 1)
                    for a, b in HALVES:
                        act.activation(XT[:, kb, b], PS[kb][:, a], ACT.Copy).then_inc(s_xth, 1)
                    act.wait_ge(s_xth, 8 * j + 2 * kb + 2)
                    act.sem_inc(s_free[kb], 1)
                act.sem_inc(s_xt, 1)
                act.wait_ge(s_y, j + 1)
                act.activation(E[:, :, :], N[:, :, :], ACT.Exp).then_inc(s_x, 1)

        @block.tensor
        def _(pe):
            pe.wait_ge(s_w, 32)
            pe.sem_inc(s_taken, 1)
            with pe.Fori(0, NST) as j:
                pe.wait_ge(s_o, j + 1)
                for kb in range(4):
                    pe.wait_ge(s_free[kb], (4, 3, 1, 1)[kb] * j + 1)
                    transposed(pe, K["I32"][:, :], PS[kb], O, ST, kb * P).then_inc(s_full[kb], 1)
                pe.wait_ge(s_xt, j + 1)
                for i in range(ST):
                    k, per, nth = i % 2, 4 - i % 2, 1 + i // 2
                    pe.wait_ge(s_free[k], per * j + nth + 1)
                    for kb in range(4):
                        m = pe.matmul(PS[k][:, 0:D], XT[:, kb, i * P:(i + 1) * P], W[:, kb, :], start=kb == 0, stop=kb == 3)
                    m.then_inc(s_full[k], 1)
    final_norm(nc, K, "gat_ln", None)
    sem.clear()


def deep_gin(nc, A, T, K, PS):
    with nc.sbuf_tensor("dg_wf", [P, 2 + LAYERS * KB2, D], F32) as WF, nc.sbuf_tensor("dg_ob", [P, D], F32) as OB, \
            nc.sbuf_tensor("dg_g", [P, 2 + (LAYERS - 1) * KB2, F2], F32) as G, \
            nc.sbuf_tensor("dg_cr", [P, LAYERS, 2, F2], F32) as CR:
        fold_weights(nc, A, K, PS, WF, OB, G, CR)
        with nc.sbuf_tensor("dg_tab", [P, TILES, 2 * F2], F16) as TAB, nc.sbuf_tensor("dg_st", [P, KB2, SW], F32) as OT:
            conv_layers(nc, T, K, PS, WF, OB, G, CR, TAB, OT, 0, 1, 2)
            conv_layers(nc, T, K, PS, WF, OB, G, CR, TAB, OT, 1, LAYERS - 1, KB2)
            last_share(nc, T, K, PS, WF, TAB, OT)
    final_norm(nc, K, "dg_ln", None)


def own_rows(pe, K, TAB, ps, j, fb):
    for i in range(ST):
        for part in range(2):
            a = part * F2 + fb * P
            w = TAB[:, bass.ds(j * ST + i, 1), a:a + P].rearrange("p a w -> p (a w)")
            m = pe.matmul(ps[:, cols(i)], w, K["I16"][:, :], start=part == 0, stop=part == 1)
    return m


def load_table(sp, T, TAB, s_tab, q):
    v = T["tab2"].rearrange("(j t p) w -> j p t w", t=ST, p=P)
    sp.dma_start(TAB[:, q * ST:(q + 1) * ST, :], v[q]).then_inc(s_tab[q], 16)


def conv_layers(nc, T, K, PS, WF, OB, G, CR, TAB, OT, first, count, kbs):
    sem = Semaphores(nc)
    n_ = lambda x: sem(f"dc{first}_" + x)
    s_lay, s_taken, s_taken2, s_taken3, s_hl, s_tabout, s_zt, s_ot, s_drain, s_self = (n_(x) for x in (
        "layer", "taken", "taken2", "taken3", "split", "tab_out", "zt", "own_t", "drained", "self"))
    s_tab = [n_(f"tab{q}") for q in range(ST)]
    s_cin, s_cout = [n_(f"c_in{q}") for q in range(ST)], [n_(f"c_out{q}") for q in range(ST)]
    s_full, s_free = [n_(f"full{k}") for k in range(4)], [n_(f"free{k}") for k in range(4)]
    tab_d = T["tab2"].rearrange("(j t p) w -> j p t w", t=ST, p=P)
    U = kbs // 2

    def sums_use(g, fb):
        return fb % 2, U * g + fb // 2 + 1

    def own_use(g, fb):
        return 2 + fb % 2, (U + 3 - fb % 2) * g + fb // 2 + 1

    def tile_use(g, i):
        return 2 + i % 2, (U + 3 - i % 2) * g + U + i // 2 + 1

    with nc.sbuf_tensor(f"dc{first}_c", [P, ST, ST, SW], F16) as C, \
            nc.sbuf_tensor(f"dc{first}_hf", [P, 2, F2], F32) as HF, nc.sbuf_tensor(f"dc{first}_hl", [P, ST, 2 * F2], F16) as HL, \
            nc.sbuf_tensor(f"dc{first}_row", [P, 2, F2], F32) as RW, nc.sbuf_tensor(f"dc{first}_dg", [P, ST], F32) as DG, \
            nc.sbuf_tensor(f"dc{first}_zt", [P, kbs, SW], F32) as ZT, nc.Block() as block:
        @block.sync
        def _(sp):
            with sp.Fori(0, count) as l:
                with sp.Fori(0, NST) as j:
                    load_counts(sp, T, C, s_cin, s_cout, j, l * NST + j)

        @block.gpsimd
        def _(pool):
            pool.sem_inc(s_drain, NST)
            with pool.Fori(0, count) as l:
                with pool.Fori(0, NST) as j:
                    g = l * NST + j
                    pool.wait_ge(s_hl, g + 1)
                    pool.sem_inc(s_taken2, 1)
                    pool.dma_start(tab_d[bass.ds(j, 1), :, :, :].rearrange("a p t w -> (a p) t w"), HL[:, :, :]).then_inc(s_tabout, 16)
                    pool.wait_ge(s_tabout, 16 * (g + 1))
                    pool.sem_inc(s_drain, 1)

        @block.vector
        def _(dve):
            ch = Chain(dve, s_self)

            def sums(g):
                for fb in range(kbs):
                    k, n = sums_use(g, fb)
                    dve.wait_ge(s_full[k], n)
                    if fb == kbs - 1:
                        dve.sem_inc(s_cout[ST - 1], 1)
                    dve.wait_ge(s_ot, 2 * (kbs * g + fb + 1))
                    dve.sem_inc(s_taken, 1)
                    for a, b in HALVES:
                        dve.tensor_tensor(ZT[:, fb, b], PS[k][:, a], OT[:, fb, b], ALU.add).then_inc(s_zt, 1)
                    dve.wait_ge(s_zt, 2 * (kbs * g + fb + 1))
                    dve.sem_inc(s_free[k], 1)

            def tiles(g, j):
                dve.wait_ge(s_drain, g + NST)
                dve.sem_inc(s_taken, 1)
                ch(dve.tensor_copy(DG[:, :], K["deg1"][:, bass.ds(j * ST, ST)]))
                for i in range(ST):
                    k, n = tile_use(g, i)
                    dve.wait_ge(s_full[k], n)
                    dve.sem_inc(s_taken, 1)
                    ch.run(dve.scalar_tensor_tensor(out=HF[:, 0, :], in0=RW[:, 0, :], scalar=DG[:, i:i + 1], in1=PS[k][:, 0:F2],
                                                    op0=ALU.mult, op1=ALU.add))
                    xs = K["X"][:, bass.ds(j * ST + i, 1), :]
                    ch(dve.tensor_tensor(xs, xs, PS[k][:, 512:512 + D].unsqueeze(1), ALU.add))
                    dve.sem_inc(s_free[k], 1)
                    ch(dve.tensor_tensor(HF[:, 1, :], HF[:, 0, :], RW[:, 1, :], ALU.add))
                    ch(dve.tensor_scalar(HF[:, 0, :], HF[:, 1, :], 0.0, None, ALU.max))
                    split16(ch, dve, HF[:, 0, :], HL[:, i, 0:F2], HL[:, i, F2:])
                dve.sem_inc(s_hl, 1)

            if not first:
                for q in range(ST):
                    t = slice(q * ST, (q + 1) * ST)
                    split16(ch, dve, K["X"][:, t, :], TAB[:, t, 0:D], TAB[:, t, F2:F2 + D])
                    dve.sem_inc(s_tab[q], 16)
                ch(dve.tensor_tensor(K["X"][:, :, :], K["X"][:, :, :], OB[:, :].unsqueeze(1).broadcast_to([P, TILES, D]), ALU.add))
                ch.reset()
            with dve.Fori(0, count) as l:
                ch(dve.tensor_copy(RW[:, :, :], CR[:, bass.ds(first + l, 1), :, :].rearrange("p a b n -> p (a b) n")))
                sums(l * NST)
                ch.reset()
                with dve.Fori(0, NST - 1) as j:
                    g = l * NST + j
                    tiles(g, j)
                    sums(g + 1)
                    ch.reset()
                tiles(l * NST + NST - 1, NST - 1)
                ch.reset()

        @block.scalar
        def _(act):
            for q in range(ST):
                act.sem_inc(s_cout[q], 1)
            for k in range(4):
                act.sem_inc(s_free[k], 1)
            with act.Fori(0, count) as l:
                if first:
                    act.wait_ge(s_lay, l + 1)
                    for q in range(ST):
                        act.wait_ge(s_drain, NST * l + q + 1)
                        act.sem_inc(s_taken3, 1)
                        load_table(act, T, TAB, s_tab, q)
                with act.Fori(0, NST) as j:
                    g = l * NST + j
                    for fb in range(kbs):
                        k, n = own_use(g, fb)
                        act.wait_ge(s_full[k], n)
                        for a, b in HALVES:
                            act.activation(OT[:, fb, b], PS[k][:, a], ACT.Copy).then_inc(s_ot, 1)
                        act.wait_ge(s_ot, 2 * (kbs * g + fb + 1))
                        act.sem_inc(s_free[k], 1)

        @block.tensor
        def _(pe):
            def sums(l, g, fb):
                k, n = sums_use(g, fb)
                pe.wait_ge(s_free[k], n)
                neighbour_sum(pe, TAB, C, PS[k], fb, F2, s_cin, s_cout, g, fb == kbs - 1, lambda: None,
                              lambda q: pe.wait_ge(s_tab[q], 16 * (l + 1))).then_inc(s_full[k], 1)

            def own(j, g):
                for fb in range(kbs):
                    k, n = own_use(g, fb)
                    pe.wait_ge(s_free[k], n)
                    own_rows(pe, K, TAB, PS[k], j, fb).then_inc(s_full[k], 1)

            def product(l, g):
                pe.wait_ge(s_zt, 2 * kbs * (g + 1))
                for i in range(ST):
                    k, n = tile_use(g, i)
                    pe.wait_ge(s_free[k], n)
                    nodes = slice(i * P, (i + 1) * P)
                    at = lambda w, kb: w[:, bass.ds(2 + KB2 * l + kb, 1), :].rearrange("p a n -> p (a n)") if first else w[:, kb, :]
                    for kb in range(kbs):
                        pe.matmul(PS[k][:, 0:F2], ZT[:, kb, nodes], at(G, kb), start=kb == 0, stop=kb == kbs - 1)
                    for kb in range(kbs):
                        m = pe.matmul(PS[k][:, 512:512 + D], OT[:, kb, nodes], at(WF, kb), start=kb == 0, stop=kb == kbs - 1)
                    m.then_inc(s_full[k], 1)

            pe.sem_inc(s_lay, 1)
            with pe.Fori(0, count) as l:
                sums(l, l * NST, 0)
                own(0, l * NST)
                for fb in range(1, kbs):
                    sums(l, l * NST, fb)
                with pe.Fori(0, NST - 1) as j:
                    g = l * NST + j
                    sums(l, g + 1, 0)
                    product(l, g)
                    own(j + 1, g + 1)
                    for fb in range(1, kbs):
                        sums(l, g + 1, fb)
                k, n = sums_use(l * NST + NST - 1, kbs - 1)
                pe.wait_ge(s_full[k], n)
                pe.sem_inc(s_lay, 1)
                product(l, l * NST + NST - 1)
    sem.clear()


def last_share(nc, T, K, PS, WF, TAB, OT):
    sem = Semaphores(nc)
    n_ = lambda x: sem("ls_" + x)
    s_ot, s_self, s_taken, s_full, s_tab = n_("own_t"), n_("self"), n_("taken"), n_("products"), [n_(f"tab{q}") for q in range(ST)]
    s_own, s_read, s_taken2 = [n_(f"own{k}") for k in range(4)], n_("read"), n_("taken2")
    with nc.Block() as block:
        @block.sync
        def _(sp):
            for q in range(ST):
                load_table(sp, T, TAB, s_tab, q)

        @block.scalar
        def _(act):
            act.sem_inc(s_read, 1)
            with act.Fori(0, NST) as j:
                for fb in range(KB2):
                    act.wait_ge(s_own[fb], j + 1)
                    for a, b in HALVES:
                        act.activation(OT[:, fb, b], PS[fb][:, a], ACT.Copy).then_inc(s_ot, 1)

        @block.vector
        def _(dve):
            ch = Chain(dve, s_self)
            with dve.Fori(0, NST) as j:
                for i in range(ST):
                    dve.wait_ge(s_full, ST * j + i + 1)
                    dve.sem_inc(s_taken, 1)
                    xs = K["X"][:, bass.ds(j * ST + i, 1), :]
                    ps = PS[i % 4][:, 768:] if i < 4 else PS[0][:, 768:]
                    ch.run(dve.tensor_tensor(xs, xs, ps.unsqueeze(1), ALU.add))
                    if i in (0, ST - 1):
                        ch.sync()
                        dve.sem_inc(s_read, 1)
                ch.reset()

        @block.tensor
        def _(pe):
            for j in range(NST):
                pe.wait_ge(s_tab[j], 16)
                pe.wait_ge(s_read, 2 * j + 1)
                for fb in range(KB2):
                    if fb == 0:
                        pe.sem_inc(s_taken2, 1)
                    own_rows(pe, K, TAB, PS[fb], j, fb).then_inc(s_own[fb], 1)
                pe.wait_ge(s_ot, 2 * KB2 * (j + 1))
                for i in range(ST):
                    if i == 4:
                        pe.wait_ge(s_read, 2 * j + 2)
                    for kb in range(KB2):
                        m = pe.matmul(PS[i % 4][:, 768:], OT[:, kb, i * P:(i + 1) * P], WF[:, 2 + (LAYERS - 1) * KB2 + kb, :],
                                      start=kb == 0, stop=kb == KB2 - 1)
                    m.then_inc(s_full, 1)
    sem.clear()


def fold_weights(nc, A, K, PS, WF, OB, G, CR):
    sem = Semaphores(nc)
    n_ = lambda x: sem("fo_" + x)
    s_w, s_b, s_w1, s_self, s_full, s_free, s_bb, s_bf, s_done = (n_(x) for x in (
        "w", "b", "w1", "self", "full", "free", "bias", "bias_full", "done"))
    KB = KB2
    with nc.sbuf_tensor("fo_wt", [P, 2, KB, F2], F32) as WT, nc.sbuf_tensor("fo_wo", [P, LAYERS + 1, KB, D], F32) as WO, \
            nc.sbuf_tensor("fo_b", [P, LAYERS + 1, KB], F32) as B, nc.sbuf_tensor("fo_bb", [P, LAYERS + 1, KB, P], F32) as BB, \
            nc.sbuf_tensor("fo_w1", [P, LAYERS, KB, F2], F32) as W1, nc.Block() as block:
        @block.sync
        def _(sp):
            sp.dma_start(B[:, 0, :], A["L2_gnn_in_bc"]).then_inc(s_b, 16)
            for l in range(LAYERS):
                sp.dma_start(B[:, l + 1, :], A["L2_gnn_conv_b2c"][l]).then_inc(s_b, 16)
                sp.dma_start(CR[:, l, 1, :], row_bc(A["L2_gnn_conv_b1"][l])).then_inc(s_b, 16)
            sp.dma_start(OB[:, :], row_bc(A["L2_gnn_out_b"])).then_inc(s_b, 16)
            sp.dma_start(WO[:, :, :, :].rearrange("p l k n -> p (l k) n"),
                         A["L2_gnn_out_W"].rearrange("(k p) n -> p k n", p=P)).then_inc(s_b, 16)
            sp.dma_start(WT[:, 0, :, 0:D], A["L2_gnn_in_WT"].rearrange("(k p) n -> p k n", p=P)).then_inc(s_w, 16)
            sp.dma_start(W1[:, :, :, :].rearrange("p l k n -> p (l k) n"),
                         A["L2_gnn_conv_W1"].rearrange("l (k p) n -> p (l k) n", p=P)).then_inc(s_w1, 16)
            for l in range(LAYERS):
                if l:
                    sp.wait_ge(s_free, 2 + KB * (l - 1))
                else:
                    sp.wait_ge(s_w, 16)
                sp.wait_ge(s_w, 16 * (l + 1))
                sp.dma_start(WT[:, (l + 1) % 2, :, :], A["L2_gnn_conv_W2T"][l].rearrange("(k p) n -> p k n", p=P)).then_inc(s_w, 16)

        @block.tensor
        def _(pe):
            pe.wait_ge(s_b, 16 * (2 * LAYERS + 3))
            pe.wait_ge(s_w1, 16)
            n = 0
            for l in range(LAYERS + 1):
                pe.wait_ge(s_w, 16 * (l + 1))
                for ib in range(2 if l == 0 else KB):
                    if n >= 2:
                        pe.wait_ge(s_free, n - 1)
                    for kb in range(KB):
                        m = pe.matmul(PS[n % 2][:, 0:D], WT[:, l % 2, kb, ib * P:(ib + 1) * P], WO[:, l, kb, :], start=kb == 0, stop=kb == KB - 1)
                    if l < LAYERS:
                        for kb in range(KB):
                            m = pe.matmul(PS[n % 2][:, 512:512 + F2], WT[:, l % 2, kb, ib * P:(ib + 1) * P], W1[:, l, kb, :],
                                          start=kb == 0, stop=kb == KB - 1)
                    m.then_inc(s_full, 1)
                    n += 1
            pe.wait_ge(s_bb, 1)
            for l in range(LAYERS + 1):
                for kb in range(KB):
                    m = pe.matmul(PS[2][:, 0:D], BB[:, l, kb, :], WO[:, l, kb, :], start=l + kb == 0, stop=l + kb == LAYERS + KB - 1)
            for l in range(LAYERS):
                ps = PS[2][:, 512:] if l == 0 else PS[3][:, (l - 1) * 512:l * 512]
                for kb in range(KB):
                    m = pe.matmul(ps, BB[:, l, kb, :], W1[:, l, kb, :], start=kb == 0, stop=kb == KB - 1)
            m.then_inc(s_bf, 1)

        @block.vector
        def _(dve):
            ch = Chain(dve, s_self)
            dve.wait_ge(s_b, 16 * (2 * LAYERS + 3))
            for l in range(LAYERS + 1):
                for kb in range(KB):
                    ch.run(dve.tensor_scalar(BB[:, l, kb, :], K["ones"][:, :], B[:, l, kb:kb + 1], None, ALU.mult))
            ch.sync()
            dve.sem_inc(s_bb, 1)
            for n in range(2 + LAYERS * KB):
                dve.wait_ge(s_full, n + 1)
                ch.run(dve.tensor_copy(WF[:, n, :], PS[n % 2][:, 0:D]))
                if n < 2 + (LAYERS - 1) * KB:
                    ch.run(dve.tensor_copy(G[:, n, :], PS[n % 2][:, 512:512 + F2]))
                ch.sync()
                dve.sem_inc(s_free, 1)
            dve.wait_ge(s_bf, 1)
            for l in range(LAYERS):
                ps = PS[2][:, 512:] if l == 0 else PS[3][:, (l - 1) * 512:l * 512]
                dve.tensor_copy(CR[:, l, 0, :], ps)
            ch(dve.tensor_tensor(OB[:, :], PS[2][:, 0:D], OB[:, :], ALU.add))
    sem.clear()


def att_nodes(nc, A, T, K, PS):
    sem = Semaphores(nc)
    n_ = lambda x: sem("an_" + x)
    s_w, s_self, s_taken, s_taken2, s_zero, s_xs, s_xt, s_ut, s_ft, s_rb, s_cb, s_cbh, s_out, s_drain = (n_(x) for x in (
        "w", "self", "taken", "taken2", "zero", "xs", "xt", "ut", "ft", "rb", "cb", "cbh", "out", "drained"))
    s_full, s_free = [n_(f"full{k}") for k in range(4)], [n_(f"free{k}") for k in range(4)]
    HB = 2 * ATT
    with nc.sbuf_tensor("an_w1", [P, PH, 2, D], F32) as W1, nc.sbuf_tensor("an_w2", [P, PH, 2, P], F32) as W2, \
            nc.sbuf_tensor("an_b1", [P, PH, 2], F32) as B1, nc.sbuf_tensor("an_b2", [P, 2], F32) as B2, \
            nc.sbuf_tensor("an_a", [P, 2, 2, HB], F32) as AA, nc.sbuf_tensor("an_ab", [P, 2, HB], F32) as AB, \
            nc.sbuf_tensor("an_xs", [P, ST, D], F32) as XS, nc.sbuf_tensor("an_xt", [P, 2, SW], F32) as XT, \
            nc.sbuf_tensor("an_ut", [P, 8, SW], F32) as UT, nc.sbuf_tensor("an_ft", [P, 2, SW], F32) as FT, \
            nc.sbuf_tensor("an_rb", [P, 2, ST, AW], F32) as RB, nc.sbuf_tensor("an_cb", [P, 2, ST, AW + PF], F32) as CB, \
            nc.Block() as block:
        NLOAD = 2 + PH + PH + 2 * PH + 1

        @block.sync
        def _(sp):
            sp.wait_ge(s_zero, 2)
            sp.dma_start(W1[:, :, :, :].rearrange("p h k n -> p (h k) n"),
                         A["L3_gnn_W1"].rearrange("h (k p) n -> p (h k) n", p=P)).then_inc(s_w, 16)
            sp.dma_start(B2[:, :], A["L3_gnn_b2c"]).then_inc(s_w, 16)
            for h in range(PH):
                lo = h % 2 * PO
                sp.dma_start(B1[:, h, :], A["L3_gnn_b1"][h]).then_inc(s_w, 16)
                sp.dma_start(W2[:, h, :, lo:lo + PO], A["L3_gnn_W2"][h].rearrange("(k p) n -> p k n", p=P)).then_inc(s_w, 16)
                for side in range(2):
                    sp.dma_start(AA[lo:lo + PO, h // 2, side, h % 2 * ATT:(h % 2 + 1) * ATT],
                                 A["L3_gnn_A1"][h, side * PO:(side + 1) * PO, :]).then_inc(s_w, 16)
            sp.dma_start(AB[:, :, :].rearrange("p a b -> p (a b)"), row_bc(A["L3_gnn_ab1"].rearrange("h n -> (h n)"))).then_inc(s_w, 16)

            def store(j, h, turn):
                sp.wait_ge(s_rb, j + 1)
                v = T["att_row"].rearrange("(j t p) w -> j p t w", t=ST, p=P)
                sp.dma_start(v[bass.ds(j, 1), :, :, :].rearrange("a p t w -> (a p) t w"), RB[:, h, :, :]).then_inc(s_out, 16)
                sp.wait_ge(s_cb, j + 1)
                v = T["att_col"].rearrange("(j t p) w -> j p t w", t=ST, p=P)
                sp.dma_start(v[bass.ds(j, 1), :, :, :].rearrange("a p t w -> (a p) t w"), CB[:, h, :, :]).then_inc(s_out, 16)
                sp.wait_ge(s_out, 32 * (j + 1))
                sp.sem_inc(s_drain, 1)
            in_turn(sp, store)

        @block.vector
        def _(dve):
            ch = Chain(dve, s_self)
            dve.memset(W2[:, :, :, :], 0.0).then_inc(s_zero, 1)
            dve.memset(AA[:, :, :, :], 0.0).then_inc(s_zero, 1)
            dve.sem_inc(s_drain, 2)
            ch(dve.tensor_copy(XS[:, :, :], K["X"][:, 0:ST, :]))
            dve.sem_inc(s_xs, 1)
            dve.wait_ge(s_w, 16 * NLOAD)
            dve.sem_inc(s_taken, 1)
            ch.reset()

            def rows(j, h):
                dve.wait_ge(s_drain, j + 1)
                for i in range(ST):
                    dve.wait_ge(s_full[2], 9 * j + 4 + i + 1)
                    dve.sem_inc(s_taken, 1)
                    ch(dve.tensor_tensor(RB[:, h, i, :].rearrange("p (a b) -> p a b", a=2),
                                         PS[2][:, :].rearrange("p (a b) -> p a b", a=2)[:, :, 0:HB], AB[:, :, :], ALU.add))
                    dve.sem_inc(s_free[2], 1)
                dve.sem_inc(s_rb, 1)

            with dve.Fori(0, NST // 2) as it:
                for h in range(2):
                    j = 2 * it + h
                    dve.wait_ge(s_full[1], 2 * j + 1)
                    ch(dve.tensor_copy(XS[:, :, :], K["X"][:, bass.ds((j + 1) * ST, ST), :]))
                    dve.sem_inc(s_xs, 1)
                    rows(j, h)
                    ch.reset()
            rows(NST - 1, 0)

        @block.scalar
        def _(act):
            for k in range(4):
                act.sem_inc(s_free[k], 1)
            act.wait_ge(s_w, 16 * NLOAD)
            act.sem_inc(s_taken, 1)

            def copy(k, n, out, s_done, before, func=ACT.Copy, **kw):
                act.wait_ge(s_full[k], n)
                for a, b in HALVES:
                    act.activation(out[:, b], PS[k][:, a], func, **kw).then_inc(s_done, 1)
                act.wait_ge(s_done, before + 2)
                act.sem_inc(s_free[k], 1)

            def rows(j):
                for kb in range(2):
                    copy(kb, 2 * j + 1, XT[:, kb, :], s_xt, 4 * j + 2 * kb)

            def units(j, h, turn):
                for hp in range(2):
                    for u in range(4):
                        copy(2 + u % 2, 9 * j + 2 * hp + u // 2 + 1, UT[:, 4 * hp + u, :], s_ut, 16 * j + 8 * hp + 2 * u,
                             ACT.Relu, bias=B1[:, 2 * hp + u // 2, u % 2:u % 2 + 1])
                for hp in range(2):
                    copy(hp, 2 * j + 2, FT[:, hp, :], s_ft, 4 * j + 2 * hp, ACT.Identity, bias=B2[:, hp:hp + 1])
                if not (isinstance(j, int) and j == NST - 1):
                    rows(j + 1)
                act.wait_ge(s_drain, j + 1)
                act.sem_inc(s_taken, 1)
                for i in range(ST):
                    act.wait_ge(s_full[3], 9 * j + 4 + i + 1)
                    pv = PS[3][:, :].rearrange("p (a b) -> p a b", a=2)
                    act.activation(CB[:, h, i, 0:AW].rearrange("p (a b) -> p a b", a=2), pv[:, :, 0:HB], ACT.Copy).then_inc(s_cbh, 1)
                    act.activation(CB[:, h, i, AW:].rearrange("p (a b) -> p a b", a=2), pv[:, :, HB:HB + P], ACT.Copy).then_inc(s_cbh, 1)
                    act.wait_ge(s_cbh, 2 * (ST * j + i + 1))
                    act.sem_inc(s_free[3], 1)
                act.sem_inc(s_cb, 1)

            rows(0)
            in_turn(act, units)

        @block.tensor
        def _(pe):
            def rows(j):
                pe.wait_ge(s_xs, j + 1)
                for kb in range(2):
                    pe.wait_ge(s_free[kb], 2 * j + 1)
                    transposed(pe, K["I32"][:, :], PS[kb], XS, ST, kb * P).then_inc(s_full[kb], 1)

            def features(j):
                pe.wait_ge(s_xt, 4 * j + 4)
                for hp in range(2):
                    for u in range(4):
                        k = 2 + u % 2
                        pe.wait_ge(s_free[k], 9 * j + 2 * hp + u // 2 + 1)
                        for a, b in HALVES:
                            for kb in range(2):
                                m = pe.matmul(PS[k][:, a], W1[:, 2 * hp + u // 2, kb, u % 2 * P:(u % 2 + 1) * P],
                                              XT[:, kb, b], start=kb == 0, stop=kb == 1)
                        m.then_inc(s_full[k], 1)
                for hp in range(2):
                    pe.wait_ge(s_ut, 16 * j + 8 * hp + 8)
                    pe.wait_ge(s_free[hp], 2 * j + 2)
                    for a, b in HALVES:
                        for u in range(4):
                            m = pe.matmul(PS[hp][:, a], W2[:, 2 * hp + u // 2, u % 2, :], UT[:, 4 * hp + u, b], start=u == 0, stop=u == 3)
                    m.then_inc(s_full[hp], 1)

            def units(j):
                pe.wait_ge(s_ft, 4 * j + 4)
                for i in range(ST):
                    for side in range(2):
                        k = 2 + side
                        pe.wait_ge(s_free[k], 9 * j + 4 + i + 1)
                        for hp in range(2):
                            f = FT[:, hp, i * P:(i + 1) * P]
                            m = pe.matmul(PS[k][:, 512 * hp:512 * hp + HB], f, AA[:, hp, side, :], start=True, stop=True)
                            if side:
                                m = pe.matmul(PS[k][:, 512 * hp + HB:512 * hp + HB + P], f, K["I32"][:, :], start=True, stop=True)
                        m.then_inc(s_full[k], 1)

            rows(0)
            pe.wait_ge(s_w, 16 * NLOAD)
            pe.sem_inc(s_taken2, 1)
            with pe.Fori(0, NST - 1) as j:
                features(j)
                rows(j + 1)
                units(j)
            features(NST - 1)
            units(NST - 1)
    sem.clear()


def att_edges(nc, A, T, K, PS):
    sem = Semaphores(nc)
    ks = range(RING)
    with nc.sbuf_tensor("ae_w", [P, CHUNKS, PH], F32) as WA:
        n_ = lambda x: [sem(f"ae_{x}{h}") for h in range(2)]
        s_r, s_c, s_id, s_used, s_spill = (n_(x) for x in ("row_in", "col_in", "ids", "used", "spilt"))
        s_w, s_self, s_taken, s_taken2 = (sem("ae_" + x) for x in ("w", "self", "taken", "taken2"))
        spill = T["spill"].rearrange("(g k p) n -> g p k n", p=P, k=RING)
        with nc.sbuf_tensor("ae_r", [P, 2, RING, AW], F32) as R, nc.sbuf_tensor("ae_c", [P, 2, RING, AW + PF], F32) as C, \
                nc.sbuf_tensor("ae_rows", [P, 2, AW], F32) as RW, nc.sbuf_tensor("ae_id", [P, 2, 2, RING], I32) as ID, \
                nc.sbuf_tensor("ae_ew", [P, CHUNKS], F32) as EW, nc.sbuf_tensor("ae_ewk", [P, RING], F32) as EWK, \
                nc.sbuf_tensor("ae_z", [P, RING, AW], F32) as Z, nc.sbuf_tensor("ae_y", [P, RING, AW], F32) as Y, \
                nc.sbuf_tensor("ae_e", [P, RING * PH], F32) as E, nc.Block() as block:
            @block.sync
            def _(sp):
                for h in range(PH):
                    sp.dma_start(RW[:, 0, h * ATT:(h + 1) * ATT], row_bc(A["L3_gnn_A1"][h, ATT - 1, :])).then_inc(s_w, 16)
                sp.dma_start(RW[:, 1, :], row_bc(A["L3_gnn_A2"].rearrange("h n a -> (h n a)"))).then_inc(s_w, 16)
                sp.dma_start(EW[:, :], A["ew_col"]).then_inc(s_w, 16)
                with sp.Fori(0, GROUPS // 2) as it:
                    for h in range(2):
                        sp.wait_ge(s_c[h], 16 * RING * (it + 1))
                        sp.dma_start(spill[bass.ds(2 * it + h, 1), :, :, :].rearrange("a p k n -> (a p) k n"),
                                     C[:, h, :, AW:]).then_inc(s_spill[h], 16)
                for h in range(2):
                    sp.wait_ge(s_spill[h], 16 * (GROUPS // 2))

            @block.gpsimd
            def _(pool):
                def gathers(h):
                    for k in ks:
                        pool.indirect_dma_start(out=R[:, h, k, :], out_offset=None, in_=T["att_row"],
                                                in_offset=bass.IndirectOffsetOnAxis(ap=ID[:, h, 0, k:k + 1], axis=0)).then_inc(s_r[h], 16)
                        pool.indirect_dma_start(out=C[:, h, k, :], out_offset=None, in_=T["att_col"],
                                                in_offset=bass.IndirectOffsetOnAxis(ap=ID[:, h, 1, k:k + 1], axis=0)).then_inc(s_c[h], 16)
                for h in range(2):
                    pool.wait_ge(s_id[h], 1)
                    gathers(h)
                with pool.Fori(1, GROUPS // 2) as it:
                    for h in range(2):
                        pool.wait_ge(s_id[h], it + 1)
                        pool.wait_ge(s_used[h], it)
                        pool.wait_ge(s_spill[h], 16 * it)
                        pool.sem_inc(s_taken, 1)
                        gathers(h)

            @block.vector
            def _(dve):
                ch = Chain(dve, s_self)
                dve.wait_ge(s_w, 16 * (PH + 2))
                for h in range(2):
                    ch.run(dve.tensor_copy(ID[:, h, 0, :], K["srci"][:, h * RING:(h + 1) * RING]))
                    ch.run(dve.tensor_copy(ID[:, h, 1, :], K["dsti"][:, h * RING:(h + 1) * RING]))
                    ch.sync()
                    dve.sem_inc(s_id[h], 1)
                ch.reset()
                with dve.Fori(0, GROUPS // 2) as it:
                    for h in range(2):
                        n = 2 * it + h
                        dve.wait_ge(s_r[h], 16 * RING * (it + 1))
                        dve.wait_ge(s_c[h], 16 * RING * (it + 1))
                        dve.sem_inc(s_taken2, 1)
                        ch.run(dve.tensor_copy(ID[:, h, 0, :], K["srci"][:, bass.ds((n + 2) * RING, RING)]))
                        ch.run(dve.tensor_copy(ID[:, h, 1, :], K["dsti"][:, bass.ds((n + 2) * RING, RING)]))
                        ch.run(dve.tensor_copy(EWK[:, :], EW[:, bass.ds(n * RING, RING)]))
                        ch(dve.tensor_tensor(Z[:, :, :], R[:, h, :, :], C[:, h, :, 0:AW], ALU.add))
                        dve.sem_inc(s_id[h], 1)
                        dve.sem_inc(s_used[h], 1)
                        for k in ks:
                            ch.run(dve.scalar_tensor_tensor(out=Z[:, k, :], in0=RW[:, 0, :], scalar=EWK[:, k:k + 1], in1=Z[:, k, :],
                                                            op0=ALU.mult, op1=ALU.add))
                        ch.sync()
                        for k in ks:
                            for q in range(PH):
                                u = slice(q * ATT, (q + 1) * ATT)
                                ch.run(dve.scalar_tensor_tensor(out=Y[:, k, u], in0=Z[:, k, u], scalar=0.0, in1=RW[:, 1, u], op0=ALU.max,
                                                                op1=ALU.mult, accum_out=E[:, k * PH + q:k * PH + q + 1]))
                        ch.sync()
                        ch(dve.tensor_copy(WA[:, bass.ds(n * RING, RING), :].rearrange("p k h -> p (k h)"), E[:, :]))
                    ch.reset()

        s_w, s_self, s_part, s_max, s_sub, s_e = (sem("am_" + x) for x in ("w", "self", "part", "max", "sub", "exp"))
        FULL, REM = EDGES // P, EDGES % P
        with nc.sbuf_tensor("am_b", [P, PH], F32) as B, nc.sbuf_tensor("am_m", [P, PH], F32) as MX, \
                nc.sbuf_tensor("am_a", [P, PH], F32) as MA, nc.sbuf_tensor("am_t", [P, CHUNKS, PH], F32) as TM, nc.Block() as block:
            @block.sync
            def _(sp):
                sp.dma_start(B[:, :], row_bc(A["L3_gnn_ab2"].rearrange("h a -> (h a)"))).then_inc(s_w, 16)

            @block.vector
            def _(dve):
                ch = Chain(dve, s_self)
                dve.wait_ge(s_w, 16)
                ch(dve.tensor_tensor(TM[:, :, :], WA[:, :, :], B[:, :].unsqueeze(1).broadcast_to([P, CHUNKS, PH]), ALU.add))
                ch(dve.scalar_tensor_tensor(out=WA[:, :, :], in0=TM[:, :, :], scalar=0.2, in1=TM[:, :, :], op0=ALU.mult, op1=ALU.max))
                ch(dve.tensor_reduce(MX[:, :], WA[:, 0:FULL, :].rearrange("p c h -> p h c"), AX.X, ALU.max))
                ch(dve.tensor_tensor(MX[0:REM, :], MX[0:REM, :], WA[0:REM, FULL, :], ALU.max))
                dve.sem_inc(s_part, 1)
                dve.wait_ge(s_max, 1)
                top = MA[:, :].unsqueeze(1).broadcast_to([P, CHUNKS, PH])
                ch(dve.tensor_tensor(WA[:, :, :], WA[:, :, :], top, ALU.min))
                ch(dve.tensor_tensor(TM[:, :, :], WA[:, :, :], top, ALU.subtract))
                dve.sem_inc(s_sub, 1)

            @block.gpsimd
            def _(pool):
                pool.wait_ge(s_part, 1)
                pool.partition_all_reduce(MA[:, :], MX[:, :], P, MAX_OF_ALL).then_inc(s_max, 1)

            @block.scalar
            def _(act):
                act.wait_ge(s_sub, 1)
                act.activation(WA[:, :, :], TM[:, :, :], ACT.Exp).then_inc(s_e, 1)

        n_ = lambda x: [sem(f"aw_{x}{h}") for h in range(2)]
        s_f, s_ff, s_rin, s_rf = (n_(x) for x in ("feats_in", "feats_free", "rows_in", "rows_free"))
        s_sc = T["scat3"]
        s_self, s_taken, s_taken2, s_taken3, s_m, s_mg, s_cp, s_ix = (sem("aw_" + x) for x in (
            "self", "taken", "taken2", "taken3", "msg", "merged", "copied", "index"))
        srow = A["src_row"].rearrange("(g n) -> g n", n=RING * P)
        with nc.sbuf_tensor("aw_f", [P, 2, RING, PF], F32) as F, nc.sbuf_tensor("aw_m", [P, 2, RING, PW], F32) as M, \
                nc.sbuf_tensor("aw_o", [P, 2, RING, PW], F32) as O, nc.sbuf_tensor("aw_s", [P, 2, RING, P], F32) as S, \
                nc.sbuf_tensor("aw_j", [P, RING, P], F32) as J, nc.sbuf_tensor("aw_r", [P, 2, RING * P], I32) as R, \
                nc.sbuf_tensor("aw_c", [P, 3, RING], F32) as EC, nc.sbuf_tensor("aw_tg", [P, RING], F32) as TG, \
                nc.sbuf_tensor("aw_ix", [P, 2, RING], I32) as IX, nc.Block() as block:
            @block.sync
            def _(sp):
                with sp.Fori(0, GROUPS // 2) as it:
                    for h in range(2):
                        g = bass.ds(2 * it + h, 1)
                        sp.wait_ge(s_rf[h], it + 1)
                        sp.dma_start(R[:, h, :], row_bc(srow[g, :].rearrange("a n -> (a n)"))).then_inc(s_rin[h], 16)
                        sp.wait_ge(s_ff[h], it + 1)
                        sp.dma_start(F[:, h, :, :], spill[g, :, :, :].rearrange("a p k n -> (a p) k n")).then_inc(s_f[h], 16)

            @block.gpsimd
            def _(pool):
                with pool.Fori(0, GROUPS // 2) as it:
                    for h in range(2):
                        n = 2 * it + h
                        pool.wait_ge(s_ix, n + 1)
                        for k in ks:
                            pool.wait_ge(s_cp, RING * (n + 2) + k + 1)
                            pool.wait_ge(s_sc[k], 16 * (n + 2))
                            pool.sem_inc(s_taken, 1)
                            pool.indirect_dma_start(out=T["acc3"][k], out_offset=bass.IndirectOffsetOnAxis(ap=IX[:, h, k:k + 1], axis=0),
                                                    in_=O[:, h, k, :], in_offset=None, compute_op=ALU.add).then_inc(s_sc[k], 16)
                for k in ks:
                    pool.wait_ge(s_sc[k], 16 * (GROUPS + 2))

            @block.vector
            def _(dve):
                ch = Chain(dve, s_self)
                for h in range(2):
                    dve.sem_inc(s_rf[h], 1)
                    dve.sem_inc(s_ff[h], 1)
                with dve.Fori(0, GROUPS // 2) as it:
                    for h in range(2):
                        n = 2 * it + h
                        ch.run(dve.tensor_copy(TG[:, :], K["srcf"][:, bass.ds(n * RING, RING)]))
                        ch.sync()
                        dve.wait_ge(s_cp, RING * (n + 1))
                        dve.wait_ge(s_rin[h], 16 * (it + 1))
                        dve.sem_inc(s_taken2, 1)
                        same_targets(dve, ch, K, R[:, h, :].rearrange("p (k x) -> p k x", k=RING), TG[:, :], S[:, h, :, :],
                                     J[:, :, :], EC)
                        dve.sem_inc(s_rf[h], 1)
                        ch(dve.tensor_copy(M[:, h, :, PF:], WA[:, bass.ds(n * RING, RING), :]))
                        dve.wait_ge(s_f[h], 16 * (it + 1))
                        for k in ks:
                            dve.tensor_tensor(M[:, h, k, 0:PF].rearrange("p (h o) -> p h o", h=PH),
                                              F[:, h, k, :].rearrange("p (h o) -> p h o", h=PH),
                                              M[:, h, k, PF:].unsqueeze(2).broadcast_to([P, PH, PO]), ALU.mult).then_inc(s_m, 1)
                        target_index(dve, ch, TG[:, :], EC, IX[:, h, :], s_sc, n)
                        dve.sem_inc(s_ix, 1)
                        dve.wait_ge(s_m, RING * (n + 1))
                        dve.sem_inc(s_ff[h], 1)
                    ch.reset()

            @block.scalar
            def _(act):
                act.sem_inc(s_cp, 2 * RING)
                with act.Fori(0, GROUPS // 2) as it:
                    for h in range(2):
                        for k in ks:
                            n = 2 * it + h
                            act.wait_ge(s_sc[k], 16 * (n + 1))
                            act.wait_ge(s_mg, RING * n + k + 1)
                            act.sem_inc(s_taken3, 1)
                            act.activation(O[:, h, k, :], PS[k][:, 0:PW], ACT.Copy).then_inc(s_cp, 1)

            @block.tensor
            def _(pe):
                with pe.Fori(0, GROUPS // 2) as it:
                    for h in range(2):
                        merge_group(pe, 2 * it + h + 1, S[:, h, :, :], M[:, h, :, :], PS, PW, s_m, s_cp, s_mg)
    sem.clear()



def att_out(nc, A, T, K, PS):
    sem = Semaphores(nc)
    s_in, s_free = [sem(f"ao_in{h}") for h in range(2)], [sem(f"ao_free{h}") for h in range(2)]
    s_self, s_taken = sem("ao_self"), sem("ao_taken")
    with nc.sbuf_tensor("ao_acc", [P, 2, RING, ST, PW], F32) as AC, nc.sbuf_tensor("ao_d", [P, ST, PH], F32) as DN, \
            nc.sbuf_tensor("ao_s", [P, ST, PW], F32) as SM, nc.sbuf_tensor("ao_o", [P, ST, D], F32) as O, nc.Block() as block:
        @block.sync
        def _(sp):
            def load(j, h, turn):
                sp.wait_ge(s_free[h], turn + 1)
                for k in range(RING):
                    v = T["acc3"][k][0:NP, :].rearrange("(j t p) w -> j p t w", t=ST, p=P)
                    sp.dma_start(AC[:, h, k, :, :], v[bass.ds(j, 1), :, :, :].rearrange("a p t w -> (a p) t w")).then_inc(s_in[h], 16)
            in_turn(sp, load)

        @block.vector
        def _(dve):
            ch = Chain(dve, s_self)
            for h in range(2):
                dve.sem_inc(s_free[h], 1)

            def divide(j, h, turn):
                dve.wait_ge(s_in[h], 16 * RING * (turn + 1))
                dve.sem_inc(s_taken, 1)
                ch.run(dve.tensor_tensor(AC[:, h, 0, :, :], AC[:, h, 0, :, :], AC[:, h, 1, :, :], ALU.add))
                ch(dve.tensor_tensor(AC[:, h, 2, :, :], AC[:, h, 2, :, :], AC[:, h, 3, :, :], ALU.add))
                ch(dve.tensor_tensor(SM[:, :, :], AC[:, h, 0, :, :], AC[:, h, 2, :, :], ALU.add))
                dve.sem_inc(s_free[h], 1)
                ch(dve.tensor_scalar(DN[:, :, :], SM[:, :, PF:], 1e-10, None, ALU.add))
                ch(dve.reciprocal(DN[:, :, :], DN[:, :, :]))
                for i in range(ST):
                    ch.run(dve.tensor_tensor(O[:, i, :].rearrange("p (h o) -> p h o", h=PH),
                                             SM[:, i, 0:PF].rearrange("p (h o) -> p h o", h=PH),
                                             DN[:, i, :].unsqueeze(2).broadcast_to([P, PH, PO]), ALU.mult))
                ch.sync()
                xs = K["X"][:, bass.ds(j * ST, ST), :]
                ch(dve.tensor_tensor(xs, xs, O[:, :, :], ALU.add))
                ch.reset()
            in_turn(dve, divide)
    final_norm(nc, K, "att_ln", None)
    sem.clear()


PHASES = 10


def kernel(**inputs):
    import numpy as np
    import concourse.bacc as bacc
    from concourse.bass_utils import run_bass_kernel_spmd

    nc = bacc.Bacc("TRN2", target_bir_lowering=False, num_devices=1)
    arrays = layout(inputs)
    A = {n: nc.dram_tensor(n, a.shape, mybir.dt.from_np(a.dtype), kind="ExternalInput").ap() for n, a in arrays.items()}
    out = nc.dram_tensor("out", (NODES, D), F32, kind="ExternalOutput").ap()
    gnn_kernel(nc, A, out)
    r = run_bass_kernel_spmd(nc, [arrays], core_ids=[0])
    return r.results[0]["out"]


def layout(inputs):
    import numpy as np

    a = {n: np.ascontiguousarray(v) for n, v in inputs.items()}
    pad = NODES + np.arange(EP - EDGES) % (NP - NODES)
    o = {"x": np.concatenate([a["x"], np.zeros((NP - NODES, D), a["x"].dtype)])}
    for n in ("src", "dst"):
        row = np.concatenate([a[n], pad.astype(a[n].dtype)])
        o[n + "_row"] = row
        o[n + "_col"] = np.ascontiguousarray(row.reshape(CHUNKS, P).T)
    ew = np.concatenate([a["edge_weight"], np.zeros(EP - EDGES, a["edge_weight"].dtype)])
    o["ew_col"] = np.ascontiguousarray(ew.reshape(CHUNKS, P).T)
    for n, v in a.items():
        if n[:2] in ("L0", "L1", "L2", "L3"):
            o[n] = v
    def columns(v, n):
        return np.ascontiguousarray(v.reshape(v.shape[:-1] + (n, P)).swapaxes(-1, -2))

    o["L0_gnn_b1"] = columns(a["L0_gnn_b1"], 2)
    o["L2_gnn_conv_b2c"] = columns(a["L2_gnn_conv_b2"], 4)
    o["L2_gnn_in_bc"] = columns(a["L2_gnn_in_b"], KB2)
    o["L3_gnn_b1"] = columns(a["L3_gnn_b1"], 2)
    o["L3_gnn_b2c"] = columns(a["L3_gnn_b2"].reshape(PF), 2)
    o["L1_gnn_W"] = np.ascontiguousarray(a["L1_gnn_W"].transpose(1, 0, 2).reshape(D, GH))
    o["L2_gnn_in_WT"] = np.ascontiguousarray(a["L2_gnn_in_W"].T)
    o["L2_gnn_conv_W2T"] = np.ascontiguousarray(a["L2_gnn_conv_W2"].transpose(0, 2, 1))
    return o
```
